# Optimizing a Trainium2 kernel written in Bass

```python
import numpy as np
import jax
import jax.numpy as jnp

def _softmax(x, axis=-1):
    return jax.nn.softmax(x, axis=axis)

def _gelu(x):
    return jax.nn.gelu(x, approximate=True)

def _silu(x):
    return jax.nn.silu(x)

def _sigmoid(x):
    return jax.nn.sigmoid(x)

def _layernorm(x, axis=-1, eps=1e-05):
    m = jnp.mean(x, axis=axis, keepdims=True)
    v = jnp.var(x, axis=axis, keepdims=True)
    return (x - m) / jnp.sqrt(v + eps)

def _scatter_add(tgt, idx, src, axis=0):
    return tgt.at[idx].add(src)

def _segment_sum(src, seg, n):
    return jax.ops.segment_sum(src, seg, n)
kernel_name = 'mk_prb_d2_jaxref_r8_cee307'

def setup_inputs(seed: int=0):
    np.random.seed(seed)
    _w = jnp.asarray

    def _L0_attn_setup():
        import jax, jax.numpy as jnp
        import numpy as np
        DIM = 128
        N_HEADS = 16
        HEAD_DIM = DIM // N_HEADS
        D_LATENT = 32
        B, T = (1, 512)
        key = jax.random.key(seed)
        ks = jax.random.split(key, 6)
        s = 0.02
        return {'x': jax.random.normal(ks[0], (B, T, DIM), dtype=jnp.float32), 'W_DKV': jax.random.normal(ks[1], (DIM, D_LATENT), dtype=jnp.float32) * s, 'W_UK': jax.random.normal(ks[2], (D_LATENT, DIM), dtype=jnp.float32) * s, 'W_UV': jax.random.normal(ks[3], (D_LATENT, DIM), dtype=jnp.float32) * s, 'W_UQ': jax.random.normal(ks[4], (DIM, DIM), dtype=jnp.float32) * s, 'W_O': jax.random.normal(ks[5], (DIM, DIM), dtype=jnp.float32) * s}
    _L0_attn_in = _L0_attn_setup()

    def _L0_ffn_setup():
        import jax, jax.numpy as jnp
        import numpy as np
        BLOCK = 16
        _GRID = jnp.array([0.0, 0.5, 1.0, 1.5, 2.0, 3.0, 4.0, 6.0], dtype=jnp.float32)
        _MID = jnp.array([0.25, 0.75, 1.25, 1.75, 2.5, 3.5, 5.0], dtype=jnp.float32)

        def fp4_quant_dequant(x):
            shape = x.shape
            xb = x.reshape(shape[:-1] + (shape[-1] // BLOCK, BLOCK))
            scale = jnp.max(jnp.abs(xb), axis=-1, keepdims=True) / 6.0
            scale = jnp.maximum(scale, jnp.float32(1e-12))
            xn = xb / scale
            idx = jnp.searchsorted(_MID, jnp.abs(xn))
            q = _GRID[idx] * jnp.sign(xn) * scale
            return q.reshape(shape)

        def fp4_linear(x, w):
            xq = fp4_quant_dequant(x)
            wq = fp4_quant_dequant(w)
            return jnp.einsum('bsk,nk->bsn', xq, wq)
        key = jax.random.key(seed)
        k1, k2, k3, k4 = jax.random.split(key, 4)
        H, I = (128, 352)
        x = jax.random.normal(k1, (4, 512, H), dtype=jnp.float32)
        w_gate = jax.random.normal(k2, (I, H), dtype=jnp.float32) * 0.02
        w_up = jax.random.normal(k3, (I, H), dtype=jnp.float32) * 0.02
        w_down = jax.random.normal(k4, (H, I), dtype=jnp.float32) * 0.02
        return {'x': x, 'w_gate': w_gate, 'w_up': w_up, 'w_down': w_down}
    _L0_ffn_in = _L0_ffn_setup()

    def _L1_attn_setup():
        import jax, jax.numpy as jnp
        import numpy as np
        D_MODEL = 128
        NHEAD = 16
        HEAD_DIM = D_MODEL // NHEAD
        SCALE = float(np.sqrt(HEAD_DIM))
        key = jax.random.key(seed)
        ks = jax.random.split(key, 6)
        B, T = (2, 256)
        x = jax.random.normal(ks[0], (B, T, D_MODEL), dtype=jnp.float32)
        s = 1.0 / np.sqrt(D_MODEL)
        qkv_w = jax.random.uniform(ks[1], (3 * D_MODEL, D_MODEL), jnp.float32, -s, s)
        qkv_b = jax.random.uniform(ks[2], (3 * D_MODEL,), jnp.float32, -s, s)
        out_w = jax.random.uniform(ks[3], (D_MODEL, D_MODEL), jnp.float32, -s, s)
        out_b = jax.random.uniform(ks[4], (D_MODEL,), jnp.float32, -s, s)
        decay_alpha = jnp.full((NHEAD,), 0.1, dtype=jnp.float32)
        return {'x': x, 'qkv_w': qkv_w, 'qkv_b': qkv_b, 'out_w': out_w, 'out_b': out_b, 'decay_alpha': decay_alpha}
    _L1_attn_in = _L1_attn_setup()

    def _L1_ffn_setup():
        import jax, jax.numpy as jnp
        import numpy as np
        E, D, H = (32, 128, 128)
        TOP_K = 2
        key = jax.random.key(seed)
        k0, k1, k2, k3 = jax.random.split(key, 4)
        x = jax.random.normal(k0, (2, 256, D), dtype=jnp.float32)
        Wg = jax.random.normal(k1, (D, E), dtype=jnp.float32) * 0.02
        W1 = jax.random.normal(k2, (E, D, H), dtype=jnp.float32) * 0.02
        b1 = jnp.zeros((E, H), dtype=jnp.float32)
        W2 = jax.random.normal(k3, (E, H, D), dtype=jnp.float32) * 0.02
        b2 = jnp.zeros((E, D), dtype=jnp.float32)
        return {'x': x, 'Wg': Wg, 'W1': W1, 'b1': b1, 'W2': W2, 'b2': b2}
    _L1_ffn_in = _L1_ffn_setup()
    _d = {'L0_attn_x': _L0_attn_in['x'], 'L0_attn_W_DKV': _L0_attn_in['W_DKV'], 'L0_attn_W_UK': _L0_attn_in['W_UK'], 'L0_attn_W_UV': _L0_attn_in['W_UV'], 'L0_attn_W_UQ': _L0_attn_in['W_UQ'], 'L0_attn_W_O': _L0_attn_in['W_O'], 'L0_ffn_w_gate': _L0_ffn_in['w_gate'], 'L0_ffn_w_up': _L0_ffn_in['w_up'], 'L0_ffn_w_down': _L0_ffn_in['w_down'], 'L1_attn_qkv_w': _L1_attn_in['qkv_w'], 'L1_attn_qkv_b': _L1_attn_in['qkv_b'], 'L1_attn_out_w': _L1_attn_in['out_w'], 'L1_attn_out_b': _L1_attn_in['out_b'], 'L1_attn_decay_alpha': _L1_attn_in['decay_alpha'], 'L1_ffn_Wg': _L1_ffn_in['Wg'], 'L1_ffn_W1': _L1_ffn_in['W1'], 'L1_ffn_b1': _L1_ffn_in['b1'], 'L1_ffn_W2': _L1_ffn_in['W2'], 'L1_ffn_b2': _L1_ffn_in['b2']}
    _x0 = _d['L0_attn_x']
    _d['L0_attn_x'] = jax.random.normal(jax.random.fold_in(jax.random.key(seed), 1), (8, 512, 128), dtype=_x0.dtype)
    del _x0
    return _d

def reference(L0_attn_x, L0_attn_W_DKV, L0_attn_W_UK, L0_attn_W_UV, L0_attn_W_UQ, L0_attn_W_O, L0_ffn_w_gate, L0_ffn_w_up, L0_ffn_w_down, L1_attn_qkv_w, L1_attn_qkv_b, L1_attn_out_w, L1_attn_out_b, L1_attn_decay_alpha, L1_ffn_Wg, L1_ffn_W1, L1_ffn_b1, L1_ffn_W2, L1_ffn_b2):

    def _L0_attn_ref(x, W_DKV, W_UK, W_UV, W_UQ, W_O):
        import jax, jax.numpy as jnp
        import numpy as np
        DIM = 128
        N_HEADS = 16
        HEAD_DIM = DIM // N_HEADS
        D_LATENT = 32
        B, T = (1, 512)
        b, t, d = x.shape
        h, hd = (N_HEADS, HEAD_DIM)
        c_kv = x @ W_DKV
        k = (c_kv @ W_UK).reshape(b, t, h, hd)
        v = (c_kv @ W_UV).reshape(b, t, h, hd)
        q = (x @ W_UQ).reshape(b, t, h, hd)
        scale = 1.0 / jnp.sqrt(jnp.asarray(hd, x.dtype))
        scores = jnp.einsum('bqhd,bkhd->bhqk', q, k) * scale
        causal = jnp.tril(jnp.ones((t, t), dtype=bool))
        scores = jnp.where(causal, scores, jnp.asarray(-jnp.inf, scores.dtype))
        probs = jax.nn.softmax(scores, axis=-1)
        ctx = jnp.einsum('bhqk,bkhd->bqhd', probs, v).reshape(b, t, d)
        return ctx @ W_O

    def _L0_ffn_ref(x, w_gate, w_up, w_down):
        import jax, jax.numpy as jnp
        import numpy as np
        BLOCK = 16
        _GRID = jnp.array([0.0, 0.5, 1.0, 1.5, 2.0, 3.0, 4.0, 6.0], dtype=jnp.float32)
        _MID = jnp.array([0.25, 0.75, 1.25, 1.75, 2.5, 3.5, 5.0], dtype=jnp.float32)

        def fp4_quant_dequant(x):
            shape = x.shape
            xb = x.reshape(shape[:-1] + (shape[-1] // BLOCK, BLOCK))
            scale = jnp.max(jnp.abs(xb), axis=-1, keepdims=True) / 6.0
            scale = jnp.maximum(scale, jnp.float32(1e-12))
            xn = xb / scale
            idx = jnp.searchsorted(_MID, jnp.abs(xn))
            q = _GRID[idx] * jnp.sign(xn) * scale
            return q.reshape(shape)

        def fp4_linear(x, w):
            xq = fp4_quant_dequant(x)
            wq = fp4_quant_dequant(w)
            return jnp.einsum('bsk,nk->bsn', xq, wq)
        gate = fp4_linear(x, w_gate)
        y = fp4_linear(x, w_up)
        h = jax.nn.silu(gate) * y
        return fp4_linear(h, w_down)

    def _L1_attn_ref(x, qkv_w, qkv_b, out_w, out_b, decay_alpha):
        import jax, jax.numpy as jnp
        import numpy as np
        D_MODEL = 128
        NHEAD = 16
        HEAD_DIM = D_MODEL // NHEAD
        SCALE = float(np.sqrt(HEAD_DIM))
        B, T, D = x.shape
        qkv = x @ qkv_w.T + qkv_b
        qkv = qkv.reshape(B, T, 3, NHEAD, HEAD_DIM).transpose(2, 0, 3, 1, 4)
        q, k, v = (qkv[0], qkv[1], qkv[2])
        logits = jnp.einsum('bhqd,bhkd->bhqk', q, k) / SCALE
        pos = jnp.arange(T, dtype=jnp.float32)
        dist = jnp.abs(pos[None, :] - pos[:, None])
        alpha = jax.nn.softplus(decay_alpha)
        logits = logits - alpha[:, None, None] * dist[None]
        attn = jax.nn.softmax(logits, axis=-1)
        out = jnp.einsum('bhqk,bhkd->bhqd', attn, v)
        out = out.transpose(0, 2, 1, 3).reshape(B, T, D)
        out = out @ out_w.T + out_b
        return out

    def _L1_ffn_ref(x, Wg, W1, b1, W2, b2):
        import jax, jax.numpy as jnp
        import numpy as np
        E, D, H = (32, 128, 128)
        TOP_K = 2
        orig_shape = x.shape
        xf = x.reshape(-1, x.shape[-1])
        scores = jax.nn.softmax(xf @ Wg, axis=-1)
        top_w, top_idx = jax.lax.top_k(scores, TOP_K)
        top_w = jax.nn.softmax(top_w, axis=-1)
        combine = jnp.sum(jax.nn.one_hot(top_idx, E, dtype=xf.dtype) * top_w[..., None], axis=1)
        hdn = jax.nn.gelu(jnp.einsum('td,edh->eth', xf, W1) + b1[:, None, :], approximate=False)
        y_e = jnp.einsum('eth,ehd->etd', hdn, W2) + b2[:, None, :]
        y = jnp.einsum('etd,te->td', y_e, combine)
        return y.reshape(orig_shape)
    x = L0_attn_x
    xn = _layernorm(x, axis=-1)
    x = x + _L0_attn_ref(xn, L0_attn_W_DKV, L0_attn_W_UK, L0_attn_W_UV, L0_attn_W_UQ, L0_attn_W_O) + _L0_ffn_ref(xn, L0_ffn_w_gate, L0_ffn_w_up, L0_ffn_w_down)
    xn = _layernorm(x, axis=-1)
    x = x + _L1_attn_ref(xn, L1_attn_qkv_w, L1_attn_qkv_b, L1_attn_out_w, L1_attn_out_b, L1_attn_decay_alpha) + _L1_ffn_ref(xn, L1_ffn_Wg, L1_ffn_W1, L1_ffn_b1, L1_ffn_W2, L1_ffn_b2)
    return x

_drawn_inputs = setup_inputs


def setup_inputs(seed=0):
    import zlib

    import numpy as np

    out = dict(_drawn_inputs(seed))
    spreads = {'L1_attn_decay_alpha': (0.10000000149011612, 0.6),
     'L1_ffn_b1': (0.0, 0.8),
     'L1_ffn_b2': (0.0, 0.1)}
    factors = {'L0_attn_W_DKV': 8.0,
     'L0_attn_W_UK': 8.0,
     'L0_attn_W_UV': 8.0,
     'L0_attn_W_UQ': 8.0,
     'L0_attn_W_O': 8.0,
     'L0_ffn_w_gate': 4.307,
     'L0_ffn_w_up': 4.183,
     'L0_ffn_w_down': 4.118,
     'L1_ffn_W1': 3.053,
     'L1_ffn_W2': 2.758,
     'L1_attn_qkv_b': 3.832}
    for name, (base, spread) in spreads.items():
        noise = np.random.default_rng([zlib.crc32(name.encode()), seed]).standard_normal(out[name].shape)
        drawn = base * np.exp(spread * noise) if base else spread * noise
        out[name] = jnp.asarray(drawn.astype(out[name].dtype))
    for name, factor in factors.items():
        out[name] = (out[name] * factor).astype(out[name].dtype)
    return out
```

```python
from contextlib import ExitStack

import numpy as np

import concourse.bass as bass
from concourse import mybir

F32 = mybir.dt.float32
BF16 = mybir.dt.bfloat16
I32 = mybir.dt.int32
ALU = mybir.AluOpType
ACT = mybir.ActivationFunctionType
AX = mybir.AxisListType.X

P = 128
D = 128
SEQS = 8
T = 512
NT = T // P
TILES = SEQS * NT
HEADS = 16
HD = D // HEADS
LATENT = 32
FF = 352
FFC = 3
BLK = 16
EXPERTS = 32
SLOT_TILES = 96
HALF = HEADS // 2
EPS = 1e-5

Q_PARTS = (0, 0, 0, 1, 1, 2)
K_PARTS = (0, 1, 2, 0, 1, 0)
PRODUCT_ROWS = len(Q_PARTS) * HD
BIAS_ROWS = NT * 2 * 3
MAX_ROW = PRODUCT_ROWS + BIAS_ROWS
ROWS = MAX_ROW + 3
A_ROWS = MAX_ROW
NEG = -1e30
ROUND = 1.5 * 2.0 ** 23


def score_units(layer):
    a, b = [], []
    if layer == 1:
        a = [(i, [2 * p, 2 * p + 1]) for p in range(HALF // 2) for i in range(NT)]
        b = [(kt, [h]) for kt in range(NT) for h in range(HALF)]
    else:
        for i in (3, 2, 1, 0):
            n = {3: 2, 2: 2, 1: 4, 0: 8}[i]
            a += [(i, list(range(h, h + n))) for h in range(0, HALF, n)]
        for kt in range(NT):
            n = {0: 1, 1: 1, 2: 2, 3: 4}[kt]
            b += [(kt, list(range(h, h + n))) for h in range(0, HALF, n)]
    return a, b


STEPS = 2 * SEQS + 2
PV_LAG = 2


def projections(layer):
    return ["C", "Q", "K"] if layer == 0 else ["Q", "K"]


def script(layer, k):
    a, b = score_units(layer)
    out = []
    if k == 0:
        out += [("PJ", p) for p in projections(layer)]
    units_a = list(range(len(a))) if k < 2 * SEQS else []
    units_b = list(range(len(b))) if k >= 2 else []
    side = []
    if 1 <= k <= 2 * SEQS:
        side.append(("MT", 0))
    if k % 2 == 0 and k < 2 * SEQS:
        side.append(("V", 0))
    if k % 2 == 0 and k // 2 + 1 < SEQS:
        side += [("PN", p) for p in projections(layer)]
    if k % 2 == 1 and k >= 3:
        side.append(("OT", 0))
    held = 4 if (k % 2 == 1 and k >= 3 and units_a) else 0
    body_a = units_a[:len(units_a) - held]
    late_a = units_a[len(units_a) - held:]
    done_b = 0
    n_slots = max(len(body_a), 1)
    for s in range(n_slots):
        if s < len(body_a):
            out.append(("A", body_a[s]))
        upto = len(units_b) * (s + 1) // n_slots
        while done_b < upto:
            out.append(("B", done_b))
            if done_b >= PV_LAG:
                out.append(("PV", done_b - PV_LAG))
            done_b += 1
        if s % 2 == 1 and side:
            out.append(side.pop(0))
    out += side
    if units_b:
        out += [("PV", m) for m in range(len(units_b) - PV_LAG, len(units_b))]
        out.append(("OC", 0))
    if k % 2 == 1 and k >= 3:
        tail = [("OT", 1), ("ONT", 0), ("WO", 0)]
        if late_a:
            out.append(("A", late_a[0]))
            for n, item in enumerate(tail):
                out += [item, ("A", late_a[n + 1])]
        else:
            out += tail
    return out


class Counts:

    def __init__(self, per_step):
        self.c = [0]
        for n in per_step:
            self.c.append(self.c[-1] + n)
        self.round = self.c[6] - self.c[2]
        assert self.c[10] - self.c[6] == self.round == self.c[14] - self.c[10]

    def at(self, k, g):
        return self.c[k] + g * self.round if 2 <= k <= 6 else self.c[k]


def run_steps(engine, step):
    step(0, 0)
    step(1, 0)
    with engine.Fori(0, 3) as g:
        for r in range(4):
            step(2 + r, g)
    for k in range(14, STEPS):
        step(k, 0)


MISC = ("PJ", "PN", "V", "MT", "OT", "ONT", "WO")


class Net:
    def __init__(self, nc, ins, out):
        self.nc, self.ins, self.out = nc, ins, out
        self.ctx = ExitStack()

    def sb(self, name, shape, dt=F32, ctx=None):
        return (ctx or self.ctx).enter_context(self.nc.sbuf_tensor(name, shape, dt))

    def pb(self, name, shape, dt=F32, ctx=None):
        return (ctx or self.ctx).enter_context(self.nc.psum_tensor(name, shape, dt))

    def sem(self, name, ctx=None):
        return (ctx or self.ctx).enter_context(self.nc.semaphore(name))

    def dram(self, name, shape, dt=F32):
        return self.nc.dram_tensor(name, shape, dt, kind="Internal").ap()



def load_constants(n):
    nc, I = n.nc, n.ins
    n.x = n.sb("x", [P, TILES, D])
    n.ident = n.sb("ident", [P, P])
    n.identb = n.sb("identb", [P, P], BF16)
    n.mask_q = n.sb("mask_q", [P, P], BF16)
    n.mask_k = n.sb("mask_k", [P, P], BF16)
    n.dist = n.sb("dist", [P, P], BF16)
    n.ones = n.sb("ones", [1, P])
    n.zeros = n.sb("zeros", [P, T])
    n.ones_b = n.sb("ones_b", [P, P], BF16)
    n.upper = n.sb("upper", [P, P], BF16)
    n.xnT_dram = n.dram("xnT_dram", (SEQS, D, T))
    n.const_sem = n.sem("constants_loaded")
    n.x_sem = n.sem("x_loaded")
    n.memset_sem = n.sem("ones_set")
    x_v = I["L0_attn_x"].rearrange("b (i p) d -> p (b i) d", p=P)
    with nc.Block() as block:
        @block.sync
        def _(sp):
            sp.dma_start(n.ident[:], I["c_ident"]).then_inc(n.x_sem, 16)
            for s in range(4):
                sp.dma_start(n.x[:, 8 * s:8 * s + 8, :], x_v[:, 8 * s:8 * s + 8, :]).then_inc(n.x_sem, 16)
            sp.wait_ge(n.const_sem, 16 * 5)
            sp.wait_ge(n.x_sem, 16 * 5)

        @block.gpsimd
        def _(pool):
            for dst, src in ((n.identb, "c_ident"), (n.mask_q, "c_mask_q"), (n.mask_k, "c_mask_k"),
                             (n.dist, "c_dist"), (n.upper, "c_upper")):
                pool.dma_start(dst[:], I[src]).then_inc(n.const_sem, 16)

        @block.vector
        def _(dve):
            dve.memset(n.ones[:], 1.0)
            dve.memset(n.zeros[:], 0.0)
            dve.memset(n.ones_b[:], 1.0).then_inc(n.memset_sem, 1)
            dve.wait_ge(n.memset_sem, 1)



MIDS_LOW = (0.25, 0.75, 1.25, 1.75)


def quant_scales(dve, ab, am, sc, rs, half, sem, base):
    dve.tensor_reduce(am, ab, AX, ALU.max).then_inc(sem, 1)
    dve.wait_ge(sem, base + 1)
    dve.tensor_scalar(sc, am, 1.0 / 6.0, 1e-12, ALU.mult, ALU.max).then_inc(sem, 1)
    dve.wait_ge(sem, base + 2)
    dve.tensor_scalar(half, sc, 0.5, None, ALU.mult).then_inc(sem, 1)
    dve.reciprocal(rs, sc).then_inc(sem, 1)


def quant_grid(dve, a, u, t, sem, base):
    dve.tensor_scalar(u, a, 5.0, 2.0, ALU.is_gt, ALU.mult).then_inc(sem, 1)
    dve.tensor_scalar(t, a, MIDS_LOW[0], None, ALU.is_gt).then_inc(sem, 1)
    dve.wait_ge(sem, base + 1)
    dve.scalar_tensor_tensor(u, a, 3.5, u, ALU.is_gt, ALU.add).then_inc(sem, 1)
    dve.wait_ge(sem, base + 2)
    dve.scalar_tensor_tensor(t, a, MIDS_LOW[1], t, ALU.is_gt, ALU.add).then_inc(sem, 1)
    dve.wait_ge(sem, base + 3)
    dve.scalar_tensor_tensor(u, a, 2.5, u, ALU.is_gt, ALU.add).then_inc(sem, 1)
    dve.wait_ge(sem, base + 4)
    dve.scalar_tensor_tensor(t, a, MIDS_LOW[2], t, ALU.is_gt, ALU.add).then_inc(sem, 1)
    dve.wait_ge(sem, base + 6)
    dve.scalar_tensor_tensor(t, a, MIDS_LOW[3], t, ALU.is_gt, ALU.add).then_inc(sem, 1)
    dve.wait_ge(sem, base + 7)
    dve.scalar_tensor_tensor(t, u, 2.0, t, ALU.mult, ALU.add).then_inc(sem, 1)


SCALES_INC, GRID_INC = 4, 8


def bc(ap, n):
    return ap.unsqueeze(2).broadcast_to([ap.shape[0], ap.shape[1], n])


def blocks(ap):
    return ap.rearrange("p (m k) -> p m k", k=BLK)



def layernorm_stats(n, layer):
    nc = n.nc
    with ExitStack() as c:
        st = n.sb(f"bn{layer}", [P, TILES, 6], ctx=c)
        dm = n.sb(f"bn_dm{layer}", [P, TILES], ctx=c)
        m2 = n.sb(f"bn_m2{layer}", [P, TILES], ctx=c)
        sd = n.sb(f"bn_sd{layer}", [P, TILES], ctx=c)
        s = n.sem(f"stats_step{layer}", c)
        s_sd = n.sem(f"sd_ready{layer}", c)
        with nc.Block() as block:
            @block.vector
            def _(dve):
                with dve.Fori(0, SEQS) as b:
                    for i in range(NT):
                        dve.bn_stats(st[:, bass.ds(b * NT + i, 1), :].rearrange("p o k -> p (o k)"),
                                     n.x[:, bass.ds(b * NT + i, 1), :].rearrange("p o k -> p (o k)")).then_inc(s, 1)
                v = TILES
                dve.wait_ge(s, v)
                dve.tensor_tensor(n.mean[:], st[:, :, 1], st[:, :, 4], ALU.add).then_inc(s, 1)
                dve.tensor_tensor(dm[:], st[:, :, 1], st[:, :, 4], ALU.subtract).then_inc(s, 1)
                dve.tensor_tensor(m2[:], st[:, :, 2], st[:, :, 5], ALU.add).then_inc(s, 1)
                dve.wait_ge(s, v + 3)
                dve.tensor_scalar(n.mean[:], n.mean[:], 0.5, None, ALU.mult).then_inc(s, 1)
                dve.tensor_tensor(dm[:], dm[:], dm[:], ALU.mult).then_inc(s, 1)
                dve.wait_ge(s, v + 5)
                dve.scalar_tensor_tensor(m2[:], dm[:], float(P // 4), m2[:], ALU.mult, ALU.add).then_inc(s, 1)
                dve.wait_ge(s, v + 6)
                dve.tensor_scalar(m2[:], m2[:], 1.0 / D, EPS, ALU.mult, ALU.add).then_inc(s, 1)
                dve.wait_ge(s_sd, 1)
                dve.reciprocal(n.rstd[:], sd[:]).then_inc(s, 1)
                dve.wait_ge(s, v + 8)

            @block.scalar
            def _(act):
                act.wait_ge(s, TILES + 7)
                act.activation(sd[:], m2[:], ACT.Sqrt).then_inc(s_sd, 1)



def prepare_ffn_weights(n, c):
    nc, I = n.nc, n.ins
    W = 2 * FFC * D + FF
    n.wguT = n.sb("wguT", [P, 2 * FF], ctx=c)
    n.wdT = n.sb("wdT", [P, FFC, D], ctx=c)
    with ExitStack() as k:
        w = n.sb("w_raw", [P, W], ctx=k)
        ab = n.sb("w_abs", [P, W], ctx=k)
        sg = n.sb("w_sign", [P, W], ctx=k)
        t = n.sb("w_t", [P, W], ctx=k)
        u = n.sb("w_u", [P, W], ctx=k)
        am, sc, rs, hs = (n.sb(f"w_{x}", [P, W // BLK], ctx=k) for x in ("am", "sc", "rs", "hs"))
        ps = n.pb("w_ps", [P, 3, 512], ctx=k)
        zeroed, loaded, signed, scaled, normed, gridded, quantised, turned, kept = (
            n.sem(f"w_{x}", k) for x in ("zeroed", "loaded", "signed", "scaled", "normed", "gridded",
                                         "quantised", "turned", "kept"))
        rem = FF - 2 * P
        with nc.Block() as block:
            @block.sync
            def _(sp):
                sp.wait_ge(zeroed, 1)
                for s, name in enumerate(("L0_ffn_w_gate", "L0_ffn_w_up")):
                    for q in range(FFC):
                        r = P if q < 2 else rem
                        sp.dma_start(w[0:r, (s * FFC + q) * D:(s * FFC + q + 1) * D],
                                     I[name][q * P:q * P + r, :]).then_inc(loaded, 16)
                sp.dma_start(w[:, 2 * FFC * D:], I["L0_ffn_w_down"]).then_inc(loaded, 16)

            @block.scalar
            def _(act):
                act.wait_ge(loaded, 16 * 7)
                act.activation(ab[:], w[:], ACT.Abs).then_inc(signed, 1)
                act.activation(sg[:], w[:], ACT.Sign).then_inc(signed, 1)
                act.wait_ge(turned, 2)
                act.activation(n.wguT[:, 0:FF], ps[:, 0, 0:FF], ACT.Copy).then_inc(kept, 1)
                act.activation(n.wguT[:, FF:2 * FF], ps[:, 1, 0:FF], ACT.Copy).then_inc(kept, 1)
                act.wait_ge(turned, 3)
                act.activation(n.wdT[:, 0:2, :], ps[:, 2, 0:2 * D].rearrange("p (c d) -> p c d", c=2),
                               ACT.Copy).then_inc(kept, 1)
                act.activation(n.wdT[0:rem, 2, :], ps[0:rem, 2, 2 * D:3 * D], ACT.Copy).then_inc(kept, 1)
                act.wait_ge(kept, 4)

            @block.vector
            def _(dve):
                dve.memset(w[:], 0.0).then_inc(zeroed, 1)
                dve.wait_ge(signed, 1)
                quant_scales(dve, blocks(ab[:]), am[:], sc[:], rs[:], hs[:], scaled, 0)
                dve.wait_ge(normed, 1)
                quant_grid(dve, ab[:], u[:], t[:], gridded, 0)

            @block.gpsimd
            def _(pool):
                pool.wait_ge(scaled, SCALES_INC)
                pool.tensor_tensor(blocks(ab[:]), blocks(ab[:]), bc(rs[:], BLK), ALU.mult).then_inc(normed, 1)
                pool.wait_ge(gridded, GRID_INC)
                pool.tensor_tensor(blocks(t[:]), blocks(t[:]), bc(hs[:], BLK), ALU.mult).then_inc(quantised, 1)
                pool.wait_ge(quantised, 1)
                pool.wait_ge(signed, 2)
                pool.tensor_tensor(t[:], t[:], sg[:], ALU.mult).then_inc(quantised, 1)

            @block.tensor
            def _(pe):
                pe.wait_ge(quantised, 2)
                for s in range(2):
                    for q in range(FFC):
                        r = P if q < 2 else rem
                        m = pe.transpose(ps[:, s, q * P:q * P + r],
                                         t[0:r, (s * FFC + q) * D:(s * FFC + q + 1) * D], n.ident[0:r, 0:r])
                    m.then_inc(turned, 1)
                for q in range(FFC):
                    r = P if q < 2 else rem
                    m = pe.transpose(ps[0:r, 2, q * D:(q + 1) * D],
                                     t[:, 2 * FFC * D + q * P:2 * FFC * D + q * P + r], n.ident[:])
                m.then_inc(turned, 1)


def run_ffn_steps(engine, stages):
    def iteration(it, shift):
        for off, f in stages:
            b = it + off
            if 0 <= b < SEQS:
                f(b + 2 * shift, b % 2)
    for it in (-2, -1, 0, 1):
        iteration(it, 0)
    with engine.Fori(0, 2) as g:
        for it in (2, 3):
            iteration(it, g)
    for it in range(6, SEQS + 1):
        iteration(it, 0)


def ffn(n):
    nc = n.nc
    HW = NT * FF
    with ExitStack() as c:
        prepare_ffn_weights(n, c)
        buf = {}
        for w, size in (("x", T), ("h", HW)):
            for name in ("v", "ab", "sg", "t"):
                buf[w + name] = n.sb(f"f_{w}{name}", [P, 2, size], ctx=c)
            buf[w + "u"] = n.sb(f"f_{w}u", [P, size], ctx=c)
            for name in ("am", "sc"):
                buf[w + name] = n.sb(f"f_{w}{name}", [P, size // BLK], ctx=c)
            for name in ("rs", "hs"):
                buf[w + name] = n.sb(f"f_{w}{name}", [P, 2, size // BLK], ctx=c)
        xqT = n.sb("f_xqT", [P, T], ctx=c)
        xnT = n.sb("f_xnT", [P, 2, T], ctx=c)
        silu = n.sb("f_silu", [P, 2, FF], ctx=c)
        hqT = n.sb("f_hqT", [P, FFC, T], ctx=c)
        ps_n = n.pb("f_ps_n", [P, T], ctx=c)
        ps_x = n.pb("f_ps_x", [P, T], ctx=c)
        ps_g = n.pb("f_ps_g", [P, 2, 512], ctx=c)
        ps_u = n.pb("f_ps_u", [P, 2, 512], ctx=c)
        ps_h = n.pb("f_ps_h", [P, T], ctx=c)
        ps_d = n.pb("f_ps_d", [P, NT, D], ctx=c)
        S = {x: n.sem("ffn_" + x, c) for x in (
            "normed", "xn_turned", "xn_kept", "x_split", "x_scaled", "x_div", "x_grid", "x_q",
            "xq_turned", "xq_kept", "gate_up", "silu", "h_ready", "h_split", "h_scaled", "h_div",
            "h_grid", "h_q", "hq_turned", "hq_kept", "down", "added")}
        stored = [n.sem(f"ffn_xnT_stored{p}", c) for p in range(2)]
        rem = FF - 2 * P

        with nc.Block() as block:
            @block.sync
            def _(sp):
                with sp.Fori(0, SEQS // 2) as g:
                    for p in range(2):
                        b = 2 * g + p
                        sp.wait_ge(S["xn_kept"], b + 1)
                        sp.dma_start(n.xnT_dram[bass.ds(b, 1)].rearrange("o d t -> d (o t)"),
                                     xnT[:, p, :]).then_inc(stored[p], 16)
                for p in range(2):
                    sp.wait_ge(stored[p], 16 * SEQS // 2)

            @block.vector
            def _(dve):
                def s1(b, p):
                    if not (isinstance(b, int) and b < 2):
                        dve.wait_ge(S["x_split"], 2 * (b - 1))
                        dve.wait_ge(S["xn_turned"], b - 1)
                    for i in range(NT):
                        tile = b * NT + i
                        dve.tensor_scalar(buf["xv"][:, p, i * D:(i + 1) * D],
                                          n.x[:, bass.ds(tile, 1), :].rearrange("p o k -> p (o k)"),
                                          n.mean[:, bass.ds(tile, 1)], n.rstd[:, bass.ds(tile, 1)],
                                          ALU.subtract, ALU.mult).then_inc(S["normed"], 1)
                    dve.wait_ge(S["x_split"], 2 * b + 1)
                    if not (isinstance(b, int) and b < 2):
                        dve.wait_ge(S["x_q"], 2 * (b - 1))
                    quant_scales(dve, blocks(buf["xab"][:, p]), buf["xam"][:], buf["xsc"][:],
                                 buf["xrs"][:, p], buf["xhs"][:, p], S["x_scaled"], SCALES_INC * b)

                def s3(b, p):
                    dve.wait_ge(S["x_div"], b + 1)
                    if not (isinstance(b, int) and b < 2):
                        dve.wait_ge(S["xq_turned"], b - 1)
                    quant_grid(dve, buf["xab"][:, p], buf["xu"][:], buf["xt"][:, p], S["x_grid"], GRID_INC * b)

                def s5(b, p):
                    if not (isinstance(b, int) and b < 2):
                        dve.wait_ge(S["h_split"], 2 * (b - 1))
                    for i in range(NT):
                        dve.wait_ge(S["silu"], NT * b + i + 1)
                        dve.tensor_tensor(buf["hv"][:, p, i * FF:(i + 1) * FF], ps_u[:, i % 2, 0:FF],
                                          silu[:, i % 2, :], ALU.mult).then_inc(S["h_ready"], 1)

                def s6(b, p):
                    dve.wait_ge(S["h_split"], 2 * b + 1)
                    if not (isinstance(b, int) and b < 2):
                        dve.wait_ge(S["h_q"], 2 * (b - 1))
                    quant_scales(dve, blocks(buf["hab"][:, p]), buf["ham"][:], buf["hsc"][:],
                                 buf["hrs"][:, p], buf["hhs"][:, p], S["h_scaled"], SCALES_INC * b)

                def s8(b, p):
                    dve.wait_ge(S["h_div"], b + 1)
                    if not (isinstance(b, int) and b < 2):
                        dve.wait_ge(S["hq_turned"], FFC * (b - 1))
                    quant_grid(dve, buf["hab"][:, p], buf["hu"][:], buf["ht"][:, p], S["h_grid"], GRID_INC * b)

                def s10(b, p):
                    dve.wait_ge(S["down"], b + 1)
                    xv = n.x[:, bass.ds(b * NT, NT), :]
                    dve.tensor_tensor(xv, ps_d[:], xv, ALU.add).then_inc(S["added"], 1)

                run_ffn_steps(dve, [(1, s3), (0, s6), (2, s1), (0, s8), (1, s5), (-1, s10)])
                dve.wait_ge(S["added"], SEQS)

            @block.scalar
            def _(act):
                def a1(b, p):
                    act.wait_ge(S["normed"], NT * b + NT)
                    if not (isinstance(b, int) and b < 2):
                        act.wait_ge(S["x_grid"], GRID_INC * (b - 1))
                        act.wait_ge(S["x_q"], 2 * (b - 1))
                    act.activation(buf["xab"][:, p], buf["xv"][:, p], ACT.Abs).then_inc(S["x_split"], 1)
                    act.activation(buf["xsg"][:, p], buf["xv"][:, p], ACT.Sign).then_inc(S["x_split"], 1)
                    act.wait_ge(S["xn_turned"], b + 1)
                    if not (isinstance(b, int) and b < 2):
                        act.wait_ge(stored[p], 8 * (b - p))
                    act.activation(xnT[:, p, :], ps_n[:], ACT.Copy).then_inc(S["xn_kept"], 1)

                def a5(b, p):
                    act.wait_ge(S["xq_turned"], b + 1)
                    if not (isinstance(b, int) and b < 1):
                        act.wait_ge(S["gate_up"], NT * b)
                    act.activation(xqT[:], ps_x[:], ACT.Copy).then_inc(S["xq_kept"], 1)
                    for i in range(NT):
                        act.wait_ge(S["gate_up"], NT * b + i + 1)
                        if i >= 2:
                            act.wait_ge(S["h_ready"], NT * b + i - 1)
                        elif not (isinstance(b, int) and b < 1):
                            act.wait_ge(S["h_ready"], NT * b + i - 1)
                        act.activation(silu[:, i % 2, :], ps_g[:, i % 2, 0:FF], ACT.Silu).then_inc(S["silu"], 1)

                def a6(b, p):
                    act.wait_ge(S["h_ready"], NT * b + NT)
                    if not (isinstance(b, int) and b < 2):
                        act.wait_ge(S["h_grid"], GRID_INC * (b - 1))
                        act.wait_ge(S["h_q"], 2 * (b - 1))
                    act.activation(buf["hab"][:, p], buf["hv"][:, p], ACT.Abs).then_inc(S["h_split"], 1)
                    act.activation(buf["hsg"][:, p], buf["hv"][:, p], ACT.Sign).then_inc(S["h_split"], 1)

                def a10(b, p):
                    for q in range(FFC):
                        act.wait_ge(S["hq_turned"], FFC * b + q + 1)
                        if not (isinstance(b, int) and b < 1):
                            act.wait_ge(S["down"], b)
                        r = P if q < 2 else rem
                        act.activation(hqT[0:r, q, :], ps_h[0:r, :], ACT.Copy).then_inc(S["hq_kept"], 1)

                run_ffn_steps(act, [(0, a6), (2, a1), (1, a5), (-1, a10)])

            @block.gpsimd
            def _(pool):
                def divide(w, b, p):
                    pool.wait_ge(S[w + "_scaled"], SCALES_INC * (b + 1))
                    v = blocks(buf[w + "ab"][:, p])
                    pool.tensor_tensor(v, v, bc(buf[w + "rs"][:, p], BLK), ALU.mult).then_inc(S[w + "_div"], 1)

                def scale(w, b, p):
                    pool.wait_ge(S[w + "_grid"], GRID_INC * (b + 1))
                    v = blocks(buf[w + "t"][:, p])
                    pool.tensor_tensor(v, v, bc(buf[w + "hs"][:, p], BLK), ALU.mult).then_inc(S[w + "_q"], 1)
                    pool.wait_ge(S[w + "_q"], 2 * b + 1)
                    pool.wait_ge(S[w + "_split"], 2 * b + 2)
                    pool.tensor_tensor(buf[w + "t"][:, p], buf[w + "t"][:, p], buf[w + "sg"][:, p],
                                       ALU.mult).then_inc(S[w + "_q"], 1)

                run_ffn_steps(pool, [(1, lambda b, p: scale("x", b, p)), (0, lambda b, p: divide("h", b, p)),
                                     (2, lambda b, p: divide("x", b, p)), (0, lambda b, p: scale("h", b, p))])

            @block.tensor
            def _(pe):
                def p1(b, p):
                    pe.wait_ge(S["normed"], NT * b + NT)
                    if not (isinstance(b, int) and b < 1):
                        pe.wait_ge(S["xn_kept"], b)
                    for i in range(NT):
                        m = pe.transpose(ps_n[:, i * P:(i + 1) * P], buf["xv"][:, p, i * D:(i + 1) * D], n.ident[:])
                    m.then_inc(S["xn_turned"], 1)

                def p5(b, p):
                    pe.wait_ge(S["x_q"], 2 * b + 2)
                    if not (isinstance(b, int) and b < 1):
                        pe.wait_ge(S["xq_kept"], b)
                    for i in range(NT):
                        m = pe.transpose(ps_x[:, i * P:(i + 1) * P], buf["xt"][:, p, i * D:(i + 1) * D], n.ident[:])
                    m.then_inc(S["xq_turned"], 1)
                    pe.wait_ge(S["xq_kept"], b + 1)
                    for i in range(NT):
                        if i >= 2 or not (isinstance(b, int) and b < 1):
                            pe.wait_ge(S["h_ready"], NT * b + i - 1)
                        pe.matmul(ps_g[:, i % 2, 0:FF], xqT[:, i * P:(i + 1) * P], n.wguT[:, 0:FF], start=True, stop=True)
                        pe.matmul(ps_u[:, i % 2, 0:FF], xqT[:, i * P:(i + 1) * P], n.wguT[:, FF:2 * FF],
                                  start=True, stop=True).then_inc(S["gate_up"], 1)

                def p10(b, p):
                    pe.wait_ge(S["h_q"], 2 * b + 2)
                    for q in range(FFC):
                        if q or not (isinstance(b, int) and b < 1):
                            pe.wait_ge(S["hq_kept"], FFC * b + q)
                        r = P if q < 2 else rem
                        for i in range(NT):
                            m = pe.transpose(ps_h[0:r, i * P:(i + 1) * P],
                                             buf["ht"][:, p, i * FF + q * P:i * FF + q * P + r], n.ident[:])
                        m.then_inc(S["hq_turned"], 1)
                    pe.wait_ge(S["hq_kept"], FFC * (b + 1))
                    if not (isinstance(b, int) and b < 1):
                        pe.wait_ge(S["added"], b)
                    for i in range(NT):
                        for q in range(FFC):
                            r = P if q < 2 else rem
                            m = pe.matmul(ps_d[:, i, :], hqT[0:r, q, i * P:(i + 1) * P], n.wdT[0:r, q, :],
                                          start=(q == 0), stop=(q == FFC - 1))
                    m.then_inc(S["down"], 1)

                run_ffn_steps(pe, [(2, p1), (1, p5), (-1, p10)])



def softplus_rows(n, c):
    nc, I = n.nc, n.ins
    n.alpha_eye = n.sb("alpha_eye", [P, HEADS, 3, P], BF16, ctx=c)
    n.qrows = n.dram("qrows", (HEADS, BIAS_ROWS, T), BF16)
    A = HEADS + 1
    with ExitStack() as k:
        raw = n.sb("al_raw", [P, A], ctx=k)
        neg = n.sb("al_neg", [P, A], ctx=k)
        e = n.sb("al_e", [P, A], ctx=k)
        al = n.sb("alpha", [P, A], ctx=k)
        ap = n.sb("alpha_parts", [P, 3, A], BF16, ctx=k)
        apf = n.sb("alpha_parts_f", [P, 3, A], ctx=k)
        pat = n.sb("al_pat", [P, T], ctx=k)
        qb = n.sb("al_rows", [P, 3, T], BF16, ctx=k)
        loaded, stored = n.sem("al_loaded", k), n.sem("al_stored", k)
        v, a = n.sem("al_vec", k), n.sem("al_act", k)
        with nc.Block() as block:
            @block.sync
            def _(sp):
                sp.dma_start(raw[:, 0:1], I["alpha_rows"]).then_inc(loaded, 16)
                sp.dma_start(raw[:, 1:A], I["alpha_all"]).then_inc(loaded, 16)
                sp.dma_start(pat[:], I["c_qpat"]).then_inc(loaded, 16)
                sp.wait_ge(v, 14)
                sp.dma_start(n.qrows.rearrange("h (r s) t -> (h r) s t", s=3), qb[:]).then_inc(stored, 16)
                sp.wait_ge(stored, 16)

            @block.scalar
            def _(act):
                act.wait_ge(v, 2)
                act.activation(e[:], neg[:], ACT.Exp).then_inc(a, 1)
                act.wait_ge(v, 3)
                act.activation(e[:], e[:], ACT.Ln).then_inc(a, 1)

            @block.vector
            def _(dve):
                step = 0

                def then(ins):
                    nonlocal step
                    ins.then_inc(v, 1)
                    step += 1
                    dve.wait_ge(v, step)
                dve.wait_ge(loaded, 48)
                then(dve.tensor_scalar(neg[:], raw[:], -1.0, None, ALU.mult))
                then(dve.tensor_tensor(neg[:], neg[:], raw[:], ALU.min))
                dve.wait_ge(a, 1)
                then(dve.tensor_scalar(e[:], e[:], 1.0, None, ALU.add))
                dve.wait_ge(a, 2)
                then(dve.scalar_tensor_tensor(al[:], raw[:], 0.0, e[:], ALU.max, ALU.add))
                then(dve.tensor_copy(ap[:, 0, :], al[:]))
                then(dve.tensor_tensor(e[:], al[:], ap[:, 0, :], ALU.subtract))
                then(dve.tensor_copy(ap[:, 1, :], e[:]))
                then(dve.tensor_tensor(ap[:, 2, :], e[:], ap[:, 1, :], ALU.subtract))
                then(dve.tensor_scalar(pat[:], pat[:], al[:, 0:1], None, ALU.mult))
                then(dve.tensor_copy(qb[:, 0, :], pat[:]))
                then(dve.tensor_tensor(pat[:], pat[:], qb[:, 0, :], ALU.subtract))
                then(dve.tensor_copy(qb[:, 1, :], pat[:]))
                then(dve.tensor_tensor(qb[:, 2, :], pat[:], qb[:, 1, :], ALU.subtract))
                then(dve.tensor_copy(apf[:], ap[:]))
                for h in range(HEADS):
                    for s in range(3):
                        m = dve.tensor_scalar(n.alpha_eye[:, h, s, :], n.identb[:], apf[:, s, 1 + h:2 + h], None,
                                              ALU.mult)
                then(m)


def attention(n, layer):
    nc, I = n.nc, n.ins
    c = ExitStack()
    with c:
        if layer == 1:
            softplus_rows(n, c)
        L = f"a{layer}_"
        wq = n.sb(L + "wq", [P, D], ctx=c)
        wk = n.sb(L + "wk", [P, D], ctx=c)
        wv = n.sb(L + "wv", [P, D], ctx=c)
        wo = n.sb(L + "wo", [P, D], ctx=c)
        bq = n.sb(L + "bq", [P, 1], ctx=c)
        bqs = n.sb(L + "bqs", [P, 1], ctx=c)
        bk = n.sb(L + "bk", [P, 1], ctx=c)
        bv = n.sb(L + "bv", [1, D], ctx=c)
        bo = n.sb(L + "bo", [1, D], ctx=c)
        wdkv = n.sb(L + "wdkv", [P, LATENT], ctx=c)
        ckv = n.sb(L + "ckv", [LATENT, 2, T], ctx=c)
        Q = n.sb(L + "Q", [ROWS, 4, HALF, T], BF16, ctx=c)
        K = n.sb(L + "K", [ROWS, 4, HALF, T], BF16, ctx=c)
        xnT = n.sb(L + "xnT", [P, 2, T], ctx=c)
        qkf = n.sb(L + "qkf", [P, 2, T], ctx=c)
        parts = n.sb(L + "parts", [P, 2, 3, T], BF16, ctx=c)
        maxes = n.sb(L + "maxes", [P, 2, NT, HALF], ctx=c)
        nm = n.sb(L + "nm", [HALF, T], ctx=c)
        mparts = n.sb(L + "mparts", [HALF, 2, 3, T], BF16, ctx=c)
        V = n.sb(L + "V", [P, 2, NT, 4, 4, 32], ctx=c)
        Pt = n.sb(L + "Pt", [P, 4, T], ctx=c)
        Ob = n.sb(L + "Ob", [P, 2, T], ctx=c)
        rden = n.sb(L + "rden", [P, 2, 4 * NT, 2], ctx=c)
        ON = n.sb(L + "ON", [P, NT, D], ctx=c)
        ONT = n.sb(L + "ONT", [P, T], ctx=c)
        psA = n.pb(L + "psA", [P, 2, 2, T], ctx=c)
        psB = n.pb(L + "psB", [P, 2, T], ctx=c)
        psO = n.pb(L + "psO", [P, T], ctx=c)
        psM = n.pb(L + "psM", [P, T], ctx=c)
        scr = n.dram(L + "stack", (2, 2, HEADS, PRODUCT_ROWS, T), BF16)
        a_ready = n.sem(L + "scores_for_max_ready", c)
        a_free = n.sem(L + "maxima_taken", c)
        b_ready = n.sem(L + "scores_for_exp_ready", c)
        p_ready = n.sem(L + "exp_ready", c)
        pv_done = n.sem(L + "pv_done", c)
        misc_ready = n.sem(L + "misc_ready", c)
        misc_free = n.sem(L + "misc_read", c)
        o_copied = n.sem(L + "outputs_copied", c)
        den_ready = n.sem(L + "den_ready", c)
        split_step = n.sem(L + "split_step", c)
        parts_ready = n.sem(L + "parts_ready", c)
        parts_written = n.sem(L + "parts_written", c)
        xnT_loaded = [n.sem(L + f"xnT_loaded{p}", c) for p in range(2)]
        stack_loaded = [n.sem(L + f"stack_loaded{s}", c) for s in range(4)]
        max_ready = n.sem(L + "max_parts_ready", c)
        max_loaded = [n.sem(L + f"max_loaded{s}", c) for s in range(4)]
        w_loaded = n.sem(L + "weights_loaded", c)
        k_const = n.sem(L + "key_rows_loaded", c)
        zeroed = n.sem(L + "zeroed", c)
        bias_rows = n.sem(L + "bias_rows_loaded", c)
        scaled = n.sem(L + "bias_scaled", c)

        units_a, units_b = score_units(layer)
        scripts = [script(layer, k) for k in range(STEPS)]

        def counts(*kinds):
            return Counts([sum(x[0] in kinds for x in scripts[k]) for k in range(STEPS)])
        nA, nB, nM, nO = counts("A"), counts("B"), counts(*MISC), counts("OC")
        nMT = counts("MT")
        nQK = Counts([sum(x[0] in ("PJ", "PN") and x[1] != "C" for x in scripts[k]) for k in range(STEPS)])
        nOT = counts("OT")
        SCALE = float(1.0 / np.sqrt(np.float32(HD)))

        def misc_index(k, g, pos):
            return nM.at(k, g) + sum(x[0] in MISC for x in scripts[k][:pos])


        def loads(hb, g):
            return hb // 4 + 1 + g

        with nc.Block() as block:
            @block.sync
            def _(sp):
                if layer == 0:
                    loads_ = [(wq[:], I["L0_attn_W_UQ"]), (wdkv[:], I["L0_attn_W_DKV"]),
                              (wk[0:LATENT, :], I["L0_attn_W_UK"]), (wv[0:LATENT, :], I["L0_attn_W_UV"])]
                    wo_src = I["L0_attn_W_O"]
                else:
                    qkv, b = I["qkv_wT"], I["L1_attn_qkv_b"]
                    loads_ = [(wq[:], qkv[:, 0:D]), (wk[:], qkv[:, D:2 * D]), (wv[:], qkv[:, 2 * D:3 * D]),
                              (bq[:], b[0:D].unsqueeze(1)), (bk[:], b[D:2 * D].unsqueeze(1)),
                              (bv[:], b[2 * D:3 * D].unsqueeze(0)), (bo[:], I["L1_attn_out_b"].unsqueeze(0))]
                    wo_src = I["out_wT"]
                wo_v = wo_src.rearrange("(r j d) n -> j r d n", j=4, d=HD)
                for j in range(4):
                    for r in range(4):
                        loads_.append((wo[32 * j + HD * r:32 * j + HD * (r + 1), :], wo_v[j, r]))
                for dst, src in loads_:
                    sp.dma_start(dst, src).then_inc(w_loaded, 16)
                sp.wait_ge(w_loaded, 16 * len(loads_))
                if layer == 1:
                    sp.wait_ge(zeroed, 2)
                    for s in range(4):
                        sp.dma_start(Q[PRODUCT_ROWS:MAX_ROW, s],
                                     n.qrows[HALF * (s % 2):HALF * (s % 2 + 1)].rearrange("h r t -> r h t")
                                     ).then_inc(bias_rows, 16)
                    sp.wait_ge(bias_rows, 64)

            @block.gpsimd
            def _(pool):
                for s in range(4):
                    pool.dma_start(K[PRODUCT_ROWS:ROWS, s],
                                   I["c_krows"].unsqueeze(1).broadcast_to([ROWS - PRODUCT_ROWS, HALF, T])
                                   ).then_inc(k_const, 16)
                pool.wait_ge(k_const, 64)

            @block.vector
            def _(dve):
                dve.memset(V[:], 0.0).then_inc(zeroed, 1)
                dve.memset(Q[:].bitcast(F32), 0.0).then_inc(zeroed, 1)
                dve.wait_ge(zeroed, 2)
                for r in range(4):
                    col = 16 * (1 - r // 2) + r % 2
                    for p in range(2):
                        dve.memset(V[:, p, :, r, :, col], 1.0).then_inc(zeroed, 1)
                dve.wait_ge(zeroed, 10)
                if layer == 1:
                    dve.wait_ge(w_loaded, 16 * 23)
                    dve.tensor_scalar(bqs[:], bq[:], SCALE, None, ALU.mult).then_inc(scaled, 1)
                    dve.wait_ge(scaled, 1)

        with nc.Block() as block:
            @block.sync
            def _(sp):
                def load_xnT(b, p):
                    sp.dma_start(xnT[:, p, :], n.xnT_dram[bass.ds(b, 1)].rearrange("o d t -> d (o t)")
                                 ).then_inc(xnT_loaded[p], 16)

                def write_parts(k, g, p, last):
                    q_done = nQK.at(k, g) + (2 if k == 0 and p == 1 else 0) + 2
                    copies = [(s, r, part) for s, which in enumerate((Q_PARTS, K_PARTS)) for r, part in enumerate(which)]
                    if not last:
                        sp.wait_ge(parts_ready, q_done)
                    for s, r, part in (copies[-1:] if last else copies[:-1]):
                        sp.dma_start(scr[p, s, :, r * HD:(r + 1) * HD, :], parts[:, s, part, :]).then_inc(parts_written, 16)
                    if not last:
                        return
                    sp.wait_ge(parts_written, 16 * 12 * (q_done // 2) if isinstance(q_done, int)
                               else 16 * 12 * (nQK.at(k, 0) // 2 + 1) + 16 * 12 * (nQK.round // 2) * g)

                def load_stack(hb, p):
                    t = hb % 2
                    for s, dst in enumerate((Q, K)):
                        sp.dma_start(dst[0:PRODUCT_ROWS, hb % 4],
                                     scr[p, s, HALF * t:HALF * (t + 1)].rearrange("h r t -> r h t")
                                     ).then_inc(stack_loaded[hb % 4], 16)

                load_xnT(0, 0)

                def step(k, g):
                    if k == 0:
                        load_xnT(1, 1)
                    for pos, (what, arg) in enumerate(scripts[k]):
                        if what == "PJ" and arg == "K":
                            write_parts(k, g, 0, False)
                            write_parts(k, g, 0, True)
                            load_stack(0, 0)
                            load_stack(1, 0)
                        elif what == "PN" and arg == "K":
                            write_parts(k, g, (k // 2 + 1) % 2, False)
                        elif what == "MT":
                            sp.wait_ge(max_ready, nMT.at(k, g) + 1)
                            for s in range(3):
                                sp.dma_start(Q[MAX_ROW + s:MAX_ROW + s + 1, (k - 1) % 4],
                                             mparts[:, (k - 1) % 2, s, :]).then_inc(max_loaded[(k - 1) % 4], 16)
                            if k % 2 == 0 and k // 2 + 1 < SEQS:
                                load_xnT(k // 2 + 1 + 2 * g, (k // 2 + 1) % 2)
                    if k + 2 < 2 * SEQS:
                        if k >= 2:
                            sp.wait_ge(b_ready, nB.at(k, g) + len(units_b))
                        if k % 2 == 0:
                            write_parts(k, g, (k // 2 + 1) % 2, True)
                        load_stack(k + 2, ((k + 2) // 2) % 2)
                run_steps(sp, step)

            @block.tensor
            def _(pe):
                def step(k, g):
                    t = k % 2
                    for pos, (what, arg) in enumerate(scripts[k]):
                        if what in MISC:
                            idx = misc_index(k, g, pos)
                            if not (isinstance(idx, int) and idx == 0):
                                pe.wait_ge(misc_free, idx)
                        if what in ("PJ", "PN"):
                            b = 0 if what == "PJ" else k // 2 + 1
                            if arg == projections(layer)[0]:
                                pe.wait_ge(xnT_loaded[b % 2], 16 * (b // 2 + 1 + g))
                            x = xnT[:, b % 2, :]
                            if arg == "C":
                                m = pe.matmul(psM[0:LATENT, :], wdkv[:], x, start=True, stop=True)
                            elif arg == "Q":
                                m = pe.matmul(psM[:], wq[:], x, start=True, stop=True)
                            elif layer == 0:
                                m = pe.matmul(psM[:], wk[0:LATENT, :], ckv[:, b % 2, :], start=True, stop=True)
                            else:
                                m = pe.matmul(psM[:], wk[:], x, start=True, stop=True)
                            m.then_inc(misc_ready, 1)
                        elif what == "V":
                            p = (k // 2) % 2
                            for i in range(NT):
                                o = psM[:, i * D:(i + 1) * D]
                                if layer == 0:
                                    m = pe.matmul(o, ckv[:, p, i * P:(i + 1) * P], wv[0:LATENT, :], start=True, stop=True)
                                else:
                                    pe.matmul(o, xnT[:, p, i * P:(i + 1) * P], wv[:], start=True, stop=False)
                                    m = pe.matmul(o, n.ones[:], bv[:], start=False, stop=True)
                            m.then_inc(misc_ready, 1)
                        elif what == "MT":
                            pe.wait_ge(a_free, nA.at(k, g))
                            for i in range(NT):
                                m = pe.transpose(psM[0:HALF, i * P:(i + 1) * P], maxes[:, (k - 1) % 2, i, :], n.ident[:])
                            m.then_inc(misc_ready, 1)
                        elif what == "A":
                            i, heads = units_a[arg]
                            u = nA.at(k, g) + arg
                            par = (nA.c[k] + arg) % 2
                            if arg == 0:
                                pe.wait_ge(stack_loaded[k % 4], 32 * loads(k, g))
                            if not (isinstance(u, int) and u < 2):
                                pe.wait_ge(a_free, u - 1)
                            w = T if layer == 1 else (i + 1) * P
                            per_bank = T // w
                            for x, h in enumerate(heads):
                                o = psA[:, par, x // per_bank, (x % per_bank) * w:(x % per_bank + 1) * w]
                                pe.matmul(o, Q[0:A_ROWS, k % 4, h, i * P:(i + 1) * P], K[0:A_ROWS, k % 4, h, 0:w],
                                          start=True, stop=False)
                                m = diagonal(pe, o[:, i * P:(i + 1) * P], HALF * t + h, n.mask_q)
                            m.then_inc(a_ready, 1)
                        elif what == "B":
                            kt, heads = units_b[arg]
                            u = nB.at(k, g) + arg
                            slot = (k - 2) % 4
                            if arg == 0:
                                pe.wait_ge(max_loaded[slot], 48 * loads(k - 2, g))
                            if nB.c[k] + arg >= 2:
                                pe.wait_ge(p_ready, u - 1)
                            q0 = 0 if layer == 1 else kt * P
                            w = T - q0
                            for x, h in enumerate(heads):
                                o = psB[:, arg % 2, x * w:(x + 1) * w]
                                pe.matmul(o, K[:, slot, h, kt * P:(kt + 1) * P], Q[:, slot, h, q0:T],
                                          start=True, stop=False)
                                m = diagonal(pe, o[:, kt * P - q0:(kt + 1) * P - q0], HALF * t + h, n.mask_k)
                            m.then_inc(b_ready, 1)
                        elif what == "PV":
                            kt, heads = units_b[arg]
                            u = nB.at(k, g) + arg
                            if arg == 0 and nO.c[k]:
                                pe.wait_ge(o_copied, nO.at(k, g))
                            pe.wait_ge(p_ready, u + 1)
                            q0 = 0 if layer == 1 else kt * P
                            w = T - q0
                            b = (k - 2) // 2
                            for x, h in enumerate(heads):
                                r, j = (HALF * t + h) // 4, h % 4
                                m = pe.matmul(psO[32 * j:32 * (j + 1), q0:T], V[:, b % 2, kt, r, j, :],
                                              Pt[:, (nB.c[k] + arg) % 4, x * w:(x + 1) * w],
                                              start=(kt == 0 and h < 4), stop=(kt == NT - 1 and h >= 4),
                                              skip_group_check=True)
                            m.then_inc(pv_done, 1)
                        elif what == "OT":
                            pe.wait_ge(o_copied, nO.at(k, g) + arg)
                            for i in range(NT):
                                m = pe.transpose(psM[:, i * P:(i + 1) * P], Ob[:, arg, i * P:(i + 1) * P], n.ident[:])
                            m.then_inc(misc_ready, 1)
                        elif what == "ONT":
                            for i in range(NT):
                                m = pe.transpose(psM[:, i * P:(i + 1) * P], ON[:, i, :], n.ident[:])
                            m.then_inc(misc_ready, 1)
                        elif what == "WO":
                            for i in range(NT):
                                o = psM[:, i * D:(i + 1) * D]
                                m = pe.matmul(o, ONT[:, i * P:(i + 1) * P], wo[:], start=True, stop=(layer == 0))
                                if layer == 1:
                                    m = pe.matmul(o, n.ones[:], bo[:], start=False, stop=True)
                            m.then_inc(misc_ready, 1)

                def diagonal(pe, o, head, mask):
                    if layer == 0:
                        return pe.matmul(o, n.identb[:], mask[:], start=False, stop=True)
                    for s in range(3):
                        m = pe.matmul(o, n.alpha_eye[:, head, s, :], n.dist[:], start=False, stop=(s == 2))
                    return m
                run_steps(pe, step)

            @block.scalar
            def _(act):
                def project(k, g, pos, b, arg):
                    idx = misc_index(k, g, pos)
                    act.wait_ge(misc_ready, idx + 1)
                    if arg == "C":
                        act.activation(ckv[:, b % 2, :], psM[0:LATENT, :], ACT.Copy).then_inc(misc_free, 1)
                        return
                    s = "QK".index(arg)
                    done = nQK.at(k, g) + (2 if what_is(k, pos) == "PN" and k == 0 else 0)
                    if not (isinstance(done, int) and done == 0):
                        act.wait_ge(parts_ready, done)
                        writes = 96 * done if isinstance(done, int) else 96 * nQK.at(k, 0) + 96 * nQK.round * g
                        act.wait_ge(parts_written, writes)
                    bias, scale = (0.0, 1.0) if layer == 0 else (bk[:], 1.0)
                    if arg == "Q":
                        bias, scale = (0.0, SCALE) if layer == 0 else (bqs[:], SCALE)
                    f = ACT.Copy if layer == 0 else ACT.Identity
                    act.activation(qkf[:, s, :], psM[:], f, bias=bias, scale=scale)
                    act.activation(parts[:, s, 0, :], psM[:], f, bias=bias, scale=scale).then_inc(misc_free, 1)

                def what_is(k, pos):
                    return scripts[k][pos][0]

                def step(k, g):
                    for pos, (what, arg) in enumerate(scripts[k]):
                        if what in ("PJ", "PN"):
                            project(k, g, pos, 0 if what == "PJ" else k // 2 + 1, arg)
                        elif what == "MT":
                            act.wait_ge(misc_ready, misc_index(k, g, pos) + 1)
                            if k > 1:
                                act.wait_ge(max_ready, nMT.at(k, g))
                            if k > 2:
                                hb = k - 3
                                act.wait_ge(max_loaded[hb % 4], 48 * loads(hb, g))
                            act.activation(nm[:], psM[0:HALF, :], ACT.Copy)
                            act.activation(mparts[:, (k - 1) % 2, 0, :], psM[0:HALF, :], ACT.Copy).then_inc(misc_free, 1)
                        elif what == "B":
                            kt, heads = units_b[arg]
                            u = nB.at(k, g) + arg
                            w = len(heads) * (T if layer == 1 else T - kt * P)
                            act.wait_ge(b_ready, u + 1)
                            if nB.c[k] + arg >= 4:
                                act.wait_ge(pv_done, u - 3)
                            act.activation(Pt[:, (nB.c[k] + arg) % 4, 0:w], psB[:, arg % 2, 0:w], ACT.Exp).then_inc(p_ready, 1)
                        elif what == "OC":
                            act.wait_ge(pv_done, nB.at(k, g) + len(units_b))
                            act.activation(Ob[:, k % 2, :], psO[:], ACT.Copy).then_inc(o_copied, 1)
                        elif what == "ONT":
                            act.wait_ge(misc_ready, misc_index(k, g, pos) + 1)
                            act.activation(ONT[:], psM[:], ACT.Copy).then_inc(misc_free, 1)
                run_steps(act, step)

            @block.vector
            def _(dve):
                def step(k, g):
                    for pos, (what, arg) in enumerate(scripts[k]):
                        if what == "A":
                            i, heads = units_a[arg]
                            par = (nA.c[k] + arg) % 2
                            w = T if layer == 1 else (i + 1) * P
                            if arg == 0 and k >= 2:
                                dve.wait_ge(misc_ready, nM.at(k, g))
                            dve.wait_ge(a_ready, nA.at(k, g) + arg + 1)
                            src = psA[:, par, :, 0:w] if T // w == 1 else \
                                psA[:, par].rearrange("p b (x w) -> p (b x) w", w=w)
                            dve.tensor_reduce(maxes[:, k % 2, i, heads[0]:heads[0] + len(heads)], src, AX,
                                              ALU.max, negate=True).then_inc(a_free, 1)
                        elif what == "V":
                            dve.wait_ge(misc_ready, misc_index(k, g, pos) + 1)
                            if k > 2:
                                dve.wait_ge(pv_done, nB.at(k, g))
                            src = psM[:].rearrange("p (i r j d) -> p i r j d", i=NT, r=4, j=4)
                            for r in range(4):
                                m = dve.tensor_copy(V[:, (k // 2) % 2, :, r, :, HD * r:HD * (r + 1)], src[:, :, r])
                            m.then_inc(misc_free, 1)
                        elif what == "OT":
                            dve.wait_ge(misc_ready, misc_index(k, g, pos) + 1)
                            o = psM[:].rearrange("p (m w) -> p m w", w=32)
                            den, val = 16 * (1 - arg), 16 * arg
                            dve.reciprocal(rden[:, arg], o[:, :, den:den + 2]).then_inc(den_ready, 1)
                            dve.wait_ge(den_ready, nOT.at(k, g) + arg + 1)
                            dve.tensor_tensor(
                                ON[:].rearrange("p i (j w) -> p (i j) w", w=32)[:, :, val:val + 16].rearrange(
                                    "p m (r d) -> p m r d", d=HD),
                                o[:, :, val:val + 16].rearrange("p m (r d) -> p m r d", d=HD),
                                rden[:, arg].unsqueeze(3).broadcast_to([P, 4 * NT, 2, HD]), ALU.mult
                            ).then_inc(misc_free, 1)
                        elif what == "WO":
                            dve.wait_ge(misc_ready, misc_index(k, g, pos) + 1)
                            b = (k - 3) // 2
                            xv = n.x[:, bass.ds((b + 2 * g) * NT, NT), :]
                            dve.tensor_tensor(xv, psM[:].rearrange("p (i d) -> p i d", i=NT), xv, ALU.add).then_inc(misc_free, 1)
                run_steps(dve, step)
                dve.wait_ge(misc_free, nM.at(STEPS, 0))

            @block.gpsimd
            def _(pool):
                nS = Counts([3 * sum((x[0] in ("PJ", "PN") and x[1] != "C") or x[0] == "MT" for x in scripts[k])
                             for k in range(STEPS)])

                def split(f, parts3, base, done):
                    pool.tensor_tensor(f, f, parts3[0], ALU.subtract).then_inc(split_step, 1)
                    pool.wait_ge(split_step, base + 1)
                    pool.tensor_tensor(parts3[1], f, n.zeros[0:f.shape[0], :], ALU.add).then_inc(split_step, 1)
                    pool.wait_ge(split_step, base + 2)
                    pool.tensor_tensor(parts3[2], f, parts3[1], ALU.subtract).then_inc(done, 1)

                def step(k, g):
                    count = 0
                    for pos, (what, arg) in enumerate(scripts[k]):
                        base = (nS.at(k, g) // 3 * 2 if isinstance(nS.at(k, g), int)
                                else nS.at(k, 0) // 3 * 2 + nS.round // 3 * 2 * g)
                        if what in ("PJ", "PN") and arg != "C":
                            pool.wait_ge(misc_free, misc_index(k, g, pos) + 1)
                            s = "QK".index(arg)
                            split(qkf[:, s, :], [parts[:, s, x, :] for x in range(3)], base + 2 * count, parts_ready)
                            count += 1
                        elif what == "MT":
                            pool.wait_ge(misc_free, misc_index(k, g, pos) + 1)
                            split(nm[:], [mparts[:, (k - 1) % 2, x, :] for x in range(3)], base + 2 * count, max_ready)
                            count += 1
                run_steps(pool, step)



def route(n, c):
    nc, I = n.nc, n.ins
    n.xs_dram = n.dram("xs", (SLOT_TILES * P, D))
    n.ys_dram = n.dram("ys", (SLOT_TILES * P, D))
    n.slots = n.sb("slots", [P, 2, TILES], I32, ctx=c)
    n.weights = n.sb("weights", [P, 2, TILES], ctx=c)
    n.tile_expert = n.sb("tile_expert", [1, SLOT_TILES], I32, ctx=c)
    E = EXPERTS
    with ExitStack() as k:
        xn = n.sb("r_xn", [P, 2, T], ctx=k)
        xn_all = n.sb("r_xn_all", [P, TILES, D], ctx=k)
        xnT = n.sb("r_xnT", [P, 2, T], ctx=k)
        wg = n.sb("r_wg", [P, E], ctx=k)
        expert = n.sb("r_expert", [P, E], ctx=k)
        slot_tile = n.sb("r_slot_tile", [1, SLOT_TILES], ctx=k)
        zero = n.sb("r_zero", [P, 12, D], ctx=k)
        logits = n.sb("r_logits", [P, TILES, E], ctx=k)
        pr = n.sb("r_p", [P, TILES, E], ctx=k)
        eq = n.sb("r_eq", [P, TILES, E], ctx=k)
        hot = [n.sb(f"r_hot{j}", [P, TILES, E], ctx=k) for j in range(2)]
        count = n.sb("r_count", [P, TILES, E], BF16, ctx=k)
        before = n.sb("r_before", [P, TILES, E], ctx=k)
        sums = [n.sb(f"r_sums{j}", [P, TILES, E], ctx=k) for j in range(2)]
        small = n.sb("r_small", [P, 12, TILES], ctx=k)
        ends = [n.sb(f"r_ends{j}", [P, E], ctx=k) for j in range(2)]
        cmp = n.sb("r_cmp", [1, SLOT_TILES, E], ctx=k)
        te = n.sb("r_te", [1, SLOT_TILES], ctx=k)
        psT = n.pb("r_psT", [P, 2, T], ctx=k)
        psL = n.pb("r_psL", [P, 2, T], ctx=k)
        psC = n.pb("r_psC", [P, 2, T], ctx=k)
        psS = n.pb("r_psS", [P, 2, T], ctx=k)
        normed, turned, kept, scored, read, copied, chain, acted, counted, loaded, zeroed, zero_written, placed = (
            n.sem("r_" + x, k) for x in ("normed", "turned", "kept", "scored", "logits_read", "xn_copied", "chain", "acted",
                                         "counted", "loaded", "zeroed", "zero_written", "placed"))
        stored = [n.sem(f"r_stored{p}", k) for p in range(2)]
        shifted, gap_ready, count_ready, combined, ct_turned, ct_kept, b2_ready, b2_added, slots_ready = (
            n.sem("r_" + x, k) for x in ("shifted", "gap_ready", "count_ready", "combined", "ct_turned", "ct_kept",
                                         "b2_ready", "b2_added", "slots_ready"))
        b2 = n.sb("r_b2", [E, D], ctx=k)
        ct = n.sb("r_ct", [E, 2, T], ctx=k)
        with nc.Block() as block:
            @block.sync
            def _(sp):
                sp.dma_start(wg[:], I["L1_ffn_Wg"]).then_inc(loaded, 16)
                sp.dma_start(b2[:], I["L1_ffn_b2"]).then_inc(loaded, 16)
                sp.dma_start(expert[:], I["c_expert"]).then_inc(loaded, 16)
                sp.dma_start(slot_tile[:], I["c_slot_tile"]).then_inc(loaded, 16)
                sp.wait_ge(zeroed, 1)
                for s in range(SLOT_TILES // 12):
                    sp.dma_start(n.xs_dram[s * 12 * P:(s + 1) * 12 * P].rearrange("(t p) d -> p t d", p=P),
                                 zero[:]).then_inc(zero_written, 16)
                with sp.Fori(0, SEQS // 2) as g:
                    for p in range(2):
                        b = 2 * g + p
                        sp.wait_ge(kept, b + 1)
                        sp.dma_start(n.xnT_dram[bass.ds(b, 1)].rearrange("o d t -> d (o t)"),
                                     xnT[:, p, :]).then_inc(stored[p], 16)
                for p in range(2):
                    sp.wait_ge(stored[p], 16 * SEQS // 2)

            @block.tensor
            def _(pe):
                pe.wait_ge(loaded, 64)
                def turn(b, p, first):
                    pe.wait_ge(normed, NT * b + NT)
                    if not first:
                        pe.wait_ge(kept, b - 1)
                    for i in range(NT):
                        m = pe.transpose(psT[:, p, i * P:(i + 1) * P], xn[:, p, i * D:(i + 1) * D], n.ident[:])
                    m.then_inc(turned, 1)

                def score(b, p, first):
                    pe.wait_ge(kept, b + 1)
                    if not first:
                        pe.wait_ge(read, b - 1)
                    for i in range(NT):
                        m = pe.matmul(psL[:, p, i * E:(i + 1) * E], xnT[:, p, i * P:(i + 1) * P], wg[:],
                                      start=True, stop=True)
                    m.then_inc(scored, 1)
                for b in range(2):
                    turn(b, b, True)
                    score(b, b, True)
                with pe.Fori(0, SEQS // 2 - 1) as g:
                    for p in range(2):
                        turn(2 * g + 2 + p, p, False)
                        score(2 * g + 2 + p, p, False)
                pe.wait_ge(count_ready, 1)
                cv = count[:].rearrange("p t e -> p (t e)")
                for s in range(2):
                    pe.matmul(psC[:, s, :], n.upper[:], cv[:, s * T:(s + 1) * T], start=True, stop=True)
                    m = pe.matmul(psS[:, s, :], n.ones_b[:], cv[:, s * T:(s + 1) * T], start=True, stop=True)
                m.then_inc(counted, 1)
                pe.wait_ge(combined, 1)
                for b in range(SEQS):
                    if b >= 2:
                        pe.wait_ge(ct_kept, b - 1)
                    for i in range(NT):
                        m = pe.transpose(psT[0:E, b % 2, i * P:(i + 1) * P], eq[:, b * NT + i, :], n.ident[:])
                    m.then_inc(ct_turned, 1)
                    pe.wait_ge(ct_kept, b + 1)
                    if b >= 2:
                        pe.wait_ge(b2_added, b - 1)
                    for i in range(NT):
                        m = pe.matmul(psL[:, b % 2, i * D:(i + 1) * D], ct[:, b % 2, i * P:(i + 1) * P], b2[:],
                                      start=True, stop=True)
                    m.then_inc(b2_ready, 1)

            @block.scalar
            def _(act):
                def body(b, p, first):
                    act.wait_ge(turned, b + 1)
                    if not first:
                        act.wait_ge(stored[p], 8 * (b - p))
                        act.wait_ge(scored, b - 1)
                    act.activation(xnT[:, p, :], psT[:, p, :], ACT.Copy).then_inc(kept, 1)
                    act.activation(xn_all[:, bass.ds(b * NT, NT), :],
                                   xn[:, p, :].rearrange("p (i d) -> p i d", d=D), ACT.Copy).then_inc(copied, 1)
                    act.wait_ge(scored, b + 1)
                    act.activation(logits[:, bass.ds(b * NT, NT), :],
                                   psL[:, p, 0:NT * E].rearrange("p (i e) -> p i e", e=E), ACT.Copy).then_inc(read, 1)
                for b in range(2):
                    body(b, b, True)
                with act.Fori(0, SEQS // 2 - 1) as g:
                    for p in range(2):
                        body(2 * g + 2 + p, p, False)
                act.wait_ge(shifted, 1)
                act.activation(pr[:], pr[:], ACT.Exp).then_inc(acted, 1)
                act.wait_ge(gap_ready, 1)
                act.activation(small[:, 6, :], small[:, 6, :], ACT.Exp).then_inc(acted, 1)
                for b in range(SEQS):
                    act.wait_ge(ct_turned, b + 1)
                    if b >= 2:
                        act.wait_ge(b2_ready, b - 1)
                    act.activation(ct[:, b % 2, :], psT[0:E, b % 2, :], ACT.Copy).then_inc(ct_kept, 1)

            @block.vector
            def _(dve):
                dve.memset(zero[:], 0.0).then_inc(zeroed, 1)
                def norm(b, p, first):
                    if not first:
                        dve.wait_ge(copied, b - 1)
                        dve.wait_ge(turned, b - 1)
                    for i in range(NT):
                        tile = b * NT + i
                        dve.tensor_scalar(xn[:, p, i * D:(i + 1) * D],
                                          n.x[:, bass.ds(tile, 1), :].rearrange("p o k -> p (o k)"),
                                          n.mean[:, bass.ds(tile, 1)], n.rstd[:, bass.ds(tile, 1)],
                                          ALU.subtract, ALU.mult).then_inc(normed, 1)
                for b in range(2):
                    norm(b, b, True)
                with dve.Fori(0, SEQS // 2 - 1) as g:
                    for p in range(2):
                        norm(2 * g + 2 + p, p, False)

                step = 0

                def then(ins, sem=None):
                    nonlocal step
                    if sem is not None:
                        ins.then_inc(sem, 1)
                        dve.wait_ge(sem, 1)
                        return
                    ins.then_inc(chain, 1)
                    step += 1
                    dve.wait_ge(chain, step)
                mx, sm, rs, top1, top2, id1, dif, id2, w0 = (small[:, j, :] for j in range(9))
                ev = expert[:].unsqueeze(1).broadcast_to([P, TILES, E])
                dve.wait_ge(read, SEQS)
                dve.wait_ge(loaded, 64)
                then(dve.tensor_reduce(mx, logits[:], AX, ALU.max))
                then(dve.tensor_tensor(pr[:], logits[:], bc(mx, E), ALU.subtract), shifted)
                dve.wait_ge(acted, 1)
                then(dve.tensor_reduce(sm, pr[:], AX, ALU.add))
                then(dve.reciprocal(rs, sm))
                then(dve.tensor_tensor(pr[:], pr[:], bc(rs, E), ALU.mult))
                for top, ix, j in ((top1, id1, 0), (top2, id2, 1)):
                    then(dve.tensor_reduce(top, pr[:], AX, ALU.max))
                    then(dve.tensor_tensor(eq[:], pr[:], bc(top, E), ALU.is_equal))
                    then(dve.tensor_tensor(eq[:], eq[:], ev, ALU.mult))
                    then(dve.tensor_reduce(ix, eq[:], AX, ALU.min))
                    then(dve.tensor_tensor(hot[j][:], ev, bc(ix, E), ALU.is_equal))
                    if j == 0:
                        then(dve.scalar_tensor_tensor(pr[:], hot[0][:], -4.0, pr[:], ALU.mult, ALU.add))
                then(dve.tensor_tensor(dif, top2, top1, ALU.subtract), gap_ready)
                then(dve.tensor_tensor(count[:], hot[0][:], hot[1][:], ALU.add), count_ready)
                dve.wait_ge(acted, 2)
                then(dve.tensor_scalar(w0, dif, 1.0, None, ALU.add))
                then(dve.reciprocal(n.weights[:, 0, :], w0))
                then(dve.tensor_tensor(n.weights[:, 1, :], dif, n.weights[:, 0, :], ALU.mult))
                then(dve.tensor_tensor(pr[:], hot[0][:], bc(n.weights[:, 0, :], E), ALU.mult))
                then(dve.tensor_tensor(eq[:], hot[1][:], bc(n.weights[:, 1, :], E), ALU.mult))
                then(dve.tensor_tensor(eq[:], eq[:], pr[:], ALU.add), combined)
                dve.wait_ge(counted, 1)
                flat = [x[:].rearrange("p t e -> p (t e)") for x in sums]
                then(dve.tensor_copy(flat[0], psS[:].rearrange("p a t -> p (a t)")))
                src = 0
                for d in (1, 2, 4, 8, 16):
                    dst = 1 - src
                    dve.tensor_copy(sums[dst][:, 0:d, :], sums[src][:, 0:d, :])
                    then(dve.tensor_tensor(sums[dst][:, d:, :], sums[src][:, d:, :], sums[src][:, :TILES - d, :], ALU.add))
                    src = dst
                bf = before[:].rearrange("p t e -> p (t e)")
                then(dve.tensor_tensor(bf, psC[:].rearrange("p a t -> p (a t)"), flat[src], ALU.add))
                then(dve.tensor_tensor(bf, bf, psS[:].rearrange("p a t -> p (a t)"), ALU.subtract))
                nt, first = n.sb("r_nt", [P, E], ctx=k), n.sb("r_first", [P, E], ctx=k)
                then(dve.tensor_scalar(nt[:], sums[src][:, TILES - 1, :], 1.0 / P, (P - 1) / P - 0.498, ALU.mult, ALU.add))
                then(dve.tensor_scalar(nt[:], nt[:], ROUND, None, ALU.add))
                then(dve.tensor_scalar(nt[:], nt[:], -ROUND, None, ALU.add))
                then(dve.tensor_copy(ends[0][:], nt[:]))
                src = 0
                for d in (1, 2, 4, 8, 16):
                    dst = 1 - src
                    dve.tensor_copy(ends[dst][:, 0:d], ends[src][:, 0:d])
                    then(dve.tensor_tensor(ends[dst][:, d:], ends[src][:, d:], ends[src][:, :E - d], ALU.add))
                    src = dst
                then(dve.tensor_tensor(first[:], ends[src][:], nt[:], ALU.subtract))
                then(dve.tensor_scalar(first[:], first[:], float(P), None, ALU.mult))
                then(dve.tensor_tensor(before[:], before[:], first[:].unsqueeze(1).broadcast_to([P, TILES, E]), ALU.add))
                for j in range(2):
                    then(dve.tensor_tensor(pr[:], before[:], hot[j][:], ALU.mult))
                    then(dve.tensor_reduce(small[:, 9 + j, :], pr[:], AX, ALU.add))
                    m = dve.tensor_copy(n.slots[:, j, :], small[:, 9 + j, :])
                    if j == 1:
                        m.then_inc(slots_ready, 1)
                then(dve.tensor_tensor(cmp[:], ends[src][0:1, :].unsqueeze(1).broadcast_to([1, SLOT_TILES, E]),
                                       bc(slot_tile[:], E), ALU.is_le))
                then(dve.tensor_reduce(te[:], cmp[:], AX, ALU.add))
                then(dve.tensor_scalar(n.tile_expert[:], te[:], float(E - 1), None, ALU.min))
                for b in range(SEQS):
                    dve.wait_ge(b2_ready, b + 1)
                    xv = n.x[:, b * NT:(b + 1) * NT, :]
                    dve.tensor_tensor(xv, psL[:, b % 2, :].rearrange("p (i d) -> p i d", d=D), xv, ALU.add).then_inc(b2_added, 1)
                dve.wait_ge(b2_added, SEQS)

            @block.gpsimd
            def _(pool):
                pool.wait_ge(slots_ready, 1)
                pool.wait_ge(zero_written, 16 * (SLOT_TILES // 12))
                pool.wait_ge(copied, SEQS)
                for t in range(TILES):
                    for j in range(2):
                        pool.indirect_dma_start(
                            out=n.xs_dram, out_offset=bass.IndirectOffsetOnAxis(ap=n.slots[:, j, t:t + 1], axis=0),
                            in_=xn_all[:, t, :], in_offset=None).then_inc(placed, 16)
                pool.wait_ge(placed, 16 * 2 * TILES)



GROUP = 4


def experts(n):
    nc, I = n.nc, n.ins
    G = SLOT_TILES // GROUP
    with ExitStack() as c:
        xs = n.sb("m_xs", [P, 2, GROUP, D], ctx=c)
        w = n.sb("m_w", [P, 2, GROUP, 2 * D + 1], ctx=c)
        xT = n.sb("m_xT", [P, 2, GROUP * P], ctx=c)
        hT = n.sb("m_hT", [P, 2, GROUP * P], ctx=c)
        ys = n.sb("m_ys", [P, 2, GROUP, D], ctx=c)
        psX = n.pb("m_psX", [P, 2, 512], ctx=c)
        psH = n.pb("m_psH", [P, 2, 512], ctx=c)
        psY = n.pb("m_psY", [P, 2, 512], ctx=c)
        xs_loaded = [n.sem(f"m_xs_loaded{p}", c) for p in range(2)]
        w_loaded = [n.sem(f"m_w_loaded{p}", c) for p in range(2)]
        ys_stored = [n.sem(f"m_ys_stored{p}", c) for p in range(2)]
        turned, x_kept, h_ready, h_kept, y_ready, y_kept = (
            n.sem("m_" + x, c) for x in ("turned", "x_kept", "h_ready", "h_kept", "y_ready", "y_kept"))

        def groups(engine, stages):
            def iteration(t, shift):
                for off, f in stages:
                    if 0 <= t + off < G:
                        f(t + off + 2 * shift, (t + off) % 2, t + off < 2 and isinstance(shift, int))
            for t in (-1, 0, 1, 2):
                iteration(t, 0)
            with engine.Fori(0, 9) as g:
                for t in (3, 4):
                    iteration(t, g)
            for t in range(21, G + 2):
                iteration(t, 0)

        with nc.Block() as block:
            @block.sync
            def _(sp):
                def load(g, p, early):
                    if not early:
                        sp.wait_ge(turned, g - 1)
                    sp.dma_start(xs[:, p], n.xs_dram.rearrange("(g t p) d -> g p t d", t=GROUP, p=P)[
                        bass.ds(g, 1)].rearrange("o p t d -> p (o t) d")).then_inc(xs_loaded[p], 16)
                    if not early:
                        sp.wait_ge(y_ready, g - 1)
                    for t in range(GROUP):
                        e = sp.value_load(n.tile_expert[0:1, bass.ds(g * GROUP + t, 1)], min_val=0, max_val=EXPERTS - 1)
                        sp.dma_start(w[:, p, t, :], I["expert_w"][bass.ds(e, 1)].rearrange("o d h -> d (o h)")
                                     ).then_inc(w_loaded[p], 16)

                def store(g, p, early):
                    sp.wait_ge(y_kept, g + 1)
                    sp.dma_start(n.ys_dram.rearrange("(g t p) d -> g p t d", t=GROUP, p=P)[
                        bass.ds(g, 1)].rearrange("o p t d -> p (o t) d"), ys[:, p]).then_inc(ys_stored[p], 16)
                groups(sp, [(1, load), (-2, store)])
                for p in range(2):
                    sp.wait_ge(ys_stored[p], 16 * G // 2)

            @block.tensor
            def _(pe):
                def turn(g, p, early):
                    pe.wait_ge(xs_loaded[p], 8 * (g - p) + 16)
                    if not early:
                        pe.wait_ge(x_kept, g - 1)
                    for t in range(GROUP):
                        m = pe.transpose(psX[:, p, t * P:(t + 1) * P], xs[:, p, t, :], n.ident[:])
                    m.then_inc(turned, 1)

                def up(g, p, early):
                    pe.wait_ge(w_loaded[p], GROUP * (8 * (g - p) + 16))
                    pe.wait_ge(x_kept, g + 1)
                    if not early:
                        pe.wait_ge(h_kept, GROUP * (g - 1))
                    for t in range(GROUP):
                        m = pe.matmul(psH[:, p, t * P:(t + 1) * P], w[:, p, t, 0:D], xT[:, p, t * P:(t + 1) * P],
                                      start=True, stop=True)
                    m.then_inc(h_ready, 1)

                def down(g, p, early):
                    pe.wait_ge(h_kept, GROUP * (g + 1))
                    if not early:
                        pe.wait_ge(y_kept, g - 1)
                    for t in range(GROUP):
                        m = pe.matmul(psY[:, p, t * D:(t + 1) * D], hT[:, p, t * P:(t + 1) * P], w[:, p, t, D:2 * D],
                                      start=True, stop=True)
                    m.then_inc(y_ready, 1)
                groups(pe, [(1, turn), (0, up), (-1, down)])

            @block.scalar
            def _(act):
                def gelu(g, p, early):
                    act.wait_ge(h_ready, g + 1)
                    if not early:
                        act.wait_ge(y_ready, g - 1)
                    for t in range(GROUP):
                        s = slice(t * P, (t + 1) * P)
                        act.activation(hT[:, p, s], psH[:, p, s], ACT.Gelu, bias=w[:, p, t, 2 * D:2 * D + 1]).then_inc(h_kept, 1)
                groups(act, [(0, gelu)])

            @block.vector
            def _(dve):
                def keep_x(g, p, early):
                    dve.wait_ge(turned, g + 1)
                    if not early:
                        dve.wait_ge(h_ready, g - 1)
                    dve.tensor_copy(xT[:, p], psX[:, p]).then_inc(x_kept, 1)

                def keep_y(g, p, early):
                    dve.wait_ge(y_ready, g + 1)
                    if not early:
                        dve.wait_ge(ys_stored[p], 8 * (g - p))
                    dve.tensor_copy(ys[:, p].rearrange("p t d -> p (t d)"), psY[:, p]).then_inc(y_kept, 1)
                groups(dve, [(1, keep_x), (-1, keep_y)])


def combine(n):
    nc = n.nc
    with ExitStack() as c:
        got = n.sb("c_got", [P, 4, 2, D], ctx=c)
        gathered = [n.sem(f"c_gathered{s}", c) for s in range(4)]
        added, stored = n.sem("c_added", c), n.sem("c_stored", c)
        with nc.Block() as block:
            @block.gpsimd
            def _(pool):
                for t in range(TILES):
                    if t >= 4:
                        pool.wait_ge(added, 2 * (t - 3))
                    for j in range(2):
                        pool.indirect_dma_start(
                            out=got[:, t % 4, j, :], out_offset=None, in_=n.ys_dram,
                            in_offset=bass.IndirectOffsetOnAxis(ap=n.slots[:, j, t:t + 1], axis=0)
                        ).then_inc(gathered[t % 4], 16)

            @block.vector
            def _(dve):
                for t in range(TILES):
                    dve.wait_ge(gathered[t % 4], 32 * (t // 4 + 1))
                    for j in range(2):
                        if j:
                            dve.wait_ge(added, 2 * t + 1)
                        dve.scalar_tensor_tensor(n.x[:, t, :], got[:, t % 4, j, :], n.weights[:, j, t:t + 1], n.x[:, t, :],
                                                 ALU.mult, ALU.add).then_inc(added, 1)

            @block.sync
            def _(sp):
                out_v = n.out.rearrange("b (i p) d -> p (b i) d", p=P)
                for b in range(SEQS):
                    sp.wait_ge(added, 2 * NT * (b + 1))
                    sp.dma_start(out_v[:, b * NT:(b + 1) * NT, :], n.x[:, b * NT:(b + 1) * NT, :]).then_inc(stored, 16)
                sp.wait_ge(stored, 16 * SEQS)


def program(nc, ins, out):
    n = Net(nc, ins, out)
    with n.ctx:
        n.mean = n.sb("mean", [P, TILES])
        n.rstd = n.sb("rstd", [P, TILES])
        load_constants(n)
        layernorm_stats(n, 0)
        ffn(n)
        attention(n, 0)
        layernorm_stats(n, 1)
        with ExitStack() as c:
            route(n, c)
            attention(n, 1)
            experts(n)
            combine(n)


INPUTS = ['L0_attn_x', 'L0_attn_W_DKV', 'L0_attn_W_UK', 'L0_attn_W_UV', 'L0_attn_W_UQ', 'L0_attn_W_O',
          'L0_ffn_w_gate', 'L0_ffn_w_up', 'L0_ffn_w_down', 'L1_attn_qkv_w', 'L1_attn_qkv_b',
          'L1_attn_out_w', 'L1_attn_out_b', 'L1_attn_decay_alpha', 'L1_ffn_Wg', 'L1_ffn_W1', 'L1_ffn_b1',
          'L1_ffn_W2', 'L1_ffn_b2']


def const_arrays():
    i = np.arange(P)
    rows = np.zeros((ROWS - PRODUCT_ROWS, T), np.float32)
    t = np.arange(T)
    for kt in range(NT):
        here = (t // P == kt)
        for part in range(3):
            rows[(kt * 2 + 0) * 3 + part] = here * (t % P)
            rows[(kt * 2 + 1) * 3 + part] = here
    rows[BIAS_ROWS:] = 1.0
    pat = np.zeros((HEADS, NT, 2, T), np.float32)
    for kt in range(NT):
        sign = np.sign(t // P - kt)
        pat[:, kt, 0] = sign
        pat[:, kt, 1] = -sign * (t - P * kt)
    up = (i[:, None] < i[None, :])
    return {
        "c_ident": np.eye(P, dtype=np.float32),
        "c_mask_q": np.where(up, NEG, 0).astype(np.float32),
        "c_mask_k": np.where(up.T, NEG, 0).astype(np.float32),
        "c_dist": -np.abs(i[:, None] - i[None, :]).astype(np.float32),
        "c_upper": up.astype(np.float32),
        "c_krows": rows,
        "c_qpat": pat.reshape(P, T),
        "c_expert": np.broadcast_to(np.arange(EXPERTS, dtype=np.float32) - 2 * EXPERTS, (P, EXPERTS)).copy(),
        "c_slot_tile": np.arange(SLOT_TILES, dtype=np.float32).reshape(1, SLOT_TILES),
    }


def kernel(**inputs):
    import concourse.bacc as bacc
    from concourse.bass_utils import run_bass_kernel_spmd
    a = {k: np.ascontiguousarray(inputs[k]) for k in INPUTS}
    a["qkv_wT"] = np.ascontiguousarray(a["L1_attn_qkv_w"].T)
    a["out_wT"] = np.ascontiguousarray(a["L1_attn_out_w"].T)
    a["alpha_rows"] = np.repeat(a["L1_attn_decay_alpha"], NT * 2).reshape(P, 1)
    a["alpha_all"] = np.tile(a["L1_attn_decay_alpha"], (P, 1))
    a["expert_w"] = np.concatenate([a["L1_ffn_W1"], a["L1_ffn_W2"], a["L1_ffn_b1"][:, :, None]], axis=2)
    a.update(const_arrays())
    for k in ("L1_attn_qkv_w", "L1_attn_out_w", "L1_attn_decay_alpha", "L1_ffn_W1", "L1_ffn_W2", "L1_ffn_b1"):
        del a[k]
    nc = bacc.Bacc("TRN2", target_bir_lowering=False, num_devices=1)
    ins = {k: nc.dram_tensor("in_" + k, v.shape, mybir.dt.from_np(v.dtype), kind="ExternalInput").ap()
           for k, v in a.items()}
    out = nc.dram_tensor("out", (SEQS, T, D), F32, kind="ExternalOutput").ap()
    program(nc, ins, out)
    r = run_bass_kernel_spmd(nc, [{"in_" + k: v for k, v in a.items()}], core_ids=[0])
    return r.results[0]["out"]
```

```python
from contextlib import ExitStack

import numpy as np

import concourse.bass as bass
from concourse import mybir

F32 = mybir.dt.float32
BF16 = mybir.dt.bfloat16
I32 = mybir.dt.int32
ALU = mybir.AluOpType
ACT = mybir.ActivationFunctionType
AX = mybir.AxisListType.X

P = 128
D = 128
SEQS = 8
T = 512
NT = T // P
TILES = SEQS * NT
HEADS = 16
HD = D // HEADS
LATENT = 32
FF = 352
FFC = 3
BLK = 16
EXPERTS = 32
SLOT_TILES = 96
HALF = HEADS // 2
GROUP = 4
EXPERT_STEPS = range(2, 14)
assert SLOT_TILES == 2 * GROUP * len(EXPERT_STEPS)
LOAD_TILES = SLOT_TILES + 2 * GROUP
EPS = 1e-5
SCALE = float(1.0 / np.sqrt(np.float32(HD)))

Q_PARTS = (0, 0, 0, 1, 1, 2)
K_PARTS = (0, 1, 2, 0, 1, 0)
PRODUCT_ROWS = len(Q_PARTS) * HD
BIAS_ROWS = NT * 2 * 3
MAX_ROW = PRODUCT_ROWS + BIAS_ROWS
ROWS = MAX_ROW + 3
A_ROWS = MAX_ROW
NEG = -1e30
ROUND = 1.5 * 2.0 ** 23


def score_units(layer):
    a, b = [], []
    if layer == 1:
        a = [(i, [2 * p, 2 * p + 1]) for p in range(HALF // 2) for i in range(NT)]
        b = [(kt, [h]) for kt in range(NT) for h in range(HALF)]
    else:
        for i in (3, 2, 1, 0):
            n = {3: 2, 2: 2, 1: 4, 0: 8}[i]
            a += [(i, list(range(h, h + n))) for h in range(0, HALF, n)]
        for kt in range(NT):
            n = {0: 1, 1: 1, 2: 2, 3: 4}[kt]
            b += [(kt, list(range(h, h + n))) for h in range(0, HALF, n)]
    return a, b


STEPS = 2 * SEQS + 2
PV_LAG = 2


def projections(layer):
    return ["C", "Q", "K"] if layer == 0 else ["Q", "K"]


def script(layer, k):
    a, b = score_units(layer)
    out = []
    if k == 0:
        out += [("PJ", p) for p in projections(layer)]
    units_a = list(range(len(a))) if k < 2 * SEQS else []
    units_b = list(range(len(b))) if k >= 2 else []
    side = []
    if 1 <= k <= 2 * SEQS:
        side.append(("MT", 0))
    if k % 2 == 0 and k < 2 * SEQS:
        side.append(("V", 0))
    if k % 2 == 0 and k // 2 + 1 < SEQS:
        side += [("PN", p) for p in projections(layer)]
    if k % 2 == 1 and k >= 3:
        side.append(("OT", 0))
    if layer == 1 and k in EXPERT_STEPS:
        side += [(what, e) for what in ("EX", "EH", "EY") for e in range(2)]
    held = 4 if (k % 2 == 1 and k >= 3 and units_a) else 0
    body_a = units_a[:len(units_a) - held]
    late_a = units_a[len(units_a) - held:]
    done_b = 0
    n_slots = max(len(body_a), 1)
    for s in range(n_slots):
        if s < len(body_a):
            out.append(("A", body_a[s]))
        if side and side[0] == ("EH", 1):
            out.append(side.pop(0))
        upto = len(units_b) * (s + 1) // n_slots
        while done_b < upto:
            out.append(("B", done_b))
            if done_b >= PV_LAG:
                out.append(("PV", done_b - PV_LAG))
            done_b += 1
        if side and (s % 2 == 1 or (len(side) > (n_slots - s) // 2 and s)):
            out.append(side.pop(0))
    out += side
    if units_b:
        out += [("PV", m) for m in range(len(units_b) - PV_LAG, len(units_b))]
        out.append(("OC", 0))
    if k % 2 == 1 and k >= 3:
        tail = [("OT", 1), ("ONT", 0), ("WO", 0)]
        if late_a:
            out.append(("A", late_a[0]))
            for n, item in enumerate(tail):
                out += [item, ("A", late_a[n + 1])]
        else:
            out += tail
    return out


class Counts:

    def __init__(self, per_step):
        self.c = [0]
        for n in per_step:
            self.c.append(self.c[-1] + n)
        self.round = self.c[6] - self.c[2]
        assert self.c[10] - self.c[6] == self.round == self.c[14] - self.c[10]

    def at(self, k, g):
        return self.c[k] + g * self.round if 2 <= k <= 6 else self.c[k]


def run_steps(engine, step):
    step(0, 0)
    step(1, 0)
    with engine.Fori(0, 3) as g:
        for r in range(4):
            step(2 + r, g)
    for k in range(14, STEPS):
        step(k, 0)


MISC = ("PJ", "PN", "V", "MT", "OT", "ONT", "WO", "EX", "EH", "EY")


class Net:
    def __init__(self, nc, ins, out):
        self.nc, self.ins, self.out = nc, ins, out
        self.ctx = ExitStack()

    def sb(self, name, shape, dt=F32, ctx=None):
        return (ctx or self.ctx).enter_context(self.nc.sbuf_tensor(name, shape, dt))

    def pb(self, name, shape, dt=F32, ctx=None):
        return (ctx or self.ctx).enter_context(self.nc.psum_tensor(name, shape, dt))

    def sem(self, name, ctx=None):
        return (ctx or self.ctx).enter_context(self.nc.semaphore(name))

    def dram(self, name, shape, dt=F32):
        return self.nc.dram_tensor(name, shape, dt, kind="Internal").ap()



def load_constants(n):
    nc, I = n.nc, n.ins
    n.x = n.sb("x", [P, TILES, D])
    n.ident = n.sb("ident", [P, P])
    n.identb = n.sb("identb", [P, P], BF16)
    n.mask_q = n.sb("mask_q", [P, P], BF16)
    n.mask_k = n.sb("mask_k", [P, P], BF16)
    n.dist = n.sb("dist", [P, P], BF16)
    n.ones = n.sb("ones", [1, P])
    n.zeros = n.sb("zeros", [P, T])
    n.ones_b = n.sb("ones_b", [P, P], BF16)
    n.upper = n.sb("upper", [P, P], BF16)
    n.xnT_dram = n.dram("xnT_dram", (SEQS, D, T))
    n.const_sem = n.sem("constants_loaded")
    n.x_sem = n.sem("x_loaded")
    n.memset_sem = n.sem("ones_set")
    n.Q = n.sb("Q", [ROWS, 4, HALF, T], BF16)
    n.K = n.sb("K", [ROWS, 4, HALF, T], BF16)
    n.k_const = n.sem("key_rows_loaded")
    n.q_zeroed = n.sem("query_rows_zeroed")
    x_v = I["L0_attn_x"].rearrange("b (i p) d -> p (b i) d", p=P)
    n.qrows = n.dram("qrows", (HEADS, BIAS_ROWS, T), BF16)
    A = HEADS + 1
    n.alpha_parts = n.sb("alpha_parts", [P, 3, A])
    with ExitStack() as k, nc.Block() as block:
        raw = n.sb("al_raw", [P, A], ctx=k)
        neg = n.sb("al_neg", [P, A], ctx=k)
        e = n.sb("al_e", [P, A], ctx=k)
        al = n.sb("alpha", [P, A], ctx=k)
        ap = n.sb("al_parts_b", [P, 3, A], BF16, ctx=k)
        pat = n.sb("al_pat", [P, T], ctx=k)
        qb = n.sb("al_rows", [P, 3, T], BF16, ctx=k)
        loaded, stored = n.sem("al_loaded", k), n.sem("al_stored", k)
        v, a = n.sem("al_vec", k), n.sem("al_act", k)

        @block.scalar
        def _(act):
            act.wait_ge(v, 2)
            act.activation(e[:], neg[:], ACT.Exp).then_inc(a, 1)
            act.wait_ge(v, 3)
            act.activation(e[:], e[:], ACT.Ln).then_inc(a, 1)

        @block.sync
        def _(sp):
            sp.dma_start(raw[:, 0:1], I["alpha_rows"]).then_inc(loaded, 16)
            sp.dma_start(raw[:, 1:A], I["alpha_all"]).then_inc(loaded, 16)
            sp.dma_start(pat[:], I["c_qpat"]).then_inc(loaded, 16)
            sp.dma_start(n.ident[:], I["c_ident"]).then_inc(n.x_sem, 16)
            for s in range(4):
                sp.dma_start(n.x[:, 8 * s:8 * s + 8, :], x_v[:, 8 * s:8 * s + 8, :]).then_inc(n.x_sem, 16)
            sp.wait_ge(v, 14)
            sp.dma_start(n.qrows.rearrange("h (r s) t -> (h r) s t", s=3), qb[:]).then_inc(stored, 16)
            sp.wait_ge(n.const_sem, 16 * 5)
            sp.wait_ge(stored, 16)
            sp.wait_ge(n.x_sem, 16 * 5)

        @block.gpsimd
        def _(pool):
            for dst, src in ((n.identb, "c_ident"), (n.mask_q, "c_mask_q"), (n.mask_k, "c_mask_k"),
                             (n.dist, "c_dist"), (n.upper, "c_upper")):
                pool.dma_start(dst[:], I[src]).then_inc(n.const_sem, 16)

        @block.vector
        def _(dve):
            dve.memset(n.ones[:], 1.0)
            dve.memset(n.zeros[:], 0.0)
            dve.memset(n.ones_b[:], 1.0).then_inc(n.memset_sem, 1)
            dve.wait_ge(n.memset_sem, 1)
            step = 0

            def then(ins):
                nonlocal step
                ins.then_inc(v, 1)
                step += 1
                dve.wait_ge(v, step)
            dve.wait_ge(loaded, 48)
            then(dve.tensor_scalar(neg[:], raw[:], -1.0, None, ALU.mult))
            then(dve.tensor_tensor(neg[:], neg[:], raw[:], ALU.min))
            dve.wait_ge(a, 1)
            then(dve.tensor_scalar(e[:], e[:], 1.0, None, ALU.add))
            dve.wait_ge(a, 2)
            then(dve.scalar_tensor_tensor(al[:], raw[:], 0.0, e[:], ALU.max, ALU.add))
            then(dve.tensor_copy(ap[:, 0, :], al[:]))
            then(dve.tensor_tensor(e[:], al[:], ap[:, 0, :], ALU.subtract))
            then(dve.tensor_copy(ap[:, 1, :], e[:]))
            then(dve.tensor_tensor(ap[:, 2, :], e[:], ap[:, 1, :], ALU.subtract))
            then(dve.tensor_scalar(pat[:], pat[:], al[:, 0:1], None, ALU.mult))
            then(dve.tensor_copy(qb[:, 0, :], pat[:]))
            then(dve.tensor_tensor(pat[:], pat[:], qb[:, 0, :], ALU.subtract))
            then(dve.tensor_copy(qb[:, 1, :], pat[:]))
            then(dve.tensor_tensor(qb[:, 2, :], pat[:], qb[:, 1, :], ALU.subtract))
            then(dve.tensor_copy(n.alpha_parts[:], ap[:]))



MIDS_LOW = (0.25, 0.75, 1.25, 1.75)


def quant_scales(dve, ab, am, sc, rs, half, sem, base):
    dve.tensor_reduce(am, ab, AX, ALU.max).then_inc(sem, 1)
    dve.wait_ge(sem, base + 1)
    dve.tensor_scalar(sc, am, 1.0 / 6.0, 1e-12, ALU.mult, ALU.max).then_inc(sem, 1)
    dve.wait_ge(sem, base + 2)
    dve.tensor_scalar(half, sc, 0.5, None, ALU.mult).then_inc(sem, 1)
    dve.reciprocal(rs, sc).then_inc(sem, 1)


def quant_grid(dve, a, u, t, sem, base):
    dve.tensor_scalar(u, a, 5.0, 2.0, ALU.is_gt, ALU.mult).then_inc(sem, 1)
    dve.tensor_scalar(t, a, MIDS_LOW[0], None, ALU.is_gt).then_inc(sem, 1)
    dve.wait_ge(sem, base + 1)
    dve.scalar_tensor_tensor(u, a, 3.5, u, ALU.is_gt, ALU.add).then_inc(sem, 1)
    dve.wait_ge(sem, base + 2)
    dve.scalar_tensor_tensor(t, a, MIDS_LOW[1], t, ALU.is_gt, ALU.add).then_inc(sem, 1)
    dve.wait_ge(sem, base + 3)
    dve.scalar_tensor_tensor(u, a, 2.5, u, ALU.is_gt, ALU.add).then_inc(sem, 1)
    dve.wait_ge(sem, base + 4)
    dve.scalar_tensor_tensor(t, a, MIDS_LOW[2], t, ALU.is_gt, ALU.add).then_inc(sem, 1)
    dve.wait_ge(sem, base + 6)
    dve.scalar_tensor_tensor(t, a, MIDS_LOW[3], t, ALU.is_gt, ALU.add).then_inc(sem, 1)
    dve.wait_ge(sem, base + 7)
    dve.scalar_tensor_tensor(t, u, 2.0, t, ALU.mult, ALU.add).then_inc(sem, 1)


SCALES_INC, GRID_INC = 4, 8


def bc(ap, n):
    return ap.unsqueeze(2).broadcast_to([ap.shape[0], ap.shape[1], n])


def blocks(ap):
    return ap.rearrange("p (m k) -> p m k", k=BLK)



def layernorm_stats(n, layer):
    nc = n.nc
    with ExitStack() as c:
        st = n.sb(f"bn{layer}", [P, TILES, 6], ctx=c)
        dm = n.sb(f"bn_dm{layer}", [P, TILES], ctx=c)
        m2 = n.sb(f"bn_m2{layer}", [P, TILES], ctx=c)
        sd = n.sb(f"bn_sd{layer}", [P, TILES], ctx=c)
        s = n.sem(f"stats_step{layer}", c)
        s_sd = n.sem(f"sd_ready{layer}", c)
        with nc.Block() as block:
            @block.vector
            def _(dve):
                with dve.Fori(0, SEQS) as b:
                    for i in range(NT):
                        dve.bn_stats(st[:, bass.ds(b * NT + i, 1), :].rearrange("p o k -> p (o k)"),
                                     n.x[:, bass.ds(b * NT + i, 1), :].rearrange("p o k -> p (o k)")).then_inc(s, 1)
                v = TILES
                dve.wait_ge(s, v)
                dve.tensor_tensor(n.mean[:], st[:, :, 1], st[:, :, 4], ALU.add).then_inc(s, 1)
                dve.tensor_tensor(dm[:], st[:, :, 1], st[:, :, 4], ALU.subtract).then_inc(s, 1)
                dve.tensor_tensor(m2[:], st[:, :, 2], st[:, :, 5], ALU.add).then_inc(s, 1)
                dve.wait_ge(s, v + 3)
                dve.tensor_scalar(n.mean[:], n.mean[:], 0.5, None, ALU.mult).then_inc(s, 1)
                dve.tensor_tensor(dm[:], dm[:], dm[:], ALU.mult).then_inc(s, 1)
                dve.wait_ge(s, v + 5)
                dve.scalar_tensor_tensor(m2[:], dm[:], float(P // 4), m2[:], ALU.mult, ALU.add).then_inc(s, 1)
                dve.wait_ge(s, v + 6)
                dve.tensor_scalar(m2[:], m2[:], 1.0 / D, EPS, ALU.mult, ALU.add).then_inc(s, 1)
                dve.wait_ge(s_sd, 1)
                dve.reciprocal(n.rstd[:], sd[:]).then_inc(s, 1)
                dve.wait_ge(s, v + 8)

            @block.scalar
            def _(act):
                act.wait_ge(s, TILES + 7)
                act.activation(sd[:], m2[:], ACT.Sqrt).then_inc(s_sd, 1)



def prepare_ffn_weights(n, c):
    nc, I = n.nc, n.ins
    W = 2 * FFC * D + FF
    n.wguT = n.sb("wguT", [P, 2 * FF], ctx=c)
    n.wdT = n.sb("wdT", [P, FFC, D], ctx=c)
    with ExitStack() as k:
        w = n.sb("w_raw", [P, W], ctx=k)
        ab = n.sb("w_abs", [P, W], ctx=k)
        sg = n.sb("w_sign", [P, W], ctx=k)
        t = n.sb("w_t", [P, W], ctx=k)
        u = n.sb("w_u", [P, W], ctx=k)
        am, sc, rs, hs = (n.sb(f"w_{x}", [P, W // BLK], ctx=k) for x in ("am", "sc", "rs", "hs"))
        ps = n.pb("w_ps", [P, 3, 512], ctx=k)
        zeroed, loaded, signed, scaled, normed, gridded, quantised, turned, kept = (
            n.sem(f"w_{x}", k) for x in ("zeroed", "loaded", "signed", "scaled", "normed", "gridded",
                                         "quantised", "turned", "kept"))
        rem = FF - 2 * P
        with nc.Block() as block:
            @block.sync
            def _(sp):
                sp.wait_ge(zeroed, 1)
                for s, name in enumerate(("L0_ffn_w_gate", "L0_ffn_w_up")):
                    for q in range(FFC):
                        r = P if q < 2 else rem
                        sp.dma_start(w[0:r, (s * FFC + q) * D:(s * FFC + q + 1) * D],
                                     I[name][q * P:q * P + r, :]).then_inc(loaded, 16)
                sp.dma_start(w[:, 2 * FFC * D:], I["L0_ffn_w_down"]).then_inc(loaded, 16)

            @block.scalar
            def _(act):
                act.wait_ge(loaded, 16 * 7)
                act.activation(ab[:], w[:], ACT.Abs).then_inc(signed, 1)
                act.activation(sg[:], w[:], ACT.Sign).then_inc(signed, 1)
                act.wait_ge(turned, 2)
                act.activation(n.wguT[:, 0:FF], ps[:, 0, 0:FF], ACT.Copy).then_inc(kept, 1)
                act.activation(n.wguT[:, FF:2 * FF], ps[:, 1, 0:FF], ACT.Copy).then_inc(kept, 1)
                act.wait_ge(turned, 3)
                act.activation(n.wdT[:, 0:2, :], ps[:, 2, 0:2 * D].rearrange("p (c d) -> p c d", c=2),
                               ACT.Copy).then_inc(kept, 1)
                act.activation(n.wdT[0:rem, 2, :], ps[0:rem, 2, 2 * D:3 * D], ACT.Copy).then_inc(kept, 1)
                act.wait_ge(kept, 4)

            @block.vector
            def _(dve):
                dve.memset(w[:], 0.0).then_inc(zeroed, 1)
                dve.memset(n.Q[:].bitcast(F32), 0.0).then_inc(n.q_zeroed, 1)
                dve.wait_ge(n.q_zeroed, 1)
                dve.wait_ge(signed, 1)
                quant_scales(dve, blocks(ab[:]), am[:], sc[:], rs[:], hs[:], scaled, 0)
                dve.wait_ge(normed, 1)
                quant_grid(dve, ab[:], u[:], t[:], gridded, 0)

            @block.gpsimd
            def _(pool):
                pool.wait_ge(scaled, SCALES_INC)
                pool.tensor_tensor(blocks(ab[:]), blocks(ab[:]), bc(rs[:], BLK), ALU.mult).then_inc(normed, 1)
                pool.wait_ge(gridded, GRID_INC)
                pool.tensor_tensor(blocks(t[:]), blocks(t[:]), bc(hs[:], BLK), ALU.mult).then_inc(quantised, 1)
                pool.wait_ge(quantised, 1)
                pool.wait_ge(signed, 2)
                pool.tensor_tensor(t[:], t[:], sg[:], ALU.mult).then_inc(quantised, 1)

            @block.tensor
            def _(pe):
                pe.wait_ge(quantised, 2)
                for s in range(2):
                    for q in range(FFC):
                        r = P if q < 2 else rem
                        m = pe.transpose(ps[:, s, q * P:q * P + r],
                                         t[0:r, (s * FFC + q) * D:(s * FFC + q + 1) * D], n.ident[0:r, 0:r])
                    m.then_inc(turned, 1)
                for q in range(FFC):
                    r = P if q < 2 else rem
                    m = pe.transpose(ps[0:r, 2, q * D:(q + 1) * D],
                                     t[:, 2 * FFC * D + q * P:2 * FFC * D + q * P + r], n.ident[:])
                m.then_inc(turned, 1)


def run_ffn_steps(engine, stages):
    def iteration(it, shift):
        for off, f in stages:
            b = it + off
            if 0 <= b < SEQS:
                f(b + 2 * shift, b % 2)
    for it in (-2, -1, 0, 1):
        iteration(it, 0)
    with engine.Fori(0, 2) as g:
        for it in (2, 3):
            iteration(it, g)
    for it in range(6, SEQS + 1):
        iteration(it, 0)


def ffn(n):
    nc = n.nc
    HW = NT * FF
    with ExitStack() as c:
        prepare_ffn_weights(n, c)
        buf = {}
        for w, size in (("x", T), ("h", HW)):
            for name in ("v", "ab", "sg", "t"):
                buf[w + name] = n.sb(f"f_{w}{name}", [P, 2, size], ctx=c)
            buf[w + "u"] = n.sb(f"f_{w}u", [P, size], ctx=c)
            for name in ("am", "sc"):
                buf[w + name] = n.sb(f"f_{w}{name}", [P, size // BLK], ctx=c)
            for name in ("rs", "hs"):
                buf[w + name] = n.sb(f"f_{w}{name}", [P, 2, size // BLK], ctx=c)
        xqT = n.sb("f_xqT", [P, T], ctx=c)
        xnT = n.sb("f_xnT", [P, 2, T], ctx=c)
        silu = n.sb("f_silu", [P, 2, FF], ctx=c)
        hqT = n.sb("f_hqT", [P, FFC, T], ctx=c)
        ps_n = n.pb("f_ps_n", [P, T], ctx=c)
        ps_x = n.pb("f_ps_x", [P, T], ctx=c)
        ps_g = n.pb("f_ps_g", [P, 2, 512], ctx=c)
        ps_u = n.pb("f_ps_u", [P, 2, 512], ctx=c)
        ps_h = n.pb("f_ps_h", [P, T], ctx=c)
        ps_d = n.pb("f_ps_d", [P, NT, D], ctx=c)
        S = {x: n.sem("ffn_" + x, c) for x in (
            "normed", "xn_turned", "xn_kept", "x_split", "x_scaled", "x_div", "x_grid", "x_q",
            "xq_turned", "xq_kept", "gate_up", "silu", "h_ready", "h_split", "h_scaled", "h_div",
            "h_grid", "h_q", "hq_turned", "hq_kept", "down", "added")}
        stored = [n.sem(f"ffn_xnT_stored{p}", c) for p in range(2)]
        rem = FF - 2 * P

        with nc.Block() as block:
            @block.sync
            def _(sp):
                weights = load_attention_weights(n, sp, 0)
                with sp.Fori(0, SEQS // 2) as g:
                    for p in range(2):
                        b = 2 * g + p
                        sp.wait_ge(S["xn_kept"], b + 1)
                        sp.dma_start(n.xnT_dram[bass.ds(b, 1)].rearrange("o d t -> d (o t)"),
                                     xnT[:, p, :]).then_inc(stored[p], 16)
                for p in range(2):
                    sp.wait_ge(stored[p], 16 * SEQS // 2)
                sp.wait_ge(n.aw_loaded[0], weights)

            @block.vector
            def _(dve):
                def s1(b, p):
                    if not (isinstance(b, int) and b < 2):
                        dve.wait_ge(S["x_split"], 2 * (b - 1))
                        dve.wait_ge(S["xn_turned"], b - 1)
                    for i in range(NT):
                        tile = b * NT + i
                        dve.tensor_scalar(buf["xv"][:, p, i * D:(i + 1) * D],
                                          n.x[:, bass.ds(tile, 1), :].rearrange("p o k -> p (o k)"),
                                          n.mean[:, bass.ds(tile, 1)], n.rstd[:, bass.ds(tile, 1)],
                                          ALU.subtract, ALU.mult).then_inc(S["normed"], 1)
                    dve.wait_ge(S["x_split"], 2 * b + 1)
                    if not (isinstance(b, int) and b < 2):
                        dve.wait_ge(S["x_q"], 2 * (b - 1))
                    quant_scales(dve, blocks(buf["xab"][:, p]), buf["xam"][:], buf["xsc"][:],
                                 buf["xrs"][:, p], buf["xhs"][:, p], S["x_scaled"], SCALES_INC * b)

                def s3(b, p):
                    dve.wait_ge(S["x_div"], b + 1)
                    if not (isinstance(b, int) and b < 2):
                        dve.wait_ge(S["xq_turned"], b - 1)
                    quant_grid(dve, buf["xab"][:, p], buf["xu"][:], buf["xt"][:, p], S["x_grid"], GRID_INC * b)

                def s5(b, p):
                    if not (isinstance(b, int) and b < 2):
                        dve.wait_ge(S["h_split"], 2 * (b - 1))
                    for i in range(NT):
                        dve.wait_ge(S["silu"], NT * b + i + 1)
                        dve.tensor_tensor(buf["hv"][:, p, i * FF:(i + 1) * FF], ps_u[:, i % 2, 0:FF],
                                          silu[:, i % 2, :], ALU.mult).then_inc(S["h_ready"], 1)

                def s6(b, p):
                    dve.wait_ge(S["h_split"], 2 * b + 1)
                    if not (isinstance(b, int) and b < 2):
                        dve.wait_ge(S["h_q"], 2 * (b - 1))
                    quant_scales(dve, blocks(buf["hab"][:, p]), buf["ham"][:], buf["hsc"][:],
                                 buf["hrs"][:, p], buf["hhs"][:, p], S["h_scaled"], SCALES_INC * b)

                def s8(b, p):
                    dve.wait_ge(S["h_div"], b + 1)
                    if not (isinstance(b, int) and b < 2):
                        dve.wait_ge(S["hq_turned"], FFC * (b - 1))
                    quant_grid(dve, buf["hab"][:, p], buf["hu"][:], buf["ht"][:, p], S["h_grid"], GRID_INC * b)

                def s10(b, p):
                    dve.wait_ge(S["down"], b + 1)
                    xv = n.x[:, bass.ds(b * NT, NT), :]
                    dve.tensor_tensor(xv, ps_d[:], xv, ALU.add).then_inc(S["added"], 1)

                run_ffn_steps(dve, [(1, s3), (0, s6), (2, s1), (0, s8), (1, s5), (-1, s10)])
                dve.wait_ge(S["added"], SEQS)

            @block.scalar
            def _(act):
                def a1(b, p):
                    act.wait_ge(S["normed"], NT * b + NT)
                    if not (isinstance(b, int) and b < 2):
                        act.wait_ge(S["x_grid"], GRID_INC * (b - 1))
                        act.wait_ge(S["x_q"], 2 * (b - 1))
                    act.activation(buf["xab"][:, p], buf["xv"][:, p], ACT.Abs).then_inc(S["x_split"], 1)
                    act.activation(buf["xsg"][:, p], buf["xv"][:, p], ACT.Sign).then_inc(S["x_split"], 1)
                    act.wait_ge(S["xn_turned"], b + 1)
                    if not (isinstance(b, int) and b < 2):
                        act.wait_ge(stored[p], 8 * (b - p))
                    act.activation(xnT[:, p, :], ps_n[:], ACT.Copy).then_inc(S["xn_kept"], 1)

                def a5(b, p):
                    act.wait_ge(S["xq_turned"], b + 1)
                    if not (isinstance(b, int) and b < 1):
                        act.wait_ge(S["gate_up"], NT * b)
                    act.activation(xqT[:], ps_x[:], ACT.Copy).then_inc(S["xq_kept"], 1)
                    for i in range(NT):
                        act.wait_ge(S["gate_up"], NT * b + i + 1)
                        if i >= 2:
                            act.wait_ge(S["h_ready"], NT * b + i - 1)
                        elif not (isinstance(b, int) and b < 1):
                            act.wait_ge(S["h_ready"], NT * b + i - 1)
                        act.activation(silu[:, i % 2, :], ps_g[:, i % 2, 0:FF], ACT.Silu).then_inc(S["silu"], 1)

                def a6(b, p):
                    act.wait_ge(S["h_ready"], NT * b + NT)
                    if not (isinstance(b, int) and b < 2):
                        act.wait_ge(S["h_grid"], GRID_INC * (b - 1))
                        act.wait_ge(S["h_q"], 2 * (b - 1))
                    act.activation(buf["hab"][:, p], buf["hv"][:, p], ACT.Abs).then_inc(S["h_split"], 1)
                    act.activation(buf["hsg"][:, p], buf["hv"][:, p], ACT.Sign).then_inc(S["h_split"], 1)

                def a10(b, p):
                    for q in range(FFC):
                        act.wait_ge(S["hq_turned"], FFC * b + q + 1)
                        if not (isinstance(b, int) and b < 1):
                            act.wait_ge(S["down"], b)
                        r = P if q < 2 else rem
                        act.activation(hqT[0:r, q, :], ps_h[0:r, :], ACT.Copy).then_inc(S["hq_kept"], 1)

                run_ffn_steps(act, [(0, a6), (2, a1), (1, a5), (-1, a10)])

            @block.gpsimd
            def _(pool):
                for s in range(4):
                    pool.dma_start(n.K[PRODUCT_ROWS:ROWS, s],
                                   n.ins["c_krows"].unsqueeze(1).broadcast_to([ROWS - PRODUCT_ROWS, HALF, T])
                                   ).then_inc(n.k_const, 16)

                def divide(w, b, p):
                    pool.wait_ge(S[w + "_scaled"], SCALES_INC * (b + 1))
                    v = blocks(buf[w + "ab"][:, p])
                    pool.tensor_tensor(v, v, bc(buf[w + "rs"][:, p], BLK), ALU.mult).then_inc(S[w + "_div"], 1)

                def scale(w, b, p):
                    pool.wait_ge(S[w + "_grid"], GRID_INC * (b + 1))
                    v = blocks(buf[w + "t"][:, p])
                    pool.tensor_tensor(v, v, bc(buf[w + "hs"][:, p], BLK), ALU.mult).then_inc(S[w + "_q"], 1)
                    pool.wait_ge(S[w + "_q"], 2 * b + 1)
                    pool.wait_ge(S[w + "_split"], 2 * b + 2)
                    pool.tensor_tensor(buf[w + "t"][:, p], buf[w + "t"][:, p], buf[w + "sg"][:, p],
                                       ALU.mult).then_inc(S[w + "_q"], 1)

                run_ffn_steps(pool, [(1, lambda b, p: scale("x", b, p)), (0, lambda b, p: divide("h", b, p)),
                                     (2, lambda b, p: divide("x", b, p)), (0, lambda b, p: scale("h", b, p))])
                pool.wait_ge(n.k_const, 64)

            @block.tensor
            def _(pe):
                def p1(b, p):
                    pe.wait_ge(S["normed"], NT * b + NT)
                    if not (isinstance(b, int) and b < 1):
                        pe.wait_ge(S["xn_kept"], b)
                    for i in range(NT):
                        m = pe.transpose(ps_n[:, i * P:(i + 1) * P], buf["xv"][:, p, i * D:(i + 1) * D], n.ident[:])
                    m.then_inc(S["xn_turned"], 1)

                def p5(b, p):
                    pe.wait_ge(S["x_q"], 2 * b + 2)
                    if not (isinstance(b, int) and b < 1):
                        pe.wait_ge(S["xq_kept"], b)
                    for i in range(NT):
                        m = pe.transpose(ps_x[:, i * P:(i + 1) * P], buf["xt"][:, p, i * D:(i + 1) * D], n.ident[:])
                    m.then_inc(S["xq_turned"], 1)
                    pe.wait_ge(S["xq_kept"], b + 1)
                    for i in range(NT):
                        if i >= 2 or not (isinstance(b, int) and b < 1):
                            pe.wait_ge(S["h_ready"], NT * b + i - 1)
                        pe.matmul(ps_g[:, i % 2, 0:FF], xqT[:, i * P:(i + 1) * P], n.wguT[:, 0:FF], start=True, stop=True)
                        pe.matmul(ps_u[:, i % 2, 0:FF], xqT[:, i * P:(i + 1) * P], n.wguT[:, FF:2 * FF],
                                  start=True, stop=True).then_inc(S["gate_up"], 1)

                def p10(b, p):
                    pe.wait_ge(S["h_q"], 2 * b + 2)
                    for q in range(FFC):
                        if q or not (isinstance(b, int) and b < 1):
                            pe.wait_ge(S["hq_kept"], FFC * b + q)
                        r = P if q < 2 else rem
                        for i in range(NT):
                            m = pe.transpose(ps_h[0:r, i * P:(i + 1) * P],
                                             buf["ht"][:, p, i * FF + q * P:i * FF + q * P + r], n.ident[:])
                        m.then_inc(S["hq_turned"], 1)
                    pe.wait_ge(S["hq_kept"], FFC * (b + 1))
                    if not (isinstance(b, int) and b < 1):
                        pe.wait_ge(S["added"], b)
                    for i in range(NT):
                        for q in range(FFC):
                            r = P if q < 2 else rem
                            m = pe.matmul(ps_d[:, i, :], hqT[0:r, q, i * P:(i + 1) * P], n.wdT[0:r, q, :],
                                          start=(q == 0), stop=(q == FFC - 1))
                    m.then_inc(S["down"], 1)

                run_ffn_steps(pe, [(2, p1), (1, p5), (-1, p10)])



def allocate_attention_weights(n):
    rows = {"q": P, "k": P, "v": P, "o": P, "bv": 1, "bo": 1, "dkv": P, "bq": P, "bqs": P, "bk": P}
    cols = {"dkv": LATENT, "bq": 1, "bqs": 1, "bk": 1}
    n.aw = {x: n.sb("aw_" + x, [r, cols.get(x, D)]) for x, r in rows.items()}
    n.aw_loaded = [n.sem(f"attention_weights_loaded{x}") for x in range(2)]


def load_attention_weights(n, sp, layer):
    I, a = n.ins, n.aw
    if layer == 0:
        loads = [(a["q"][:], I["L0_attn_W_UQ"]), (a["dkv"][:], I["L0_attn_W_DKV"]),
                 (a["k"][0:LATENT, :], I["L0_attn_W_UK"]), (a["v"][0:LATENT, :], I["L0_attn_W_UV"])]
        wo_src = I["L0_attn_W_O"]
    else:
        qkv, b = I["qkv_wT"], I["L1_attn_qkv_b"]
        loads = [(a["q"][:], qkv[:, 0:D]), (a["k"][:], qkv[:, D:2 * D]), (a["v"][:], qkv[:, 2 * D:3 * D]),
                 (a["bq"][:], b[0:D].unsqueeze(1)), (a["bk"][:], b[D:2 * D].unsqueeze(1)),
                 (a["bv"][:], b[2 * D:3 * D].unsqueeze(0)), (a["bo"][:], I["L1_attn_out_b"].unsqueeze(0))]
        wo_src = I["out_wT"]
    wo_v = wo_src.rearrange("(r j d) n -> j r d n", j=4, d=HD)
    for j in range(4):
        for r in range(4):
            loads.append((a["o"][32 * j + HD * r:32 * j + HD * (r + 1), :], wo_v[j, r]))
    for dst, src in loads:
        sp.dma_start(dst, src).then_inc(n.aw_loaded[layer], 16)
    return 16 * len(loads)


def prepare_values(n):
    n.V = n.sb("V", [P, 2, NT, 4, 4, 32])
    zeroed, ones = n.sem("V_zeroed"), n.sem("V_ones")
    with n.nc.Block() as block:
        @block.vector
        def _(dve):
            dve.memset(n.V[:], 0.0).then_inc(zeroed, 1)
            dve.wait_ge(zeroed, 1)
            for r in range(4):
                col = 16 * (1 - r // 2) + r % 2
                for p in range(2):
                    dve.memset(n.V[:, p, :, r, :, col], 1.0).then_inc(ones, 1)
            dve.wait_ge(ones, 8)


def attention(n, layer):
    nc, I = n.nc, n.ins
    with ExitStack() as c:
        L = f"a{layer}_"
        wq, wk, wv, wo, bk, bqs, bv, bo, wdkv = (n.aw[x] for x in ("q", "k", "v", "o", "bk", "bqs", "bv", "bo", "dkv"))
        ckv = n.sb(L + "ckv", [LATENT, 2, T], ctx=c) if layer == 0 else None
        Q, K, V = n.Q, n.K, n.V
        xnT = n.sb(L + "xnT", [P, 2, T], ctx=c)
        qkf = n.sb(L + "qkf", [P, 2, T], ctx=c)
        parts = n.sb(L + "parts", [P, 2, 3, T], BF16, ctx=c)
        maxes = n.sb(L + "maxes", [P, 2, NT, HALF], ctx=c)
        nm = n.sb(L + "nm", [HALF, T], ctx=c)
        mparts = n.sb(L + "mparts", [HALF, 2, 3, T], BF16, ctx=c)
        Pt = n.sb(L + "Pt", [P, 4, T], ctx=c)
        Ob = n.sb(L + "Ob", [P, 2, T], ctx=c)
        rden = n.sb(L + "rden", [P, 2, 4 * NT, 2], ctx=c)
        ON = n.sb(L + "ON", [P, NT, D], ctx=c)
        ONT = n.sb(L + "ONT", [P, T], ctx=c)
        psA = n.pb(L + "psA", [P, 2, 2, T], ctx=c)
        psB = n.pb(L + "psB", [P, 2, T], ctx=c)
        psO = n.pb(L + "psO", [P, T], ctx=c)
        psM = n.pb(L + "psM", [P, T], ctx=c)
        scr = n.dram(L + "stack", (2, 2, HEADS, PRODUCT_ROWS, T), BF16)
        a_ready = n.sem(L + "scores_for_max_ready", c)
        a_free = n.sem(L + "maxima_taken", c)
        b_ready = n.sem(L + "scores_for_exp_ready", c)
        p_ready = n.sem(L + "exp_ready", c)
        pv_done = n.sem(L + "pv_done", c)
        misc_ready = n.sem(L + "misc_ready", c)
        misc_free = n.sem(L + "misc_read", c)
        o_copied = n.sem(L + "outputs_copied", c)
        den_ready = n.sem(L + "den_ready", c)
        split_step = n.sem(L + "split_step", c)
        parts_ready = n.sem(L + "parts_ready", c)
        parts_written = n.sem(L + "parts_written", c)
        xnT_loaded = [n.sem(L + f"xnT_loaded{p}", c) for p in range(2)]
        stack_loaded = [n.sem(L + f"stack_loaded{s}", c) for s in range(4)]
        max_ready = n.sem(L + "max_parts_ready", c)
        max_loaded = [n.sem(L + f"max_loaded{s}", c) for s in range(4)]
        units_a, units_b = score_units(layer)
        scripts = [script(layer, k) for k in range(STEPS)]

        def counts(*kinds):
            return Counts([sum(x[0] in kinds for x in scripts[k]) for k in range(STEPS)])
        nA, nB, nM, nO = counts("A"), counts("B"), counts(*MISC), counts("OC")
        nMT = counts("MT")
        nQK = Counts([sum(x[0] in ("PJ", "PN") and x[1] != "C" for x in scripts[k]) for k in range(STEPS)])
        nOT = counts("OT")

        def misc_index(k, g, pos):
            return nM.at(k, g) + sum(x[0] in MISC for x in scripts[k][:pos])


        def loads(hb, g):
            return hb // 4 + 1 + g

        if layer == 1:
            xs = n.slots_flat[:, 0:2 * GROUP * D].rearrange("p (e t d) -> p e t d", e=2, t=GROUP)
            wsz = 2 * D + 1
            w0 = 2 * GROUP * D
            ew = n.slots_flat[:, w0:w0 + 2 * GROUP * wsz].rearrange("p (e t h) -> p e t h", e=2, t=GROUP)
            x0 = w0 + 2 * GROUP * wsz
            xT = n.slots_flat[:, x0:x0 + 2 * GROUP * P].rearrange("p (e t) -> p e t", e=2)
            got = n.slots_flat[:, 0:16 * 2 * D].rearrange("p (s j d) -> p s j d", j=2, d=D)
            hT = n.sb("m_hT", [P, 2, GROUP * P], ctx=c)
            ys = n.sb("m_ys", [P, 2, GROUP, D], ctx=c)
            placed = n.sem("slots_filled", c)
            xs_loaded = [n.sem(f"slots_loaded{e}", c) for e in range(2)]
            w_loaded = [n.sem(f"expert_loaded{e}", c) for e in range(2)]
            ys_stored = [n.sem(f"results_stored{e}", c) for e in range(2)]
            gathered = [n.sem(f"gathered{q}", c) for q in range(4)]
            added = n.sem("choices_added", c)
            out_stored = n.sem("out_stored", c)
            out_v = n.out.rearrange("b (i p) d -> p (b i) d", p=P)

        def expert_round(k, g):
            return k - 1 + 4 * g

        with nc.Block() as block:
            @block.sync
            def _(sp):
                def load_xnT(b, p):
                    sp.dma_start(xnT[:, p, :], n.xnT_dram[bass.ds(b, 1)].rearrange("o d t -> d (o t)")
                                 ).then_inc(xnT_loaded[p], 16)

                def write_parts(k, g, p, last):
                    q_done = nQK.at(k, g) + (2 if k == 0 and p == 1 else 0) + 2
                    copies = [(s, r, part) for s, which in enumerate((Q_PARTS, K_PARTS)) for r, part in enumerate(which)]
                    if not last:
                        sp.wait_ge(parts_ready, q_done)
                    for s, r, part in (copies[-1:] if last else copies[:-1]):
                        sp.dma_start(scr[p, s, :, r * HD:(r + 1) * HD, :], parts[:, s, part, :]).then_inc(parts_written, 16)
                    if not last:
                        return
                    sp.wait_ge(parts_written, 16 * 12 * (q_done // 2) if isinstance(q_done, int)
                               else 16 * 12 * (nQK.at(k, 0) // 2 + 1) + 16 * 12 * (nQK.round // 2) * g)

                def load_stack(hb, p):
                    t = hb % 2
                    for s, dst in enumerate((Q, K)):
                        sp.dma_start(dst[0:PRODUCT_ROWS, hb % 4],
                                     scr[p, s, HALF * t:HALF * (t + 1)].rearrange("h r t -> r h t")
                                     ).then_inc(stack_loaded[hb % 4], 16)

                load_xnT(0, 0)

                def load_weights(e, first_tile):
                    for t in range(GROUP):
                        x = sp.value_load(n.tile_expert[0:1, bass.ds(first_tile + t, 1)], min_val=0, max_val=EXPERTS - 1)
                        sp.dma_start(ew[:, e, t, :], I["expert_w"][bass.ds(x, 1)].rearrange("o d h -> d (o h)")
                                     ).then_inc(w_loaded[e], 16)

                def slot_rows(dram, group):
                    return dram.rearrange("(g t p) d -> g p t d", t=GROUP, p=P)[bass.ds(group, 1)].rearrange("o p t d -> p (o t) d")

                def store_x(b0, b1):
                    sp.dma_start(out_v[:, b0 * NT:b1 * NT, :], n.x[:, b0 * NT:b1 * NT, :]).then_inc(out_stored, 16)

                def step(k, g):
                    if k == 0:
                        load_xnT(1, 1)
                    for pos, (what, arg) in enumerate(scripts[k]):
                        if what == "PJ" and arg == "K":
                            write_parts(k, g, 0, False)
                            write_parts(k, g, 0, True)
                            load_stack(0, 0)
                            load_stack(1, 0)
                        elif what == "PN" and arg == "K":
                            write_parts(k, g, (k // 2 + 1) % 2, False)
                        elif what == "MT":
                            sp.wait_ge(max_ready, nMT.at(k, g) + 1)
                            for s in range(3):
                                sp.dma_start(Q[MAX_ROW + s:MAX_ROW + s + 1, (k - 1) % 4],
                                             mparts[:, (k - 1) % 2, s, :]).then_inc(max_loaded[(k - 1) % 4], 16)
                            if k % 2 == 0 and k // 2 + 1 < SEQS:
                                load_xnT(k // 2 + 1 + 2 * g, (k // 2 + 1) % 2)
                        elif what == "EY":
                            group = 2 * (k - 2) + arg + 8 * g
                            sp.wait_ge(misc_free, misc_index(k, g, pos) + 1)
                            sp.dma_start(slot_rows(n.ys_dram, group), ys[:, arg]).then_inc(ys_stored[arg], 16)
                            load_weights(arg, (group + 2) * GROUP)
                            sp.wait_ge(ys_stored[arg], 16 * expert_round(k, g))
                            sp.dma_start(xs[:, arg], slot_rows(n.xs_dram, group + 2)).then_inc(xs_loaded[arg], 16)
                    if k + 2 < 2 * SEQS:
                        if k >= 2:
                            sp.wait_ge(b_ready, nB.at(k, g) + len(units_b))
                        if k % 2 == 0:
                            write_parts(k, g, (k // 2 + 1) % 2, True)
                        load_stack(k + 2, ((k + 2) // 2) % 2)
                    if layer == 1 and k == 1:
                        sp.wait_ge(placed, 16 * 2 * TILES)
                        for e in range(2):
                            sp.dma_start(xs[:, e], slot_rows(n.xs_dram, e)).then_inc(xs_loaded[e], 16)
                            load_weights(e, e * GROUP)
                    if layer == 1 and k == 16:
                        sp.wait_ge(added, 2 * TILES)
                        for b in range(0, SEQS - 1):
                            store_x(b, b + 1)
                run_steps(sp, step)
                if layer == 1:
                    sp.wait_ge(misc_free, nM.at(STEPS, 0))
                    store_x(SEQS - 1, SEQS)
                    sp.wait_ge(out_stored, 16 * SEQS)

            @block.tensor
            def _(pe):
                def step(k, g):
                    t = k % 2
                    for pos, (what, arg) in enumerate(scripts[k]):
                        if what in MISC:
                            idx = misc_index(k, g, pos)
                            if not (isinstance(idx, int) and idx == 0):
                                pe.wait_ge(misc_free, idx)
                        if what in ("PJ", "PN"):
                            b = 0 if what == "PJ" else k // 2 + 1
                            if arg == projections(layer)[0]:
                                pe.wait_ge(xnT_loaded[b % 2], 16 * (b // 2 + 1 + g))
                            x = xnT[:, b % 2, :]
                            if arg == "C":
                                m = pe.matmul(psM[0:LATENT, :], wdkv[:], x, start=True, stop=True)
                            elif arg == "Q":
                                m = pe.matmul(psM[:], wq[:], x, start=True, stop=True)
                            elif layer == 0:
                                m = pe.matmul(psM[:], wk[0:LATENT, :], ckv[:, b % 2, :], start=True, stop=True)
                            else:
                                m = pe.matmul(psM[:], wk[:], x, start=True, stop=True)
                            m.then_inc(misc_ready, 1)
                        elif what == "V":
                            p = (k // 2) % 2
                            for i in range(NT):
                                o = psM[:, i * D:(i + 1) * D]
                                if layer == 0:
                                    m = pe.matmul(o, ckv[:, p, i * P:(i + 1) * P], wv[0:LATENT, :], start=True, stop=True)
                                else:
                                    pe.matmul(o, xnT[:, p, i * P:(i + 1) * P], wv[:], start=True, stop=False)
                                    m = pe.matmul(o, n.ones[:], bv[:], start=False, stop=True)
                            m.then_inc(misc_ready, 1)
                        elif what == "MT":
                            pe.wait_ge(a_free, nA.at(k, g))
                            for i in range(NT):
                                m = pe.transpose(psM[0:HALF, i * P:(i + 1) * P], maxes[:, (k - 1) % 2, i, :], n.ident[:])
                            m.then_inc(misc_ready, 1)
                        elif what == "EX":
                            pe.wait_ge(xs_loaded[arg], 16 * expert_round(k, g))
                            for i in range(GROUP):
                                m = pe.transpose(psM[:, i * P:(i + 1) * P], xs[:, arg, i, :], n.ident[:])
                            m.then_inc(misc_ready, 1)
                        elif what == "EH":
                            pe.wait_ge(w_loaded[arg], 16 * GROUP * expert_round(k, g))
                            for i in range(GROUP):
                                m = pe.matmul(psM[:, i * P:(i + 1) * P], ew[:, arg, i, 0:D], xT[:, arg, i * P:(i + 1) * P],
                                              start=True, stop=True)
                            m.then_inc(misc_ready, 1)
                        elif what == "EY":
                            for i in range(GROUP):
                                m = pe.matmul(psM[:, i * D:(i + 1) * D], hT[:, arg, i * P:(i + 1) * P], ew[:, arg, i, D:2 * D],
                                              start=True, stop=True)
                            m.then_inc(misc_ready, 1)
                        elif what == "A":
                            i, heads = units_a[arg]
                            u = nA.at(k, g) + arg
                            par = (nA.c[k] + arg) % 2
                            if arg == 0:
                                pe.wait_ge(stack_loaded[k % 4], 32 * loads(k, g))
                            if not (isinstance(u, int) and u < 2):
                                pe.wait_ge(a_free, u - 1)
                            w = T if layer == 1 else (i + 1) * P
                            per_bank = T // w
                            for x, h in enumerate(heads):
                                o = psA[:, par, x // per_bank, (x % per_bank) * w:(x % per_bank + 1) * w]
                                pe.matmul(o, Q[0:A_ROWS, k % 4, h, i * P:(i + 1) * P], K[0:A_ROWS, k % 4, h, 0:w],
                                          start=True, stop=False)
                                m = diagonal(pe, o[:, i * P:(i + 1) * P], HALF * t + h, n.mask_q, 2)
                            m.then_inc(a_ready, 1)
                        elif what == "B":
                            kt, heads = units_b[arg]
                            u = nB.at(k, g) + arg
                            slot = (k - 2) % 4
                            if arg == 0:
                                pe.wait_ge(max_loaded[slot], 48 * loads(k - 2, g))
                            if nB.c[k] + arg >= 2:
                                pe.wait_ge(p_ready, u - 1)
                            q0 = 0 if layer == 1 else kt * P
                            w = T - q0
                            for x, h in enumerate(heads):
                                o = psB[:, arg % 2, x * w:(x + 1) * w]
                                pe.matmul(o, K[:, slot, h, kt * P:(kt + 1) * P], Q[:, slot, h, q0:T],
                                          start=True, stop=False)
                                m = diagonal(pe, o[:, kt * P - q0:(kt + 1) * P - q0], HALF * t + h, n.mask_k, 3)
                            m.then_inc(b_ready, 1)
                        elif what == "PV":
                            kt, heads = units_b[arg]
                            u = nB.at(k, g) + arg
                            if arg == 0 and nO.c[k]:
                                pe.wait_ge(o_copied, nO.at(k, g))
                            pe.wait_ge(p_ready, u + 1)
                            q0 = 0 if layer == 1 else kt * P
                            w = T - q0
                            b = (k - 2) // 2
                            for x, h in enumerate(heads):
                                r, j = (HALF * t + h) // 4, h % 4
                                m = pe.matmul(psO[32 * j:32 * (j + 1), q0:T], V[:, b % 2, kt, r, j, :],
                                              Pt[:, (nB.c[k] + arg) % 4, x * w:(x + 1) * w],
                                              start=(kt == 0 and h < 4), stop=(kt == NT - 1 and h >= 4),
                                              skip_group_check=True)
                            m.then_inc(pv_done, 1)
                        elif what == "OT":
                            pe.wait_ge(o_copied, nO.at(k, g) + arg)
                            for i in range(NT):
                                m = pe.transpose(psM[:, i * P:(i + 1) * P], Ob[:, arg, i * P:(i + 1) * P], n.ident[:])
                            m.then_inc(misc_ready, 1)
                        elif what == "ONT":
                            for i in range(NT):
                                m = pe.transpose(psM[:, i * P:(i + 1) * P], ON[:, i, :], n.ident[:])
                            m.then_inc(misc_ready, 1)
                        elif what == "WO":
                            for i in range(NT):
                                o = psM[:, i * D:(i + 1) * D]
                                m = pe.matmul(o, ONT[:, i * P:(i + 1) * P], wo[:], start=True, stop=(layer == 0))
                                if layer == 1:
                                    m = pe.matmul(o, n.ones[:], bo[:], start=False, stop=True)
                            m.then_inc(misc_ready, 1)

                def diagonal(pe, o, head, mask, parts_):
                    if layer == 0:
                        return pe.matmul(o, n.identb[:], mask[:], start=False, stop=True)
                    for s in range(parts_):
                        m = pe.matmul(o, n.alpha_eye[:, head, s, :], n.dist[:], start=False, stop=(s == parts_ - 1))
                    return m
                run_steps(pe, step)

            @block.scalar
            def _(act):
                def project(k, g, pos, b, arg):
                    idx = misc_index(k, g, pos)
                    act.wait_ge(misc_ready, idx + 1)
                    if arg == "C":
                        act.activation(ckv[:, b % 2, :], psM[0:LATENT, :], ACT.Copy).then_inc(misc_free, 1)
                        return
                    s = "QK".index(arg)
                    done = nQK.at(k, g) + (2 if what_is(k, pos) == "PN" and k == 0 else 0)
                    if not (isinstance(done, int) and done == 0):
                        act.wait_ge(parts_ready, done)
                        writes = 96 * done if isinstance(done, int) else 96 * nQK.at(k, 0) + 96 * nQK.round * g
                        act.wait_ge(parts_written, writes)
                    bias, scale = (0.0, 1.0) if layer == 0 else (bk[:], 1.0)
                    if arg == "Q":
                        bias, scale = (0.0, SCALE) if layer == 0 else (bqs[:], SCALE)
                    f = ACT.Copy if layer == 0 else ACT.Identity
                    act.activation(qkf[:, s, :], psM[:], f, bias=bias, scale=scale)
                    act.activation(parts[:, s, 0, :], psM[:], f, bias=bias, scale=scale).then_inc(misc_free, 1)

                def what_is(k, pos):
                    return scripts[k][pos][0]

                def step(k, g):
                    for pos, (what, arg) in enumerate(scripts[k]):
                        if what in ("PJ", "PN"):
                            project(k, g, pos, 0 if what == "PJ" else k // 2 + 1, arg)
                        elif what == "MT":
                            act.wait_ge(misc_ready, misc_index(k, g, pos) + 1)
                            if k > 1:
                                act.wait_ge(max_ready, nMT.at(k, g))
                            if k > 2:
                                hb = k - 3
                                act.wait_ge(max_loaded[hb % 4], 48 * loads(hb, g))
                            act.activation(nm[:], psM[0:HALF, :], ACT.Copy)
                            act.activation(mparts[:, (k - 1) % 2, 0, :], psM[0:HALF, :], ACT.Copy).then_inc(misc_free, 1)
                        elif what == "B":
                            kt, heads = units_b[arg]
                            u = nB.at(k, g) + arg
                            w = len(heads) * (T if layer == 1 else T - kt * P)
                            act.wait_ge(b_ready, u + 1)
                            if nB.c[k] + arg >= 4:
                                act.wait_ge(pv_done, u - 3)
                            act.activation(Pt[:, (nB.c[k] + arg) % 4, 0:w], psB[:, arg % 2, 0:w], ACT.Exp).then_inc(p_ready, 1)
                        elif what == "OC":
                            act.wait_ge(pv_done, nB.at(k, g) + len(units_b))
                            act.activation(Ob[:, k % 2, :], psO[:], ACT.Copy).then_inc(o_copied, 1)
                        elif what == "EH":
                            act.wait_ge(misc_ready, misc_index(k, g, pos) + 1)
                            for i in range(GROUP):
                                m = act.activation(hT[:, arg, i * P:(i + 1) * P], psM[:, i * P:(i + 1) * P], ACT.Gelu,
                                                   bias=ew[:, arg, i, 2 * D:2 * D + 1])
                            m.then_inc(misc_free, 1)
                        elif what == "ONT":
                            act.wait_ge(misc_ready, misc_index(k, g, pos) + 1)
                            act.activation(ONT[:], psM[:], ACT.Copy).then_inc(misc_free, 1)
                run_steps(act, step)

            @block.vector
            def _(dve):
                def add_choices(t):
                    dve.wait_ge(gathered[t // 4 % 4], 128 * (t // 16 + 1))
                    for j in range(2):
                        if j:
                            dve.wait_ge(added, 2 * t + 1)
                        dve.scalar_tensor_tensor(n.x[:, t, :], got[:, t % 16, j, :], n.weights[:, j, t:t + 1],
                                                 n.x[:, t, :], ALU.mult, ALU.add).then_inc(added, 1)

                def step(k, g):
                    for pos, (what, arg) in enumerate(scripts[k]):
                        if what == "A":
                            i, heads = units_a[arg]
                            par = (nA.c[k] + arg) % 2
                            w = T if layer == 1 else (i + 1) * P
                            if arg == 0 and k >= 2:
                                dve.wait_ge(misc_ready, nM.at(k, g))
                            dve.wait_ge(a_ready, nA.at(k, g) + arg + 1)
                            src = psA[:, par, :, 0:w] if T // w == 1 else \
                                psA[:, par].rearrange("p b (x w) -> p (b x) w", w=w)
                            dve.tensor_reduce(maxes[:, k % 2, i, heads[0]:heads[0] + len(heads)], src, AX,
                                              ALU.max, negate=True).then_inc(a_free, 1)
                            if layer == 1 and k == 15:
                                add_choices(arg)
                        elif what == "EX":
                            dve.wait_ge(misc_ready, misc_index(k, g, pos) + 1)
                            dve.tensor_copy(xT[:, arg], psM[:]).then_inc(misc_free, 1)
                        elif what == "EY":
                            dve.wait_ge(misc_ready, misc_index(k, g, pos) + 1)
                            dve.tensor_copy(ys[:, arg].rearrange("p t d -> p (t d)"), psM[:]).then_inc(misc_free, 1)
                        elif what == "V":
                            dve.wait_ge(misc_ready, misc_index(k, g, pos) + 1)
                            if k > 2:
                                dve.wait_ge(pv_done, nB.at(k, g))
                            src = psM[:].rearrange("p (i r j d) -> p i r j d", i=NT, r=4, j=4)
                            for r in range(4):
                                m = dve.tensor_copy(V[:, (k // 2) % 2, :, r, :, HD * r:HD * (r + 1)], src[:, :, r])
                            m.then_inc(misc_free, 1)
                        elif what == "OT":
                            dve.wait_ge(misc_ready, misc_index(k, g, pos) + 1)
                            o = psM[:].rearrange("p (m w) -> p m w", w=32)
                            den, val = 16 * (1 - arg), 16 * arg
                            dve.reciprocal(rden[:, arg], o[:, :, den:den + 2]).then_inc(den_ready, 1)
                            dve.wait_ge(den_ready, nOT.at(k, g) + arg + 1)
                            dve.tensor_tensor(
                                ON[:].rearrange("p i (j w) -> p (i j) w", w=32)[:, :, val:val + 16].rearrange(
                                    "p m (r d) -> p m r d", d=HD),
                                o[:, :, val:val + 16].rearrange("p m (r d) -> p m r d", d=HD),
                                rden[:, arg].unsqueeze(3).broadcast_to([P, 4 * NT, 2, HD]), ALU.mult
                            ).then_inc(misc_free, 1)
                        elif what == "WO":
                            dve.wait_ge(misc_ready, misc_index(k, g, pos) + 1)
                            if layer == 1 and k == STEPS - 1:
                                dve.wait_ge(added, 2 * TILES)
                            b = (k - 3) // 2
                            xv = n.x[:, bass.ds((b + 2 * g) * NT, NT), :]
                            dve.tensor_tensor(xv, psM[:].rearrange("p (i d) -> p i d", i=NT), xv, ALU.add).then_inc(misc_free, 1)
                    if layer == 1 and k == 16:
                        dve.wait_ge(misc_free, nM.at(k, 0))
                        for t in range(16, TILES):
                            add_choices(t)
                run_steps(dve, step)
                dve.wait_ge(misc_free, nM.at(STEPS, 0))

            @block.gpsimd
            def _(pool):
                nS = Counts([3 * sum((x[0] in ("PJ", "PN") and x[1] != "C") or x[0] == "MT" for x in scripts[k])
                             for k in range(STEPS)])

                def scatter(t0):
                    for t in range(t0, t0 + 16):
                        for j in range(2):
                            pool.indirect_dma_start(
                                out=n.xs_dram, out_offset=bass.IndirectOffsetOnAxis(ap=n.slots[:, j, t:t + 1], axis=0),
                                in_=n.slots_flat[:, t * D:(t + 1) * D], in_offset=None).then_inc(placed, 16)

                def gather(t0):
                    for t in range(t0, t0 + 16):
                        if t >= 16 and t % 4 == 0:
                            pool.wait_ge(added, 2 * (t - 12))
                        for j in range(2):
                            pool.indirect_dma_start(
                                out=got[:, t % 16, j, :], out_offset=None, in_=n.ys_dram,
                                in_offset=bass.IndirectOffsetOnAxis(ap=n.slots[:, j, t:t + 1], axis=0)
                            ).then_inc(gathered[t // 4 % 4], 16)

                def split(f, parts3, base, done):
                    pool.tensor_tensor(f, f, parts3[0], ALU.subtract).then_inc(split_step, 1)
                    pool.wait_ge(split_step, base + 1)
                    pool.tensor_tensor(parts3[1], f, n.zeros[0:f.shape[0], :], ALU.add).then_inc(split_step, 1)
                    pool.wait_ge(split_step, base + 2)
                    pool.tensor_tensor(parts3[2], f, parts3[1], ALU.subtract).then_inc(done, 1)

                def step(k, g):
                    count = 0
                    for pos, (what, arg) in enumerate(scripts[k]):
                        base = (nS.at(k, g) // 3 * 2 if isinstance(nS.at(k, g), int)
                                else nS.at(k, 0) // 3 * 2 + nS.round // 3 * 2 * g)
                        if what in ("PJ", "PN") and arg != "C":
                            pool.wait_ge(misc_free, misc_index(k, g, pos) + 1)
                            s = "QK".index(arg)
                            split(qkf[:, s, :], [parts[:, s, x, :] for x in range(3)], base + 2 * count, parts_ready)
                            count += 1
                        elif what == "MT":
                            pool.wait_ge(misc_free, misc_index(k, g, pos) + 1)
                            split(nm[:], [mparts[:, (k - 1) % 2, x, :] for x in range(3)], base + 2 * count, max_ready)
                            count += 1
                    if layer == 1 and k in (0, 1):
                        scatter(16 * k)
                    elif layer == 1 and k in (14, 15):
                        if k == 14:
                            for e in range(2):
                                pool.wait_ge(ys_stored[e], 16 * len(EXPERT_STEPS))
                                pool.wait_ge(xs_loaded[e], 16 * (len(EXPERT_STEPS) + 1))
                                pool.wait_ge(w_loaded[e], 16 * GROUP * (len(EXPERT_STEPS) + 1))
                        gather(16 * (k - 14))
                run_steps(pool, step)



def route(n, c):
    nc, I = n.nc, n.ins
    n.xs_dram = n.dram("xs", (LOAD_TILES * P, D))
    n.ys_dram = n.dram("ys", (SLOT_TILES * P, D))
    n.slots = n.sb("slots", [P, 2, TILES], I32, ctx=c)
    n.weights = n.sb("weights", [P, 2, TILES], ctx=c)
    n.tile_expert = n.sb("tile_expert", [1, LOAD_TILES], I32, ctx=c)
    E = EXPERTS
    n.slots_flat = n.sb("slots_flat", [P, 2 * GROUP * (2 * D + 2 * D + 1)], ctx=c)
    n.alpha_eye = n.sb("alpha_eye", [P, HEADS, 3, P], BF16, ctx=c)
    with ExitStack() as k:
        xn = n.sb("r_xn", [P, 2, T], ctx=k)
        xn_all = n.slots_flat[:, 0:TILES * D].rearrange("p (t d) -> p t d", d=D)
        xnT = n.sb("r_xnT", [P, 2, T], ctx=k)
        wg = n.sb("r_wg", [P, E], ctx=k)
        expert = n.sb("r_expert", [P, E], ctx=k)
        slot_tile = n.sb("r_slot_tile", [1, LOAD_TILES], ctx=k)
        ZT = 8
        assert LOAD_TILES % ZT == 0
        zero = n.sb("r_zero", [P, ZT, D], ctx=k)
        work = n.sb("r_work", [P, 4 * TILES * E], ctx=k)
        logits, pr, before, sums0 = (work[:, j * TILES * E:(j + 1) * TILES * E].rearrange("p (t e) -> p t e", e=E)
                                     for j in range(4))
        eq = n.sb("r_eq", [P, TILES, E], ctx=k)
        hot = [n.sb(f"r_hot{j}", [P, TILES, E], ctx=k) for j in range(2)]
        count = n.sb("r_count", [P, TILES, E], BF16, ctx=k)
        sums = [sums0, n.sb("r_sums1", [P, TILES, E], ctx=k)]
        small = n.sb("r_small", [P, 12, TILES], ctx=k)
        ends = [n.sb(f"r_ends{j}", [P, E], ctx=k) for j in range(2)]
        cmp = work[0:1, 0:LOAD_TILES * E].rearrange("p (t e) -> p t e", e=E)
        te = n.sb("r_te", [1, LOAD_TILES], ctx=k)
        psT = n.pb("r_psT", [P, 2, T], ctx=k)
        psL = n.pb("r_psL", [P, 2, T], ctx=k)
        psC = n.pb("r_psC", [P, 2, T], ctx=k)
        psS = n.pb("r_psS", [P, 2, T], ctx=k)
        normed, turned, kept, scored, read, copied, chain, acted, counted, loaded, zeroed, zero_written = (
            n.sem("r_" + x, k) for x in ("normed", "turned", "kept", "scored", "logits_read", "xn_copied", "chain", "acted",
                                         "counted", "loaded", "zeroed", "zero_written"))
        stored = [n.sem(f"r_stored{p}", k) for p in range(2)]
        shifted, gap_ready, count_ready, combined, ct_turned, ct_kept, b2_ready, b2_added = (
            n.sem("r_" + x, k) for x in ("shifted", "gap_ready", "count_ready", "combined", "ct_turned", "ct_kept",
                                         "b2_ready", "b2_added"))
        bias_rows, eyes, scaled = n.sem("r_bias_rows", k), n.sem("r_eyes", k), n.sem("r_scaled", k)
        b2 = n.sb("r_b2", [E, D], ctx=k)
        ct = n.sb("r_ct", [E, 2, T], ctx=k)
        with nc.Block() as block:
            @block.sync
            def _(sp):
                sp.dma_start(wg[:], I["L1_ffn_Wg"]).then_inc(loaded, 16)
                sp.dma_start(b2[:], I["L1_ffn_b2"]).then_inc(loaded, 16)
                sp.dma_start(expert[:], I["c_expert"]).then_inc(loaded, 16)
                sp.dma_start(slot_tile[:], I["c_slot_tile"]).then_inc(loaded, 16)
                load_attention_weights(n, sp, 1)
                for s in range(4):
                    sp.dma_start(n.Q[PRODUCT_ROWS:MAX_ROW, s],
                                 n.qrows[HALF * (s % 2):HALF * (s % 2 + 1)].rearrange("h r t -> r h t")
                                 ).then_inc(bias_rows, 16)
                sp.wait_ge(zeroed, 1)
                for s in range(LOAD_TILES // ZT):
                    sp.dma_start(n.xs_dram[s * ZT * P:(s + 1) * ZT * P].rearrange("(t p) d -> p t d", p=P),
                                 zero[:]).then_inc(zero_written, 16)
                with sp.Fori(0, SEQS // 2) as g:
                    for p in range(2):
                        b = 2 * g + p
                        sp.wait_ge(kept, b + 1)
                        sp.dma_start(n.xnT_dram[bass.ds(b, 1)].rearrange("o d t -> d (o t)"),
                                     xnT[:, p, :]).then_inc(stored[p], 16)
                for p in range(2):
                    sp.wait_ge(stored[p], 16 * SEQS // 2)
                sp.wait_ge(zero_written, 16 * (LOAD_TILES // ZT))
                sp.wait_ge(bias_rows, 64)

            @block.tensor
            def _(pe):
                pe.wait_ge(loaded, 64)
                def turn(b, p, first):
                    pe.wait_ge(normed, NT * b + NT)
                    if not first:
                        pe.wait_ge(kept, b - 1)
                    for i in range(NT):
                        m = pe.transpose(psT[:, p, i * P:(i + 1) * P], xn[:, p, i * D:(i + 1) * D], n.ident[:])
                    m.then_inc(turned, 1)

                def score(b, p, first):
                    pe.wait_ge(kept, b + 1)
                    if not first:
                        pe.wait_ge(read, b - 1)
                    for i in range(NT):
                        m = pe.matmul(psL[:, p, i * E:(i + 1) * E], xnT[:, p, i * P:(i + 1) * P], wg[:],
                                      start=True, stop=True)
                    m.then_inc(scored, 1)
                for b in range(2):
                    turn(b, b, True)
                    score(b, b, True)
                with pe.Fori(0, SEQS // 2 - 1) as g:
                    for p in range(2):
                        turn(2 * g + 2 + p, p, False)
                        score(2 * g + 2 + p, p, False)
                pe.wait_ge(count_ready, 1)
                cv = count[:].rearrange("p t e -> p (t e)")
                for s in range(2):
                    pe.matmul(psC[:, s, :], n.upper[:], cv[:, s * T:(s + 1) * T], start=True, stop=True)
                    m = pe.matmul(psS[:, s, :], n.ones_b[:], cv[:, s * T:(s + 1) * T], start=True, stop=True)
                m.then_inc(counted, 1)
                pe.wait_ge(combined, 1)
                for b in range(SEQS):
                    if b >= 2:
                        pe.wait_ge(ct_kept, b - 1)
                    for i in range(NT):
                        m = pe.transpose(psT[0:E, b % 2, i * P:(i + 1) * P], eq[:, b * NT + i, :], n.ident[:])
                    m.then_inc(ct_turned, 1)
                    pe.wait_ge(ct_kept, b + 1)
                    if b >= 2:
                        pe.wait_ge(b2_added, b - 1)
                    for i in range(NT):
                        m = pe.matmul(psL[:, b % 2, i * D:(i + 1) * D], ct[:, b % 2, i * P:(i + 1) * P], b2[:],
                                      start=True, stop=True)
                    m.then_inc(b2_ready, 1)

            @block.scalar
            def _(act):
                def body(b, p, first):
                    act.wait_ge(turned, b + 1)
                    if not first:
                        act.wait_ge(stored[p], 8 * (b - p))
                        act.wait_ge(scored, b - 1)
                    act.activation(xnT[:, p, :], psT[:, p, :], ACT.Copy).then_inc(kept, 1)
                    act.activation(xn_all[:, bass.ds(b * NT, NT), :],
                                   xn[:, p, :].rearrange("p (i d) -> p i d", d=D), ACT.Copy).then_inc(copied, 1)
                    act.wait_ge(scored, b + 1)
                    act.activation(logits[:, bass.ds(b * NT, NT), :],
                                   psL[:, p, 0:NT * E].rearrange("p (i e) -> p i e", e=E), ACT.Copy).then_inc(read, 1)
                for b in range(2):
                    body(b, b, True)
                with act.Fori(0, SEQS // 2 - 1) as g:
                    for p in range(2):
                        body(2 * g + 2 + p, p, False)
                for h in range(HEADS):
                    for s in range(3):
                        m = act.activation(n.alpha_eye[:, h, s, :], n.ident[:], ACT.Copy,
                                           scale=n.alpha_parts[:, s, 1 + h:2 + h])
                m.then_inc(eyes, 1)
                act.wait_ge(n.aw_loaded[1], 16 * 23)
                act.activation(n.aw["bqs"][:], n.aw["bq"][:], ACT.Copy, scale=SCALE).then_inc(scaled, 1)
                act.wait_ge(scaled, 1)
                act.wait_ge(shifted, 1)
                act.activation(pr[:], pr[:], ACT.Exp).then_inc(acted, 1)
                act.wait_ge(gap_ready, 1)
                act.activation(small[:, 6, :], small[:, 6, :], ACT.Exp).then_inc(acted, 1)
                for b in range(SEQS):
                    act.wait_ge(ct_turned, b + 1)
                    if b >= 2:
                        act.wait_ge(b2_ready, b - 1)
                    act.activation(ct[:, b % 2, :], psT[0:E, b % 2, :], ACT.Copy).then_inc(ct_kept, 1)

            @block.vector
            def _(dve):
                dve.memset(zero[:], 0.0).then_inc(zeroed, 1)
                def norm(b, p, first):
                    if not first:
                        dve.wait_ge(copied, b - 1)
                        dve.wait_ge(turned, b - 1)
                    for i in range(NT):
                        tile = b * NT + i
                        dve.tensor_scalar(xn[:, p, i * D:(i + 1) * D],
                                          n.x[:, bass.ds(tile, 1), :].rearrange("p o k -> p (o k)"),
                                          n.mean[:, bass.ds(tile, 1)], n.rstd[:, bass.ds(tile, 1)],
                                          ALU.subtract, ALU.mult).then_inc(normed, 1)
                for b in range(2):
                    norm(b, b, True)
                with dve.Fori(0, SEQS // 2 - 1) as g:
                    for p in range(2):
                        norm(2 * g + 2 + p, p, False)

                step = 0

                def then(ins, sem=None):
                    nonlocal step
                    if sem is not None:
                        ins.then_inc(sem, 1)
                        dve.wait_ge(sem, 1)
                        return
                    ins.then_inc(chain, 1)
                    step += 1
                    dve.wait_ge(chain, step)
                mx, sm, rs, top1, top2, id1, dif, id2, w0 = (small[:, j, :] for j in range(9))
                ev = expert[:].unsqueeze(1).broadcast_to([P, TILES, E])
                dve.wait_ge(read, SEQS)
                dve.wait_ge(loaded, 64)
                then(dve.tensor_reduce(mx, logits, AX, ALU.max))
                then(dve.tensor_tensor(pr[:], logits, bc(mx, E), ALU.subtract), shifted)
                dve.wait_ge(acted, 1)
                then(dve.tensor_reduce(sm, pr[:], AX, ALU.add))
                then(dve.reciprocal(rs, sm))
                then(dve.tensor_tensor(pr[:], pr[:], bc(rs, E), ALU.mult))
                for top, ix, j in ((top1, id1, 0), (top2, id2, 1)):
                    then(dve.tensor_reduce(top, pr[:], AX, ALU.max))
                    then(dve.tensor_tensor(eq[:], pr[:], bc(top, E), ALU.is_equal))
                    then(dve.tensor_tensor(eq[:], eq[:], ev, ALU.mult))
                    then(dve.tensor_reduce(ix, eq[:], AX, ALU.min))
                    then(dve.tensor_tensor(hot[j][:], ev, bc(ix, E), ALU.is_equal))
                    if j == 0:
                        then(dve.scalar_tensor_tensor(pr[:], hot[0][:], -4.0, pr[:], ALU.mult, ALU.add))
                then(dve.tensor_tensor(dif, top2, top1, ALU.subtract), gap_ready)
                then(dve.tensor_tensor(count[:], hot[0][:], hot[1][:], ALU.add), count_ready)
                dve.wait_ge(acted, 2)
                then(dve.tensor_scalar(w0, dif, 1.0, None, ALU.add))
                then(dve.reciprocal(n.weights[:, 0, :], w0))
                then(dve.tensor_tensor(n.weights[:, 1, :], dif, n.weights[:, 0, :], ALU.mult))
                then(dve.tensor_tensor(pr[:], hot[0][:], bc(n.weights[:, 0, :], E), ALU.mult))
                then(dve.tensor_tensor(eq[:], hot[1][:], bc(n.weights[:, 1, :], E), ALU.mult))
                then(dve.tensor_tensor(eq[:], eq[:], pr[:], ALU.add), combined)
                dve.wait_ge(counted, 1)
                flat = [x[:].rearrange("p t e -> p (t e)") for x in sums]
                then(dve.tensor_copy(flat[0], psS[:].rearrange("p a t -> p (a t)")))
                src = 0
                for d in (1, 2, 4, 8, 16):
                    dst = 1 - src
                    dve.tensor_copy(sums[dst][:, 0:d, :], sums[src][:, 0:d, :])
                    then(dve.tensor_tensor(sums[dst][:, d:, :], sums[src][:, d:, :], sums[src][:, :TILES - d, :], ALU.add))
                    src = dst
                bf = before.rearrange("p t e -> p (t e)")
                then(dve.tensor_tensor(bf, psC[:].rearrange("p a t -> p (a t)"), flat[src], ALU.add))
                then(dve.tensor_tensor(bf, bf, psS[:].rearrange("p a t -> p (a t)"), ALU.subtract))
                nt, first = n.sb("r_nt", [P, E], ctx=k), n.sb("r_first", [P, E], ctx=k)
                then(dve.tensor_scalar(nt[:], sums[src][:, TILES - 1, :], 1.0 / P, (P - 1) / P - 0.498, ALU.mult, ALU.add))
                then(dve.tensor_scalar(nt[:], nt[:], ROUND, None, ALU.add))
                then(dve.tensor_scalar(nt[:], nt[:], -ROUND, None, ALU.add))
                then(dve.tensor_copy(ends[0][:], nt[:]))
                src = 0
                for d in (1, 2, 4, 8, 16):
                    dst = 1 - src
                    dve.tensor_copy(ends[dst][:, 0:d], ends[src][:, 0:d])
                    then(dve.tensor_tensor(ends[dst][:, d:], ends[src][:, d:], ends[src][:, :E - d], ALU.add))
                    src = dst
                then(dve.tensor_tensor(first[:], ends[src][:], nt[:], ALU.subtract))
                then(dve.tensor_scalar(first[:], first[:], float(P), None, ALU.mult))
                then(dve.tensor_tensor(before, before, first[:].unsqueeze(1).broadcast_to([P, TILES, E]), ALU.add))
                for j in range(2):
                    then(dve.tensor_tensor(pr[:], before, hot[j][:], ALU.mult))
                    then(dve.tensor_reduce(small[:, 9 + j, :], pr[:], AX, ALU.add))
                    dve.tensor_copy(n.slots[:, j, :], small[:, 9 + j, :])
                then(dve.tensor_tensor(cmp, ends[src][0:1, :].unsqueeze(1).broadcast_to([1, LOAD_TILES, E]),
                                       bc(slot_tile[:], E), ALU.is_le))
                then(dve.tensor_reduce(te[:], cmp, AX, ALU.add))
                then(dve.tensor_scalar(n.tile_expert[:], te[:], float(E - 1), None, ALU.min))
                for b in range(SEQS):
                    dve.wait_ge(b2_ready, b + 1)
                    xv = n.x[:, b * NT:(b + 1) * NT, :]
                    dve.tensor_tensor(xv, psL[:, b % 2, :].rearrange("p (i d) -> p i d", d=D), xv, ALU.add).then_inc(b2_added, 1)
                dve.wait_ge(b2_added, SEQS)


def program(nc, ins, out):
    n = Net(nc, ins, out)
    with n.ctx:
        n.mean = n.sb("mean", [P, TILES])
        n.rstd = n.sb("rstd", [P, TILES])
        load_constants(n)
        allocate_attention_weights(n)
        layernorm_stats(n, 0)
        ffn(n)
        prepare_values(n)
        attention(n, 0)
        layernorm_stats(n, 1)
        with ExitStack() as c:
            route(n, c)
            attention(n, 1)


INPUTS = ['L0_attn_x', 'L0_attn_W_DKV', 'L0_attn_W_UK', 'L0_attn_W_UV', 'L0_attn_W_UQ', 'L0_attn_W_O',
          'L0_ffn_w_gate', 'L0_ffn_w_up', 'L0_ffn_w_down', 'L1_attn_qkv_w', 'L1_attn_qkv_b',
          'L1_attn_out_w', 'L1_attn_out_b', 'L1_attn_decay_alpha', 'L1_ffn_Wg', 'L1_ffn_W1', 'L1_ffn_b1',
          'L1_ffn_W2', 'L1_ffn_b2']


def const_arrays():
    i = np.arange(P)
    rows = np.zeros((ROWS - PRODUCT_ROWS, T), np.float32)
    t = np.arange(T)
    for kt in range(NT):
        here = (t // P == kt)
        for part in range(3):
            rows[(kt * 2 + 0) * 3 + part] = here * (t % P)
            rows[(kt * 2 + 1) * 3 + part] = here
    rows[BIAS_ROWS:] = 1.0
    pat = np.zeros((HEADS, NT, 2, T), np.float32)
    for kt in range(NT):
        sign = np.sign(t // P - kt)
        pat[:, kt, 0] = sign
        pat[:, kt, 1] = -sign * (t - P * kt)
    up = (i[:, None] < i[None, :])
    return {
        "c_ident": np.eye(P, dtype=np.float32),
        "c_mask_q": np.where(up, NEG, 0).astype(np.float32),
        "c_mask_k": np.where(up.T, NEG, 0).astype(np.float32),
        "c_dist": -np.abs(i[:, None] - i[None, :]).astype(np.float32),
        "c_upper": up.astype(np.float32),
        "c_krows": rows,
        "c_qpat": pat.reshape(P, T),
        "c_expert": np.broadcast_to(np.arange(EXPERTS, dtype=np.float32) - 2 * EXPERTS, (P, EXPERTS)).copy(),
        "c_slot_tile": np.arange(LOAD_TILES, dtype=np.float32).reshape(1, LOAD_TILES),
    }


def kernel(**inputs):
    import concourse.bacc as bacc
    from concourse.bass_utils import run_bass_kernel_spmd
    a = {k: np.ascontiguousarray(inputs[k]) for k in INPUTS}
    a["qkv_wT"] = np.ascontiguousarray(a["L1_attn_qkv_w"].T)
    a["out_wT"] = np.ascontiguousarray(a["L1_attn_out_w"].T)
    a["alpha_rows"] = np.repeat(a["L1_attn_decay_alpha"], NT * 2).reshape(P, 1)
    a["alpha_all"] = np.tile(a["L1_attn_decay_alpha"], (P, 1))
    a["expert_w"] = np.concatenate([a["L1_ffn_W1"], a["L1_ffn_W2"], a["L1_ffn_b1"][:, :, None]], axis=2)
    a.update(const_arrays())
    for k in ("L1_attn_qkv_w", "L1_attn_out_w", "L1_attn_decay_alpha", "L1_ffn_W1", "L1_ffn_W2", "L1_ffn_b1"):
        del a[k]
    nc = bacc.Bacc("TRN2", target_bir_lowering=False, num_devices=1)
    ins = {k: nc.dram_tensor("in_" + k, v.shape, mybir.dt.from_np(v.dtype), kind="ExternalInput").ap()
           for k, v in a.items()}
    out = nc.dram_tensor("out", (SEQS, T, D), F32, kind="ExternalOutput").ap()
    program(nc, ins, out)
    r = run_bass_kernel_spmd(nc, [{"in_" + k: v for k, v in a.items()}], core_ids=[0])
    return r.results[0]["out"]
```

```python
from contextlib import ExitStack

import numpy as np

import concourse.bass as bass
from concourse import mybir

F32 = mybir.dt.float32
BF16 = mybir.dt.bfloat16
I32 = mybir.dt.int32
ALU = mybir.AluOpType
ACT = mybir.ActivationFunctionType
AX = mybir.AxisListType.X

P = 128
D = 128
SEQS = 8
T = 512
NT = T // P
TILES = SEQS * NT
HEADS = 16
HD = D // HEADS
LATENT = 32
FF = 352
FFC = 3
BLK = 16
EXPERTS = 32
SLOT_TILES = 96
HALF = HEADS // 2
GROUP = 4
STEP_GROUPS = 3
FIRST, ROUND_STEPS, ROUNDS = 6, 4, 2
AFTER = FIRST + ROUND_STEPS * ROUNDS
EXPERT_STEPS = range(FIRST, AFTER)
assert SLOT_TILES == STEP_GROUPS * GROUP * len(EXPERT_STEPS)
LOAD_TILES = SLOT_TILES + STEP_GROUPS * GROUP
EPS = 1e-5
SCALE = float(1.0 / np.sqrt(np.float32(HD)))

Q_PARTS = (0, 0, 0, 1, 1, 2)
K_PARTS = (0, 1, 2, 0, 1, 0)
PRODUCT_ROWS = len(Q_PARTS) * HD
BIAS_ROWS = NT * 2 * 3
MAX_ROW = PRODUCT_ROWS + BIAS_ROWS
ROWS = MAX_ROW + 3
A_ROWS = MAX_ROW
NEG = -1e30
ROUND = 1.5 * 2.0 ** 23


def score_units(layer):
    a, b = [], []
    if layer == 1:
        a = [(i, [2 * p, 2 * p + 1]) for p in range(HALF // 2) for i in range(NT)]
        b = [(kt, [h]) for kt in range(NT) for h in range(HALF)]
    else:
        for i in (3, 2, 1, 0):
            n = {3: 2, 2: 2, 1: 4, 0: 8}[i]
            a += [(i, list(range(h, h + n))) for h in range(0, HALF, n)]
        for kt in range(NT):
            n = {0: 1, 1: 1, 2: 2, 3: 4}[kt]
            b += [(kt, list(range(h, h + n))) for h in range(0, HALF, n)]
    return a, b


STEPS = 2 * SEQS + 2
PV_LAG = 2


def projections(layer):
    return ["C", "Q", "K"] if layer == 0 else ["Q", "K"]


def script(layer, k):
    a, b = score_units(layer)
    out = []
    if k == 0:
        out += [("PJ", p) for p in projections(layer)]
    units_a = list(range(len(a))) if k < 2 * SEQS else []
    units_b = list(range(len(b))) if k >= 2 else []
    side = []
    if 1 <= k <= 2 * SEQS:
        side.append(("MT", 0))
    if k % 2 == 0 and k < 2 * SEQS:
        side.append(("V", 0))
    if layer == 0 and k >= 4 and k % 2 == 0:
        side += [("LS", 0), ("LN", 0)]
    if k % 2 == 0 and k // 2 + 1 < SEQS:
        side += [("PN", p) for p in projections(layer)]
    if k % 2 == 1 and k >= 3:
        side.append(("OT", 0))
    if layer == 0 and k >= 4 and k % 2 == 0:
        side += [("XT", 0), ("LG", 0)]
    if layer == 1 and k in EXPERT_STEPS:
        side += [(what, e) for what in ("EX", "EH", "EY") for e in range(STEP_GROUPS)]
    if layer == 1 and k in (AFTER, AFTER + 1):
        side += [(what, b) for b in range(4 * (k - AFTER), 4 * (k - AFTER) + 4) for what in ("CT", "CB")]
    held = 4 if (k % 2 == 1 and k >= 3 and units_a) else 0
    body_a = units_a[:len(units_a) - held]
    late_a = units_a[len(units_a) - held:]
    done_b = 0
    n_slots = max(len(body_a), 1)
    next_a = 0
    for s in range(n_slots):
        if s < len(body_a) and next_a <= s:
            out.append(("A", body_a[next_a]))
            next_a += 1
        if side and side[0] == ("EH", 1):
            out.append(side.pop(0))
            if next_a < len(body_a):
                out.append(("A", body_a[next_a]))
                next_a += 1
            out.append(side.pop(0))
        upto = len(units_b) * (s + 1) // n_slots
        while done_b < upto:
            out.append(("B", done_b))
            if done_b >= PV_LAG:
                out.append(("PV", done_b - PV_LAG))
            done_b += 1
        if side and side[0] != ("EH", 1) and (s % 2 == 1 or (len(side) > (n_slots - s) // 2 and s)):
            out.append(side.pop(0))
    out += side
    if units_b:
        out += [("PV", m) for m in range(len(units_b) - PV_LAG, len(units_b))]
        out.append(("OC", 0))
    if k % 2 == 1 and k >= 3:
        tail = [("OT", 1), ("ONT", 0), ("WO", 0)]
        if late_a:
            out.append(("A", late_a[0]))
            for n, item in enumerate(tail):
                out += [item, ("A", late_a[n + 1])]
        else:
            out += tail
    if layer == 0 and k == STEPS - 1:
        out += [("LS", 0), ("LN", 0), ("XT", 0), ("LG", 0)]
    if layer == 1 and k < 4:
        routed = []
        for item in out:
            routed.append(item)
            if item[0] == "A" and item[1] % 4 == 3:
                m = 4 * k + item[1] // 4
                routed += [("R", m)] + {5: [("RS", 0), ("RS", 1)], 6: [("RC", 0), ("RC", 1)]}.get(m, [])
        out = routed
    return out


class Counts:

    def __init__(self, per_step):
        self.c = [0]
        for n in per_step:
            self.c.append(self.c[-1] + n)
        self.round = self.c[FIRST + ROUND_STEPS] - self.c[FIRST]
        assert self.c[AFTER] - self.c[FIRST] == ROUNDS * self.round

    def at(self, k, g):
        return self.c[k] + g * self.round if FIRST <= k < FIRST + ROUND_STEPS else self.c[k]


def run_steps(engine, step):
    for k in range(FIRST):
        step(k, 0)
    with engine.Fori(0, ROUNDS) as g:
        for r in range(ROUND_STEPS):
            step(FIRST + r, g)
    for k in range(AFTER, STEPS):
        step(k, 0)


MISC = ("PJ", "PN", "V", "MT", "OT", "ONT", "WO", "EX", "EH", "EY", "XT", "LG", "RS", "RC", "CT", "CB")


class Net:
    def __init__(self, nc, ins, out):
        self.nc, self.ins, self.out = nc, ins, out
        self.ctx = ExitStack()

    def sb(self, name, shape, dt=F32, ctx=None):
        return (ctx or self.ctx).enter_context(self.nc.sbuf_tensor(name, shape, dt))

    def pb(self, name, shape, dt=F32, ctx=None):
        return (ctx or self.ctx).enter_context(self.nc.psum_tensor(name, shape, dt))

    def sem(self, name, ctx=None):
        return (ctx or self.ctx).enter_context(self.nc.semaphore(name))

    def dram(self, name, shape, dt=F32):
        return self.nc.dram_tensor(name, shape, dt, kind="Internal").ap()



def load_constants(n, f):
    nc, I = n.nc, n.ins
    n.x = n.sb("x", [P, TILES, D])
    n.ident = n.sb("ident", [P, P])
    n.identb = n.sb("identb", [P, P], BF16)
    n.mask_q = n.sb("mask_q", [P, P], BF16)
    n.mask_k = n.sb("mask_k", [P, P], BF16)
    n.dist = n.sb("dist", [P, P], BF16)
    n.ones = n.sb("ones", [1, P])
    n.zeros = n.sb("zeros", [P, T])
    n.ones_b = n.sb("ones_b", [P, P], BF16)
    n.upper = n.sb("upper", [P, P], BF16)
    n.xnT_dram = n.dram("xnT_dram", (SEQS, D, T))
    n.wg = n.sb("wg", [P, EXPERTS])
    n.b2 = n.sb("b2", [EXPERTS, D])
    n.expert = n.sb("expert", [P, EXPERTS])
    n.slot_tile = n.sb("slot_tile", [1, LOAD_TILES])
    n.xs_dram = n.dram("xs", (LOAD_TILES * P, D))
    n.ys_dram = n.dram("ys", (SLOT_TILES * P, D))
    n.xnT1_dram = n.dram("xnT1_dram", (SEQS, D, T))
    n.const_sem = n.sem("constants_loaded")
    n.x_sem = n.sem("x_loaded")
    n.memset_sem = n.sem("ones_set")
    n.Q = n.sb("Q", [ROWS, 4, HALF, T], BF16)
    n.K = n.sb("K", [ROWS, 4, HALF, T], BF16)
    n.k_const = n.sem("key_rows_loaded")
    n.q_zeroed = n.sem("query_rows_zeroed")
    x_v = I["L0_attn_x"].rearrange("b (i p) d -> p (b i) d", p=P)
    n.qrows = n.dram("qrows", (HEADS, BIAS_ROWS, T), BF16)
    A = HEADS + 1
    n.aw = {}
    n.aw_loaded = [n.sem(f"attention_weights_loaded{x}") for x in range(2)]
    allocate_attention_weights(n, None, 0)
    n.alpha_parts = n.sb("alpha_parts", [P, 3, A])
    n.w_raw = n.sb("w_raw", [P, 2 * FFC * D + FF], ctx=f)
    w, rem = n.w_raw, FF - 2 * P
    w_zeroed, w_loaded = n.sem("w_zeroed", f), n.sem("w_loaded", f)
    with ExitStack() as k, nc.Block() as block:
        raw = n.sb("al_raw", [P, A], ctx=k)
        neg = n.sb("al_neg", [P, A], ctx=k)
        e = n.sb("al_e", [P, A], ctx=k)
        al = n.sb("alpha", [P, A], ctx=k)
        ap = n.sb("al_parts_b", [P, 3, A], BF16, ctx=k)
        pat = n.sb("al_pat", [P, T], ctx=k)
        qb = n.sb("al_rows", [P, 3, T], BF16, ctx=k)
        loaded, stored = n.sem("al_loaded", k), n.sem("al_stored", k)
        v, a = n.sem("al_vec", k), n.sem("al_act", k)

        @block.scalar
        def _(act):
            act.wait_ge(v, 2)
            act.activation(e[:], neg[:], ACT.Exp).then_inc(a, 1)
            act.wait_ge(v, 3)
            act.activation(e[:], e[:], ACT.Ln).then_inc(a, 1)

        @block.sync
        def _(sp):
            sp.dma_start(raw[:, 0:1], I["alpha_rows"]).then_inc(loaded, 16)
            sp.dma_start(raw[:, 1:A], I["alpha_all"]).then_inc(loaded, 16)
            sp.dma_start(pat[:], I["c_qpat"]).then_inc(loaded, 16)
            sp.dma_start(n.ident[:], I["c_ident"]).then_inc(n.x_sem, 16)
            for s in range(4):
                sp.dma_start(n.x[:, 8 * s:8 * s + 8, :], x_v[:, 8 * s:8 * s + 8, :]).then_inc(n.x_sem, 16)
            sp.wait_ge(v, 14)
            sp.dma_start(n.qrows.rearrange("h (r s) t -> (h r) s t", s=3), qb[:]).then_inc(stored, 16)
            sp.wait_ge(n.const_sem, 16 * 5)
            sp.wait_ge(stored, 16)
            sp.wait_ge(w_zeroed, 1)
            for s, name in enumerate(("L0_ffn_w_gate", "L0_ffn_w_up")):
                for q in range(FFC):
                    m = P if q < 2 else rem
                    sp.dma_start(w[0:m, (s * FFC + q) * D:(s * FFC + q + 1) * D],
                                 I[name][q * P:q * P + m, :]).then_inc(w_loaded, 16)
            sp.dma_start(w[:, 2 * FFC * D:], I["L0_ffn_w_down"]).then_inc(w_loaded, 16)
            for dst, name in ((n.wg, "L1_ffn_Wg"), (n.b2, "L1_ffn_b2"), (n.expert, "c_expert"), (n.slot_tile, "c_slot_tile")):
                sp.dma_start(dst[:], I[name]).then_inc(n.x_sem, 16)
            sp.wait_ge(w_loaded, 16 * 7)
            sp.wait_ge(n.x_sem, 16 * 9)

        @block.gpsimd
        def _(pool):
            for dst, src in ((n.identb, "c_ident"), (n.mask_q, "c_mask_q"), (n.mask_k, "c_mask_k"),
                             (n.dist, "c_dist"), (n.upper, "c_upper")):
                pool.dma_start(dst[:], I[src]).then_inc(n.const_sem, 16)

        @block.vector
        def _(dve):
            for s in range(2):
                m = dve.memset(w[rem:P, (s * FFC + 2) * D:(s * FFC + 3) * D], 0.0)
            m.then_inc(w_zeroed, 1)
            dve.memset(n.ones[:], 1.0)
            dve.memset(n.zeros[:], 0.0)
            dve.memset(n.ones_b[:], 1.0).then_inc(n.memset_sem, 1)
            dve.wait_ge(n.memset_sem, 1)
            step = 0

            def then(ins):
                nonlocal step
                ins.then_inc(v, 1)
                step += 1
                dve.wait_ge(v, step)
            dve.wait_ge(loaded, 48)
            then(dve.tensor_scalar(neg[:], raw[:], -1.0, None, ALU.mult))
            then(dve.tensor_tensor(neg[:], neg[:], raw[:], ALU.min))
            dve.wait_ge(a, 1)
            then(dve.tensor_scalar(e[:], e[:], 1.0, None, ALU.add))
            dve.wait_ge(a, 2)
            then(dve.scalar_tensor_tensor(al[:], raw[:], 0.0, e[:], ALU.max, ALU.add))
            then(dve.tensor_copy(ap[:, 0, :], al[:]))
            then(dve.tensor_tensor(e[:], al[:], ap[:, 0, :], ALU.subtract))
            then(dve.tensor_copy(ap[:, 1, :], e[:]))
            then(dve.tensor_tensor(ap[:, 2, :], e[:], ap[:, 1, :], ALU.subtract))
            then(dve.tensor_scalar(pat[:], pat[:], al[:, 0:1], None, ALU.mult))
            then(dve.tensor_copy(qb[:, 0, :], pat[:]))
            then(dve.tensor_tensor(pat[:], pat[:], qb[:, 0, :], ALU.subtract))
            then(dve.tensor_copy(qb[:, 1, :], pat[:]))
            then(dve.tensor_tensor(qb[:, 2, :], pat[:], qb[:, 1, :], ALU.subtract))
            then(dve.tensor_copy(n.alpha_parts[:], ap[:]))
            dve.memset(n.Q[:].bitcast(F32), 0.0).then_inc(n.q_zeroed, 1)
            dve.wait_ge(n.q_zeroed, 1)



MIDS_LOW = (0.25, 0.75, 1.25, 1.75)


def quant_scales(dve, ab, am, sc, rs, half, sem, base):
    dve.tensor_reduce(am, ab, AX, ALU.max).then_inc(sem, 1)
    dve.wait_ge(sem, base + 1)
    dve.tensor_scalar(sc, am, 1.0 / 6.0, 1e-12, ALU.mult, ALU.max).then_inc(sem, 1)
    dve.wait_ge(sem, base + 2)
    dve.tensor_scalar(half, sc, 0.5, None, ALU.mult).then_inc(sem, 1)
    dve.reciprocal(rs, sc).then_inc(sem, 1)


def quant_grid(dve, a, u, t, sem, base):
    quant_grid_first(dve, a, u, t, sem, base)
    quant_grid_middle(dve, a, u, t, sem, base)
    quant_grid_last(dve, a, u, t, sem, base)


def quant_grid_first(dve, a, u, t, sem, base):
    dve.tensor_scalar(u, a, 5.0, 2.0, ALU.is_gt, ALU.mult).then_inc(sem, 1)
    dve.tensor_scalar(t, a, MIDS_LOW[0], None, ALU.is_gt).then_inc(sem, 1)
    dve.wait_ge(sem, base + 1)
    dve.scalar_tensor_tensor(u, a, 3.5, u, ALU.is_gt, ALU.add).then_inc(sem, 1)
    dve.wait_ge(sem, base + 2)
    dve.scalar_tensor_tensor(t, a, MIDS_LOW[1], t, ALU.is_gt, ALU.add).then_inc(sem, 1)


def quant_grid_middle(dve, a, u, t, sem, base):
    dve.wait_ge(sem, base + 3)
    dve.scalar_tensor_tensor(u, a, 2.5, u, ALU.is_gt, ALU.add).then_inc(sem, 1)
    dve.wait_ge(sem, base + 4)
    dve.scalar_tensor_tensor(t, a, MIDS_LOW[2], t, ALU.is_gt, ALU.add).then_inc(sem, 1)


def quant_grid_last(dve, a, u, t, sem, base):
    dve.wait_ge(sem, base + 6)
    dve.scalar_tensor_tensor(t, a, MIDS_LOW[3], t, ALU.is_gt, ALU.add).then_inc(sem, 1)
    dve.wait_ge(sem, base + 7)
    dve.scalar_tensor_tensor(t, u, 2.0, t, ALU.mult, ALU.add).then_inc(sem, 1)


SCALES_INC, GRID_INC = 4, 8


def bc(ap, n):
    return ap.unsqueeze(2).broadcast_to([ap.shape[0], ap.shape[1], n])


def blocks(ap):
    return ap.rearrange("p (m k) -> p m k", k=BLK)



def layernorm_stats(n, layer):
    nc = n.nc
    with ExitStack() as c:
        st = n.sb(f"bn{layer}", [P, TILES, 6], ctx=c)
        dm = n.sb(f"bn_dm{layer}", [P, TILES], ctx=c)
        m2 = n.sb(f"bn_m2{layer}", [P, TILES], ctx=c)
        sd = n.sb(f"bn_sd{layer}", [P, TILES], ctx=c)
        s = n.sem(f"stats_step{layer}", c)
        s_sd = n.sem(f"sd_ready{layer}", c)
        with nc.Block() as block:
            @block.vector
            def _(dve):
                with dve.Fori(0, SEQS) as b:
                    for i in range(NT):
                        dve.bn_stats(st[:, bass.ds(b * NT + i, 1), :].rearrange("p o k -> p (o k)"),
                                     n.x[:, bass.ds(b * NT + i, 1), :].rearrange("p o k -> p (o k)")).then_inc(s, 1)
                v = TILES
                dve.wait_ge(s, v)
                dve.tensor_tensor(n.mean[:], st[:, :, 1], st[:, :, 4], ALU.add).then_inc(s, 1)
                dve.tensor_tensor(dm[:], st[:, :, 1], st[:, :, 4], ALU.subtract).then_inc(s, 1)
                dve.tensor_tensor(m2[:], st[:, :, 2], st[:, :, 5], ALU.add).then_inc(s, 1)
                dve.wait_ge(s, v + 3)
                dve.tensor_scalar(n.mean[:], n.mean[:], 0.5, None, ALU.mult).then_inc(s, 1)
                dve.tensor_tensor(dm[:], dm[:], dm[:], ALU.mult).then_inc(s, 1)
                dve.wait_ge(s, v + 5)
                dve.scalar_tensor_tensor(m2[:], dm[:], float(P // 4), m2[:], ALU.mult, ALU.add).then_inc(s, 1)
                dve.wait_ge(s, v + 6)
                dve.tensor_scalar(m2[:], m2[:], 1.0 / D, EPS, ALU.mult, ALU.add).then_inc(s, 1)
                dve.wait_ge(s_sd, 1)
                dve.reciprocal(n.rstd[:], sd[:]).then_inc(s, 1)
                dve.wait_ge(s, v + 8)

            @block.scalar
            def _(act):
                act.wait_ge(s, TILES + 7)
                act.activation(sd[:], m2[:], ACT.Sqrt).then_inc(s_sd, 1)



def prepare_ffn_weights(n, c):
    nc, I = n.nc, n.ins
    W = 2 * FFC * D + FF
    n.wguT = n.sb("wguT", [P, 2 * FF], ctx=c)
    n.wdT = n.sb("wdT", [P, FFC, D], ctx=c)
    with ExitStack() as k:
        w = n.w_raw
        ab = n.sb("w_abs", [P, W], ctx=k)
        sg = n.sb("w_sign", [P, W], ctx=k)
        t = n.sb("w_t", [P, W], ctx=k)
        u = n.sb("w_u", [P, W], ctx=k)
        am, sc, rs, hs = (n.sb(f"w_{x}", [P, W // BLK], ctx=k) for x in ("am", "sc", "rs", "hs"))
        ps = n.pb("w_ps", [P, 3, 512], ctx=k)
        signed, scaled, normed, gridded, quantised, turned, kept = (
            n.sem(f"w_{x}", k) for x in ("signed", "scaled", "normed", "gridded",
                                         "quantised", "turned", "kept"))
        rem = FF - 2 * P
        with nc.Block() as block:
            @block.scalar
            def _(act):
                act.activation(ab[:], w[:], ACT.Abs).then_inc(signed, 1)
                act.activation(sg[:], w[:], ACT.Sign).then_inc(signed, 1)
                act.wait_ge(turned, 2)
                act.activation(n.wguT[:, 0:FF], ps[:, 0, 0:FF], ACT.Copy).then_inc(kept, 1)
                act.activation(n.wguT[:, FF:2 * FF], ps[:, 1, 0:FF], ACT.Copy).then_inc(kept, 1)
                act.wait_ge(turned, 3)
                act.activation(n.wdT[:, 0:2, :], ps[:, 2, 0:2 * D].rearrange("p (c d) -> p c d", c=2),
                               ACT.Copy).then_inc(kept, 1)
                act.activation(n.wdT[0:rem, 2, :], ps[0:rem, 2, 2 * D:3 * D], ACT.Copy).then_inc(kept, 1)
                act.wait_ge(kept, 4)

            @block.vector
            def _(dve):
                dve.wait_ge(signed, 1)
                quant_scales(dve, blocks(ab[:]), am[:], sc[:], rs[:], hs[:], scaled, 0)
                dve.wait_ge(normed, 1)
                quant_grid(dve, ab[:], u[:], t[:], gridded, 0)

            @block.gpsimd
            def _(pool):
                pool.wait_ge(scaled, SCALES_INC)
                pool.tensor_tensor(blocks(ab[:]), blocks(ab[:]), bc(rs[:], BLK), ALU.mult).then_inc(normed, 1)
                pool.wait_ge(gridded, GRID_INC)
                pool.tensor_tensor(blocks(t[:]), blocks(t[:]), bc(hs[:], BLK), ALU.mult).then_inc(quantised, 1)
                pool.wait_ge(quantised, 1)
                pool.wait_ge(signed, 2)
                pool.tensor_tensor(t[:], t[:], sg[:], ALU.mult).then_inc(quantised, 1)

            @block.tensor
            def _(pe):
                pe.wait_ge(quantised, 2)
                for s in range(2):
                    for q in range(FFC):
                        r = P if q < 2 else rem
                        m = pe.transpose(ps[:, s, q * P:q * P + r],
                                         t[0:r, (s * FFC + q) * D:(s * FFC + q + 1) * D], n.ident[0:r, 0:r])
                    m.then_inc(turned, 1)
                for q in range(FFC):
                    r = P if q < 2 else rem
                    m = pe.transpose(ps[0:r, 2, q * D:(q + 1) * D],
                                     t[:, 2 * FFC * D + q * P:2 * FFC * D + q * P + r], n.ident[:])
                m.then_inc(turned, 1)


def run_ffn_steps(engine, stages):
    def iteration(it, shift):
        for off, f in stages:
            b = it + off
            if 0 <= b < SEQS:
                f(b + 2 * shift, b % 2)
    for it in (-2, -1, 0, 1):
        iteration(it, 0)
    with engine.Fori(0, 2) as g:
        for it in (2, 3):
            iteration(it, g)
    for it in range(6, SEQS + 1):
        iteration(it, 0)


def ffn(n):
    nc = n.nc
    HW = NT * FF
    with ExitStack() as c:
        prepare_ffn_weights(n, c)
        buf = {}
        for w, size in (("x", T), ("h", HW)):
            for name in ("v", "ab", "sg", "t"):
                buf[w + name] = n.sb(f"f_{w}{name}", [P, 2, size], ctx=c)
            buf[w + "u"] = n.sb(f"f_{w}u", [P, size], ctx=c)
            for name in ("am", "sc"):
                buf[w + name] = n.sb(f"f_{w}{name}", [P, size // BLK], ctx=c)
            for name in ("rs", "hs"):
                buf[w + name] = n.sb(f"f_{w}{name}", [P, 2, size // BLK], ctx=c)
        xqT = n.sb("f_xqT", [P, T], ctx=c)
        xnT = n.sb("f_xnT", [P, 2, T], ctx=c)
        silu = n.sb("f_silu", [P, 2, FF], ctx=c)
        hqT = n.sb("f_hqT", [P, FFC, T], ctx=c)
        ps_n = n.pb("f_ps_n", [P, T], ctx=c)
        ps_x = n.pb("f_ps_x", [P, T], ctx=c)
        ps_g = n.pb("f_ps_g", [P, 2, 512], ctx=c)
        ps_u = n.pb("f_ps_u", [P, 2, 512], ctx=c)
        ps_h = n.pb("f_ps_h", [P, T], ctx=c)
        ps_d = n.pb("f_ps_d", [P, NT, D], ctx=c)
        S = {x: n.sem("ffn_" + x, c) for x in (
            "normed", "xn_turned", "xn_kept", "x_split", "x_scaled", "x_div", "x_grid", "x_q",
            "xq_turned", "xq_kept", "gate_up", "silu", "h_ready", "h_split", "h_scaled", "h_div",
            "h_grid", "h_q", "hq_turned", "hq_kept", "down", "added")}
        stored = [n.sem(f"ffn_xnT_stored{p}", c) for p in range(2)]
        slots_zeroed = n.sem("slots_zeroed", c)
        rem = FF - 2 * P

        with nc.Block() as block:
            @block.sync
            def _(sp):
                weights = load_attention_weights(n, sp, 0)
                for s in range(LOAD_TILES // NT):
                    sp.dma_start(n.xs_dram[s * NT * P:(s + 1) * NT * P].rearrange("(t p) d -> p t d", p=P),
                                 n.zeros[:].rearrange("p (t d) -> p t d", d=D)).then_inc(slots_zeroed, 16)
                with sp.Fori(0, SEQS // 2) as g:
                    for p in range(2):
                        b = 2 * g + p
                        sp.wait_ge(S["xn_kept"], b + 1)
                        sp.dma_start(n.xnT_dram[bass.ds(b, 1)].rearrange("o d t -> d (o t)"),
                                     xnT[:, p, :]).then_inc(stored[p], 16)
                for p in range(2):
                    sp.wait_ge(stored[p], 16 * SEQS // 2)
                sp.wait_ge(n.aw_loaded[0], weights)
                sp.wait_ge(slots_zeroed, 16 * (LOAD_TILES // NT))

            @block.vector
            def _(dve):
                def s1(b, p):
                    if not (isinstance(b, int) and b < 2):
                        dve.wait_ge(S["x_split"], 2 * (b - 1))
                        dve.wait_ge(S["xn_turned"], b - 1)
                    for i in range(NT):
                        tile = b * NT + i
                        dve.tensor_scalar(buf["xv"][:, p, i * D:(i + 1) * D],
                                          n.x[:, bass.ds(tile, 1), :].rearrange("p o k -> p (o k)"),
                                          n.mean[:, bass.ds(tile, 1)], n.rstd[:, bass.ds(tile, 1)],
                                          ALU.subtract, ALU.mult).then_inc(S["normed"], 1)
                    dve.wait_ge(S["x_split"], 2 * b + 1)
                    if not (isinstance(b, int) and b < 2):
                        dve.wait_ge(S["x_q"], 2 * (b - 1))
                    quant_scales(dve, blocks(buf["xab"][:, p]), buf["xam"][:], buf["xsc"][:],
                                 buf["xrs"][:, p], buf["xhs"][:, p], S["x_scaled"], SCALES_INC * b)

                def s3(b, p):
                    dve.wait_ge(S["x_div"], b + 1)
                    if not (isinstance(b, int) and b < 2):
                        dve.wait_ge(S["xq_turned"], b - 1)
                    quant_grid(dve, buf["xab"][:, p], buf["xu"][:], buf["xt"][:, p], S["x_grid"], GRID_INC * b)

                def s5(b, p):
                    if not (isinstance(b, int) and b < 2):
                        dve.wait_ge(S["h_split"], 2 * (b - 1))
                    multiply(b, p, (0, 1))

                def multiply(b, p, tiles):
                    for i in tiles:
                        dve.wait_ge(S["silu"], NT * b + i + 1)
                        dve.tensor_tensor(buf["hv"][:, p, i * FF:(i + 1) * FF], ps_u[:, i % 2, 0:FF],
                                          silu[:, i % 2, :], ALU.mult).then_inc(S["h_ready"], 1)

                def s6(b, p):
                    dve.wait_ge(S["h_split"], 2 * b + 1)
                    if not (isinstance(b, int) and b < 2):
                        dve.wait_ge(S["h_q"], 2 * (b - 1))
                    quant_scales(dve, blocks(buf["hab"][:, p]), buf["ham"][:], buf["hsc"][:],
                                 buf["hrs"][:, p], buf["hhs"][:, p], S["h_scaled"], SCALES_INC * b)

                def s5_rest(b, p):
                    multiply(b, p, (2, 3))

                def s8(b, p):
                    dve.wait_ge(S["h_div"], b + 1)
                    if not (isinstance(b, int) and b < 2):
                        dve.wait_ge(S["hq_turned"], FFC * (b - 1))
                    quant_grid_first(dve, buf["hab"][:, p], buf["hu"][:], buf["ht"][:, p], S["h_grid"], GRID_INC * b)

                def s8_middle(b, p):
                    quant_grid_middle(dve, buf["hab"][:, p], buf["hu"][:], buf["ht"][:, p], S["h_grid"], GRID_INC * b)

                def s8_last(b, p):
                    quant_grid_last(dve, buf["hab"][:, p], buf["hu"][:], buf["ht"][:, p], S["h_grid"], GRID_INC * b)

                def s10(b, p):
                    dve.wait_ge(S["down"], b + 1)
                    xv = n.x[:, bass.ds(b * NT, NT), :]
                    dve.tensor_tensor(xv, ps_d[:], xv, ALU.add).then_inc(S["added"], 1)

                run_ffn_steps(dve, [(1, s3), (0, s6), (2, s1), (0, s8), (0, s8_middle), (-1, s10), (1, s5),
                                    (0, s8_last), (1, s5_rest)])
                dve.wait_ge(S["added"], SEQS)

            @block.scalar
            def _(act):
                def a1(b, p):
                    act.wait_ge(S["normed"], NT * b + NT)
                    if not (isinstance(b, int) and b < 2):
                        act.wait_ge(S["x_grid"], GRID_INC * (b - 1))
                        act.wait_ge(S["x_q"], 2 * (b - 1))
                    act.activation(buf["xab"][:, p], buf["xv"][:, p], ACT.Abs).then_inc(S["x_split"], 1)
                    act.activation(buf["xsg"][:, p], buf["xv"][:, p], ACT.Sign).then_inc(S["x_split"], 1)

                def a1_rest(b, p):
                    act.wait_ge(S["xn_turned"], b + 1)
                    if not (isinstance(b, int) and b < 2):
                        act.wait_ge(stored[p], 8 * (b - p))
                    act.activation(xnT[:, p, :], ps_n[:], ACT.Copy).then_inc(S["xn_kept"], 1)

                def a5(b, p):
                    act.wait_ge(S["xq_turned"], b + 1)
                    if not (isinstance(b, int) and b < 1):
                        act.wait_ge(S["gate_up"], NT * b)
                    act.activation(xqT[:], ps_x[:], ACT.Copy).then_inc(S["xq_kept"], 1)
                    for i in range(NT):
                        act.wait_ge(S["gate_up"], NT * b + i + 1)
                        if i >= 2:
                            act.wait_ge(S["h_ready"], NT * b + i - 1)
                        elif not (isinstance(b, int) and b < 1):
                            act.wait_ge(S["h_ready"], NT * b + i - 1)
                        act.activation(silu[:, i % 2, :], ps_g[:, i % 2, 0:FF], ACT.Silu).then_inc(S["silu"], 1)

                def a6(b, p):
                    act.wait_ge(S["h_ready"], NT * b + NT)
                    if not (isinstance(b, int) and b < 2):
                        act.wait_ge(S["h_grid"], GRID_INC * (b - 1))
                        act.wait_ge(S["h_q"], 2 * (b - 1))
                    act.activation(buf["hab"][:, p], buf["hv"][:, p], ACT.Abs).then_inc(S["h_split"], 1)
                    act.activation(buf["hsg"][:, p], buf["hv"][:, p], ACT.Sign).then_inc(S["h_split"], 1)

                def a10(b, p):
                    for q in range(FFC):
                        act.wait_ge(S["hq_turned"], FFC * b + q + 1)
                        if not (isinstance(b, int) and b < 1):
                            act.wait_ge(S["down"], b)
                        r = P if q < 2 else rem
                        act.activation(hqT[0:r, q, :], ps_h[0:r, :], ACT.Copy).then_inc(S["hq_kept"], 1)

                run_ffn_steps(act, [(0, a6), (-1, a10), (2, a1), (2, a1_rest), (1, a5)])

            @block.gpsimd
            def _(pool):
                for s in range(4):
                    pool.dma_start(n.K[PRODUCT_ROWS:ROWS, s],
                                   n.ins["c_krows"].unsqueeze(1).broadcast_to([ROWS - PRODUCT_ROWS, HALF, T])
                                   ).then_inc(n.k_const, 16)

                def divide(w, b, p):
                    pool.wait_ge(S[w + "_scaled"], SCALES_INC * (b + 1))
                    v = blocks(buf[w + "ab"][:, p])
                    pool.tensor_tensor(v, v, bc(buf[w + "rs"][:, p], BLK), ALU.mult).then_inc(S[w + "_div"], 1)

                def scale(w, b, p):
                    pool.wait_ge(S[w + "_grid"], GRID_INC * (b + 1))
                    v = blocks(buf[w + "t"][:, p])
                    pool.tensor_tensor(v, v, bc(buf[w + "hs"][:, p], BLK), ALU.mult).then_inc(S[w + "_q"], 1)
                    pool.wait_ge(S[w + "_q"], 2 * b + 1)
                    pool.wait_ge(S[w + "_split"], 2 * b + 2)
                    pool.tensor_tensor(buf[w + "t"][:, p], buf[w + "t"][:, p], buf[w + "sg"][:, p],
                                       ALU.mult).then_inc(S[w + "_q"], 1)

                run_ffn_steps(pool, [(1, lambda b, p: scale("x", b, p)), (0, lambda b, p: divide("h", b, p)),
                                     (2, lambda b, p: divide("x", b, p)), (0, lambda b, p: scale("h", b, p))])
                pool.wait_ge(n.k_const, 64)

            @block.tensor
            def _(pe):
                def p1(b, p):
                    pe.wait_ge(S["normed"], NT * b + NT)
                    if not (isinstance(b, int) and b < 1):
                        pe.wait_ge(S["xn_kept"], b)
                    for i in range(NT):
                        m = pe.transpose(ps_n[:, i * P:(i + 1) * P], buf["xv"][:, p, i * D:(i + 1) * D], n.ident[:])
                    m.then_inc(S["xn_turned"], 1)

                def p5(b, p):
                    pe.wait_ge(S["x_q"], 2 * b + 2)
                    if not (isinstance(b, int) and b < 1):
                        pe.wait_ge(S["xq_kept"], b)
                    for i in range(NT):
                        m = pe.transpose(ps_x[:, i * P:(i + 1) * P], buf["xt"][:, p, i * D:(i + 1) * D], n.ident[:])
                    m.then_inc(S["xq_turned"], 1)
                    pe.wait_ge(S["xq_kept"], b + 1)
                    for i in range(NT):
                        if i >= 2 or not (isinstance(b, int) and b < 1):
                            pe.wait_ge(S["h_ready"], NT * b + i - 1)
                        pe.matmul(ps_g[:, i % 2, 0:FF], xqT[:, i * P:(i + 1) * P], n.wguT[:, 0:FF], start=True, stop=True)
                        pe.matmul(ps_u[:, i % 2, 0:FF], xqT[:, i * P:(i + 1) * P], n.wguT[:, FF:2 * FF],
                                  start=True, stop=True).then_inc(S["gate_up"], 1)

                def p10(b, p):
                    pe.wait_ge(S["h_q"], 2 * b + 2)
                    for q in range(FFC):
                        if q or not (isinstance(b, int) and b < 1):
                            pe.wait_ge(S["hq_kept"], FFC * b + q)
                        r = P if q < 2 else rem
                        for i in range(NT):
                            m = pe.transpose(ps_h[0:r, i * P:(i + 1) * P],
                                             buf["ht"][:, p, i * FF + q * P:i * FF + q * P + r], n.ident[:])
                        m.then_inc(S["hq_turned"], 1)
                    pe.wait_ge(S["hq_kept"], FFC * (b + 1))
                    if not (isinstance(b, int) and b < 1):
                        pe.wait_ge(S["added"], b)
                    for i in range(NT):
                        for q in range(FFC):
                            r = P if q < 2 else rem
                            m = pe.matmul(ps_d[:, i, :], hqT[0:r, q, i * P:(i + 1) * P], n.wdT[0:r, q, :],
                                          start=(q == 0), stop=(q == FFC - 1))
                    m.then_inc(S["down"], 1)

                run_ffn_steps(pe, [(-1, p10), (2, p1), (1, p5)])



def allocate_attention_weights(n, c, layer):
    rows = {"q": P, "k": P, "v": P, "o": P, "bv": 1, "bo": 1, "dkv": P, "bq": P, "bqs": P, "bk": P}
    cols = {"dkv": LATENT, "bq": 1, "bqs": 1, "bk": 1}
    n.aw[layer] = {x: n.sb(f"aw{layer}_{x}", [m, cols.get(x, D)], ctx=c)
                   for x, m in rows.items() if (x in ("q", "k", "v", "o") or (x == "dkv") == (layer == 0))}


def load_attention_weights(n, sp, layer):
    I, a = n.ins, n.aw[layer]
    if layer == 0:
        loads = [(a["q"][:], I["L0_attn_W_UQ"]), (a["dkv"][:], I["L0_attn_W_DKV"]),
                 (a["k"][0:LATENT, :], I["L0_attn_W_UK"]), (a["v"][0:LATENT, :], I["L0_attn_W_UV"])]
        wo_src = I["L0_attn_W_O"]
    else:
        qkv, b = I["qkv_wT"], I["L1_attn_qkv_b"]
        loads = [(a["q"][:], qkv[:, 0:D]), (a["k"][:], qkv[:, D:2 * D]), (a["v"][:], qkv[:, 2 * D:3 * D]),
                 (a["bq"][:], b[0:D].unsqueeze(1)), (a["bk"][:], b[D:2 * D].unsqueeze(1)),
                 (a["bv"][:], b[2 * D:3 * D].unsqueeze(0)), (a["bo"][:], I["L1_attn_out_b"].unsqueeze(0))]
        wo_src = I["out_wT"]
    wo_v = wo_src.rearrange("(r j d) n -> j r d n", j=4, d=HD)
    for j in range(4):
        for r in range(4):
            loads.append((a["o"][32 * j + HD * r:32 * j + HD * (r + 1), :], wo_v[j, r]))
    for dst, src in loads:
        sp.dma_start(dst, src).then_inc(n.aw_loaded[layer], 16)
    return 16 * len(loads)


def prepare_values(n):
    n.V = n.sb("V", [P, 2, NT, 4, 4, 32])
    zeroed, ones = n.sem("V_zeroed"), n.sem("V_ones")
    with n.nc.Block() as block:
        @block.vector
        def _(dve):
            dve.memset(n.V[:], 0.0).then_inc(zeroed, 1)
            dve.wait_ge(zeroed, 1)
            for r in range(4):
                col = 16 * (1 - r // 2) + r % 2
                for p in range(2):
                    dve.memset(n.V[:, p, :, r, :, col], 1.0).then_inc(ones, 1)
            dve.wait_ge(ones, 8)


def attention(n, layer):
    nc, I = n.nc, n.ins
    with ExitStack() as c:
        L = f"a{layer}_"
        wq, wk, wv, wo, bk, bqs, bv, bo, wdkv = (n.aw[layer].get(x) for x in ("q", "k", "v", "o", "bk", "bqs", "bv", "bo", "dkv"))
        ckv = n.sb(L + "ckv", [LATENT, 2, T], ctx=c) if layer == 0 else None
        Q, K, V = n.Q, n.K, n.V
        xnT = n.sb(L + "xnT", [P, 2, T], ctx=c)
        qkf = n.sb(L + "qkf", [P, 2, T], ctx=c)
        parts = n.sb(L + "parts", [P, 2, 3, T], BF16, ctx=c)
        maxes = n.sb(L + "maxes", [P, 2, NT, HALF], ctx=c)
        nm = n.sb(L + "nm", [HALF, T], ctx=c)
        mparts = n.sb(L + "mparts", [HALF, 2, 3, T], BF16, ctx=c)
        Pt = n.sb(L + "Pt", [P, 4, T], ctx=c)
        Ob = n.sb(L + "Ob", [P, 2, T], ctx=c)
        rden = n.sb(L + "rden", [P, 2, 4 * NT, 2], ctx=c)
        ON = n.sb(L + "ON", [P, NT, D], ctx=c)
        ONT = n.sb(L + "ONT", [P, T], ctx=c)
        psA = n.pb(L + "psA", [P, 2, 2, T], ctx=c)
        psB = n.pb(L + "psB", [P, 2, T], ctx=c)
        psO = n.pb(L + "psO", [P, T], ctx=c)
        psM = n.pb(L + "psM", [P, T], ctx=c)
        scr = n.dram(L + "stack", (2, 2, HEADS, PRODUCT_ROWS, T), BF16)
        a_ready = n.sem(L + "scores_for_max_ready", c)
        a_free = n.sem(L + "maxima_taken", c)
        b_ready = n.sem(L + "scores_for_exp_ready", c)
        p_ready = n.sem(L + "exp_ready", c)
        pv_done = n.sem(L + "pv_done", c)
        misc_ready = n.sem(L + "misc_ready", c)
        misc_free = n.sem(L + "misc_read", c)
        o_copied = n.sem(L + "outputs_copied", c)
        den_ready = n.sem(L + "den_ready", c)
        split_step = n.sem(L + "split_step", c)
        parts_ready = n.sem(L + "parts_ready", c)
        parts_written = n.sem(L + "parts_written", c)
        xnT_loaded = [n.sem(L + f"xnT_loaded{p}", c) for p in range(2)]
        stack_loaded = [n.sem(L + f"stack_loaded{s}", c) for s in range(4)]
        max_ready = n.sem(L + "max_parts_ready", c)
        max_loaded = [n.sem(L + f"max_loaded{s}", c) for s in range(4)]
        if layer == 0:
            xn1 = n.sb("xn1", [P, NT, D], ctx=c)
            xnT1 = n.sb("xnT1", [P, T], ctx=c)
            stats = n.sb("ln_stats", [P, NT, 6], ctx=c)
            mean, dm, m2, sd, rstd = (n.sb("ln_" + x, [P, NT], ctx=c) for x in ("mean", "dm", "m2", "sd", "rstd"))
            ln_step, sd_ready, xn_ready, xnT1_stored, eyes = (
                n.sem(x, c) for x in ("ln_step", "sd_ready", "xn_ready", "xnT1_stored", "alpha_eyes"))
            bias_rows = n.sem("bias_rows_loaded", c)
            bias_scaled, xn_copied = n.sem("bias_scaled", c), n.sem("xn_copied", c)
        xnT_dram = n.xnT_dram if layer == 0 else n.xnT1_dram
        xn_all = n.slots_flat[:, 0:TILES * D].rearrange("p (t d) -> p t d", d=D)

        units_a, units_b = score_units(layer)
        scripts = [script(layer, k) for k in range(STEPS)]

        def counts(*kinds):
            return Counts([sum(x[0] in kinds for x in scripts[k]) for k in range(STEPS)])
        nA, nB, nM, nO = counts("A"), counts("B"), counts(*MISC), counts("OC")
        nMT = counts("MT")
        nQK = Counts([sum(x[0] in ("PJ", "PN") and x[1] != "C" for x in scripts[k]) for k in range(STEPS)])
        nOT = counts("OT")

        def misc_index(k, g, pos):
            return nM.at(k, g) + sum(x[0] in MISC for x in scripts[k][:pos])


        def loads(hb, g):
            return hb // 4 + 1 + g

        if layer == 1:
            G3 = STEP_GROUPS
            xs = n.slots_flat[:, 0:G3 * GROUP * D].rearrange("p (e t d) -> p e t d", e=G3, t=GROUP)
            wsz = 2 * D + 1
            w0 = G3 * GROUP * D
            ew = n.slots_flat[:, w0:w0 + G3 * GROUP * wsz].rearrange("p (e t h) -> p e t h", e=G3, t=GROUP)
            x0 = w0 + G3 * GROUP * wsz
            xT = n.slots_flat[:, x0:x0 + G3 * GROUP * P].rearrange("p (e t) -> p e t", e=G3)
            hT, ys = xT, xs
            got = n.slots_flat[:, 0:16 * 2 * D].rearrange("p (s j d) -> p s j d", j=2, d=D)
            E = EXPERTS
            logits = n.logits
            work = n.sb("r_work", [P, 3 * TILES * E], ctx=c)
            pr, before, sums1 = (work[:, j * TILES * E:(j + 1) * TILES * E].rearrange("p (t e) -> p t e", e=E)
                                 for j in range(3))
            sums = [logits[:], sums1]
            CMP = LOAD_TILES // 2
            cmp = work[0:1, 0:CMP * E].rearrange("p (t e) -> p t e", e=E)
            eq = n.sb("r_eq", [P, TILES, E], ctx=c)
            tail = TILES * D
            hot0, hot1, count = (n.slots_flat[:, tail + j * TILES * E // 2:tail + (j + 1) * TILES * E // 2].bitcast(BF16)
                                 .rearrange("p (t e) -> p t e", e=E) for j in range(3))
            hot = [hot0, hot1]
            small = n.sb("r_small", [P, 11, TILES], ctx=c)
            ends = [n.sb(f"r_ends{j}", [P, E], ctx=c) for j in range(2)]
            nt, first = n.sb("r_nt", [P, E], ctx=c), n.sb("r_first", [P, E], ctx=c)
            te = n.sb("r_te", [1, LOAD_TILES], ctx=c)
            ct = n.slots_flat[0:E, tail:tail + T]
            chain, shifted, acted, gap_ready, count_ready, combined, slots_ready, experts_ready = (
                n.sem("r_" + x, c) for x in ("chain", "shifted", "acted", "gap_ready", "count_ready", "combined",
                                             "slots_ready", "experts_ready"))
            placed = n.sem("slots_filled", c)
            xs_loaded = [n.sem(f"slots_loaded{e}", c) for e in range(G3)]
            w_loaded = [n.sem(f"expert_loaded{e}", c) for e in range(G3)]
            ys_stored = [n.sem(f"results_stored{e}", c) for e in range(G3)]
            gathered = [n.sem(f"gathered{q}", c) for q in range(4)]
            added = n.sem("choices_added", c)
            out_stored = n.sem("out_stored", c)
            out_v = n.out.rearrange("b (i p) d -> p (b i) d", p=P)

        def ln_sequence(k, g):
            return (k - 4) // 2 + 2 * g if k % 2 == 0 else SEQS - 1

        def expert_round(k, g):
            return k - FIRST + 1 + ROUND_STEPS * g

        with nc.Block() as block:
            @block.sync
            def _(sp):
                def load_xnT(b, p):
                    sp.dma_start(xnT[:, p, :], xnT_dram[bass.ds(b, 1)].rearrange("o d t -> d (o t)")
                                 ).then_inc(xnT_loaded[p], 16)

                def write_parts(k, g, p, last):
                    q_done = nQK.at(k, g) + (2 if k == 0 and p == 1 else 0) + 2
                    copies = [(s, r, part) for s, which in enumerate((Q_PARTS, K_PARTS)) for r, part in enumerate(which)]
                    if not last:
                        sp.wait_ge(parts_ready, q_done)
                    for s, r, part in (copies[-1:] if last else copies[:-1]):
                        sp.dma_start(scr[p, s, :, r * HD:(r + 1) * HD, :], parts[:, s, part, :]).then_inc(parts_written, 16)
                    if not last:
                        return
                    sp.wait_ge(parts_written, 16 * 12 * (q_done // 2) if isinstance(q_done, int)
                               else 16 * 12 * (nQK.at(k, 0) // 2 + 1) + 16 * 12 * (nQK.round // 2) * g)

                def write_first(which):
                    sp.wait_ge(parts_ready, which + 1)
                    for r, part in enumerate((Q_PARTS, K_PARTS)[which]):
                        sp.dma_start(scr[0, which, :, r * HD:(r + 1) * HD, :], parts[:, which, part, :]).then_inc(parts_written, 16)

                def load_stack(hb, p):
                    t = hb % 2
                    for s, dst in enumerate((Q, K)):
                        sp.dma_start(dst[0:PRODUCT_ROWS, hb % 4],
                                     scr[p, s, HALF * t:HALF * (t + 1)].rearrange("h r t -> r h t")
                                     ).then_inc(stack_loaded[hb % 4], 16)

                load_xnT(0, 0)

                def load_weights(e, first_tile):
                    for t in range(GROUP):
                        x = sp.value_load(n.tile_expert[0:1, bass.ds(first_tile + t, 1)], min_val=0, max_val=EXPERTS - 1)
                        sp.dma_start(ew[:, e, t, :], I["expert_w"][bass.ds(x, 1)].rearrange("o d h -> d (o h)")
                                     ).then_inc(w_loaded[e], 16)

                def slot_rows(dram, group):
                    return dram.rearrange("(g t p) d -> g p t d", t=GROUP, p=P)[bass.ds(group, 1)].rearrange("o p t d -> p (o t) d")

                def store_x(b0, b1):
                    sp.dma_start(out_v[:, b0 * NT:b1 * NT, :], n.x[:, b0 * NT:b1 * NT, :]).then_inc(out_stored, 16)

                def step(k, g):
                    if k == 0:
                        load_xnT(1, 1)
                    for pos, (what, arg) in enumerate(scripts[k]):
                        if what == "PJ" and arg == "Q":
                            write_first(0)
                        elif what == "PJ" and arg == "K":
                            write_first(1)
                            sp.wait_ge(parts_written, 16 * 12)
                            load_stack(0, 0)
                            load_stack(1, 0)
                        elif what == "PN" and arg == "K":
                            write_parts(k, g, (k // 2 + 1) % 2, False)
                        elif what == "MT":
                            sp.wait_ge(max_ready, nMT.at(k, g) + 1)
                            for s in range(3):
                                sp.dma_start(Q[MAX_ROW + s:MAX_ROW + s + 1, (k - 1) % 4],
                                             mparts[:, (k - 1) % 2, s, :]).then_inc(max_loaded[(k - 1) % 4], 16)
                            if k % 2 == 0 and k // 2 + 1 < SEQS:
                                load_xnT(k // 2 + 1 + 2 * g, (k // 2 + 1) % 2)
                        elif what == "EY":
                            group = STEP_GROUPS * (k - FIRST) + arg + STEP_GROUPS * ROUND_STEPS * g
                            sp.wait_ge(misc_free, misc_index(k, g, pos) + 1)
                            sp.dma_start(slot_rows(n.ys_dram, group), ys[:, arg]).then_inc(ys_stored[arg], 16)
                            load_weights(arg, (group + STEP_GROUPS) * GROUP)
                            sp.wait_ge(ys_stored[arg], 16 * expert_round(k, g))
                            sp.dma_start(xs[:, arg], slot_rows(n.xs_dram, group + STEP_GROUPS)).then_inc(xs_loaded[arg], 16)
                        elif what == "XT":
                            sp.wait_ge(misc_free, misc_index(k, g, pos) + 1)
                            sp.dma_start(n.xnT1_dram[bass.ds(ln_sequence(k, g), 1)].rearrange("o d t -> d (o t)"),
                                         xnT1[:]).then_inc(xnT1_stored, 16)
                    if k + 2 < 2 * SEQS:
                        if k >= 2:
                            sp.wait_ge(b_ready, nB.at(k, g) + len(units_b))
                        if k % 2 == 0:
                            write_parts(k, g, (k // 2 + 1) % 2, True)
                        load_stack(k + 2, ((k + 2) // 2) % 2)
                    if layer == 0 and k == 3:
                        load_attention_weights(n, sp, 1)
                    if layer == 0 and k >= AFTER:
                        slot = (k - 2) % 4
                        sp.wait_ge(b_ready, nB.at(k, g) + len(units_b))
                        sp.dma_start(Q[PRODUCT_ROWS:MAX_ROW, slot],
                                     n.qrows[HALF * (slot % 2):HALF * (slot % 2 + 1)].rearrange("h r t -> r h t")
                                     ).then_inc(bias_rows, 16)
                    if layer == 1 and k == FIRST - 1:
                        sp.wait_ge(experts_ready, 1)
                        sp.wait_ge(placed, 16 * 2 * TILES)
                        for e in range(STEP_GROUPS):
                            sp.dma_start(xs[:, e], slot_rows(n.xs_dram, e)).then_inc(xs_loaded[e], 16)
                            load_weights(e, e * GROUP)
                    if layer == 1 and k == 16:
                        sp.wait_ge(added, 2 * TILES)
                        for b in range(0, SEQS - 1):
                            store_x(b, b + 1)
                run_steps(sp, step)
                if layer == 0:
                    sp.wait_ge(xnT1_stored, 16 * SEQS)
                    sp.wait_ge(bias_rows, 16 * 4)
                    sp.wait_ge(n.aw_loaded[1], 16 * 23)
                else:
                    sp.wait_ge(misc_free, nM.at(STEPS, 0))
                    store_x(SEQS - 1, SEQS)
                    sp.wait_ge(out_stored, 16 * SEQS)

            @block.tensor
            def _(pe):
                def step(k, g):
                    t = k % 2
                    for pos, (what, arg) in enumerate(scripts[k]):
                        if what in MISC:
                            idx = misc_index(k, g, pos)
                            if not (isinstance(idx, int) and idx == 0):
                                pe.wait_ge(misc_free, idx)
                        if what in ("PJ", "PN"):
                            b = 0 if what == "PJ" else k // 2 + 1
                            if arg == projections(layer)[0]:
                                pe.wait_ge(xnT_loaded[b % 2], 16 * (b // 2 + 1 + g))
                            x = xnT[:, b % 2, :]
                            if arg == "C":
                                m = pe.matmul(psM[0:LATENT, :], wdkv[:], x, start=True, stop=True)
                            elif arg == "Q":
                                m = pe.matmul(psM[:], wq[:], x, start=True, stop=True)
                            elif layer == 0:
                                m = pe.matmul(psM[:], wk[0:LATENT, :], ckv[:, b % 2, :], start=True, stop=True)
                            else:
                                m = pe.matmul(psM[:], wk[:], x, start=True, stop=True)
                            m.then_inc(misc_ready, 1)
                        elif what == "V":
                            p = (k // 2) % 2
                            for i in range(NT):
                                o = psM[:, i * D:(i + 1) * D]
                                if layer == 0:
                                    m = pe.matmul(o, ckv[:, p, i * P:(i + 1) * P], wv[0:LATENT, :], start=True, stop=True)
                                else:
                                    pe.matmul(o, xnT[:, p, i * P:(i + 1) * P], wv[:], start=True, stop=False)
                                    m = pe.matmul(o, n.ones[:], bv[:], start=False, stop=True)
                            m.then_inc(misc_ready, 1)
                        elif what == "MT":
                            pe.wait_ge(a_free, nA.at(k, g))
                            for i in range(NT):
                                m = pe.transpose(psM[0:HALF, i * P:(i + 1) * P], maxes[:, (k - 1) % 2, i, :], n.ident[:])
                            m.then_inc(misc_ready, 1)
                        elif what == "XT":
                            b = ln_sequence(k, g)
                            pe.wait_ge(xn_ready, b + 1)
                            for i in range(NT):
                                m = pe.transpose(psM[:, i * P:(i + 1) * P], xn1[:, i, :], n.ident[:])
                            m.then_inc(misc_ready, 1)
                        elif what == "LG":
                            for i in range(NT):
                                m = pe.matmul(psM[:, i * EXPERTS:(i + 1) * EXPERTS], xnT1[:, i * P:(i + 1) * P], n.wg[:],
                                              start=True, stop=True)
                            m.then_inc(misc_ready, 1)
                        elif what in ("RS", "RC"):
                            pe.wait_ge(count_ready, 1)
                            ones = n.ones_b if what == "RS" else n.upper
                            pe.matmul(psM[:], ones[:], count.rearrange("p t e -> p (t e)")[:, arg * T:(arg + 1) * T],
                                      start=True, stop=True).then_inc(misc_ready, 1)
                        elif what == "CT":
                            if arg == 0:
                                pe.wait_ge(combined, 1)
                            for i in range(NT):
                                m = pe.transpose(psM[0:E, i * P:(i + 1) * P], eq[:, arg * NT + i, :], n.ident[:])
                            m.then_inc(misc_ready, 1)
                        elif what == "CB":
                            for i in range(NT):
                                m = pe.matmul(psM[:, i * D:(i + 1) * D], ct[:, i * P:(i + 1) * P], n.b2[:], start=True, stop=True)
                            m.then_inc(misc_ready, 1)
                        elif what == "EX":
                            pe.wait_ge(xs_loaded[arg], 16 * expert_round(k, g))
                            for i in range(GROUP):
                                m = pe.transpose(psM[:, i * P:(i + 1) * P], xs[:, arg, i, :], n.ident[:])
                            m.then_inc(misc_ready, 1)
                        elif what == "EH":
                            pe.wait_ge(w_loaded[arg], 16 * GROUP * expert_round(k, g))
                            for i in range(GROUP):
                                m = pe.matmul(psM[:, i * P:(i + 1) * P], ew[:, arg, i, 0:D], xT[:, arg, i * P:(i + 1) * P],
                                              start=True, stop=True)
                            m.then_inc(misc_ready, 1)
                        elif what == "EY":
                            for i in range(GROUP):
                                m = pe.matmul(psM[:, i * D:(i + 1) * D], hT[:, arg, i * P:(i + 1) * P], ew[:, arg, i, D:2 * D],
                                              start=True, stop=True)
                            m.then_inc(misc_ready, 1)
                        elif what == "A":
                            i, heads = units_a[arg]
                            u = nA.at(k, g) + arg
                            par = (nA.c[k] + arg) % 2
                            if arg == 0:
                                pe.wait_ge(stack_loaded[k % 4], 32 * loads(k, g))
                            if not (isinstance(u, int) and u < 2):
                                pe.wait_ge(a_free, u - 1)
                            w = T if layer == 1 else (i + 1) * P
                            per_bank = T // w
                            for x, h in enumerate(heads):
                                o = psA[:, par, x // per_bank, (x % per_bank) * w:(x % per_bank + 1) * w]
                                pe.matmul(o, Q[0:A_ROWS, k % 4, h, i * P:(i + 1) * P], K[0:A_ROWS, k % 4, h, 0:w],
                                          start=True, stop=False)
                                m = diagonal(pe, o[:, i * P:(i + 1) * P], HALF * t + h, n.mask_q, 2)
                            m.then_inc(a_ready, 1)
                        elif what == "B":
                            kt, heads = units_b[arg]
                            u = nB.at(k, g) + arg
                            slot = (k - 2) % 4
                            if arg == 0:
                                pe.wait_ge(max_loaded[slot], 48 * loads(k - 2, g))
                            if nB.c[k] + arg >= 2:
                                pe.wait_ge(p_ready, u - 1)
                            q0 = 0 if layer == 1 else kt * P
                            w = T - q0
                            for x, h in enumerate(heads):
                                o = psB[:, arg % 2, x * w:(x + 1) * w]
                                pe.matmul(o, K[:, slot, h, kt * P:(kt + 1) * P], Q[:, slot, h, q0:T],
                                          start=True, stop=False)
                                m = diagonal(pe, o[:, kt * P - q0:(kt + 1) * P - q0], HALF * t + h, n.mask_k, 3)
                            m.then_inc(b_ready, 1)
                        elif what == "PV":
                            kt, heads = units_b[arg]
                            u = nB.at(k, g) + arg
                            if arg == 0 and nO.c[k]:
                                pe.wait_ge(o_copied, nO.at(k, g))
                            pe.wait_ge(p_ready, u + 1)
                            q0 = 0 if layer == 1 else kt * P
                            w = T - q0
                            b = (k - 2) // 2
                            for x, h in enumerate(heads):
                                r, j = (HALF * t + h) // 4, h % 4
                                m = pe.matmul(psO[32 * j:32 * (j + 1), q0:T], V[:, b % 2, kt, r, j, :],
                                              Pt[:, (nB.c[k] + arg) % 4, x * w:(x + 1) * w],
                                              start=(kt == 0 and h < 4), stop=(kt == NT - 1 and h >= 4),
                                              skip_group_check=True)
                            m.then_inc(pv_done, 1)
                        elif what == "OT":
                            pe.wait_ge(o_copied, nO.at(k, g) + arg)
                            for i in range(NT):
                                m = pe.transpose(psM[:, i * P:(i + 1) * P], Ob[:, arg, i * P:(i + 1) * P], n.ident[:])
                            m.then_inc(misc_ready, 1)
                        elif what == "ONT":
                            for i in range(NT):
                                m = pe.transpose(psM[:, i * P:(i + 1) * P], ON[:, i, :], n.ident[:])
                            m.then_inc(misc_ready, 1)
                        elif what == "WO":
                            for i in range(NT):
                                o = psM[:, i * D:(i + 1) * D]
                                m = pe.matmul(o, ONT[:, i * P:(i + 1) * P], wo[:], start=True, stop=(layer == 0))
                                if layer == 1:
                                    m = pe.matmul(o, n.ones[:], bo[:], start=False, stop=True)
                            m.then_inc(misc_ready, 1)

                def diagonal(pe, o, head, mask, parts_):
                    if layer == 0:
                        return pe.matmul(o, n.identb[:], mask[:], start=False, stop=True)
                    for s in range(parts_):
                        m = pe.matmul(o, n.alpha_eye[:, head, s, :], n.dist[:], start=False, stop=(s == parts_ - 1))
                    return m
                run_steps(pe, step)

            @block.scalar
            def _(act):
                def project(k, g, pos, b, arg):
                    idx = misc_index(k, g, pos)
                    act.wait_ge(misc_ready, idx + 1)
                    if arg == "C":
                        act.activation(ckv[:, b % 2, :], psM[0:LATENT, :], ACT.Copy).then_inc(misc_free, 1)
                        return
                    s = "QK".index(arg)
                    done = nQK.at(k, g) + (2 if what_is(k, pos) == "PN" and k == 0 else 0)
                    if not (isinstance(done, int) and done == 0):
                        act.wait_ge(parts_ready, done)
                        writes = 96 * done if isinstance(done, int) else 96 * nQK.at(k, 0) + 96 * nQK.round * g
                        act.wait_ge(parts_written, writes)
                    bias, scale = (0.0, 1.0) if layer == 0 else (bk[:], 1.0)
                    if arg == "Q":
                        bias, scale = (0.0, SCALE) if layer == 0 else (bqs[:], SCALE)
                    f = ACT.Copy if layer == 0 else ACT.Identity
                    act.activation(qkf[:, s, :], psM[:], f, bias=bias, scale=scale)
                    act.activation(parts[:, s, 0, :], psM[:], f, bias=bias, scale=scale).then_inc(misc_free, 1)

                def what_is(k, pos):
                    return scripts[k][pos][0]

                def step(k, g):
                    for pos, (what, arg) in enumerate(scripts[k]):
                        if what in ("PJ", "PN"):
                            project(k, g, pos, 0 if what == "PJ" else k // 2 + 1, arg)
                        elif what == "MT":
                            act.wait_ge(misc_ready, misc_index(k, g, pos) + 1)
                            if k > 1:
                                act.wait_ge(max_ready, nMT.at(k, g))
                            if k > 2:
                                hb = k - 3
                                act.wait_ge(max_loaded[hb % 4], 48 * loads(hb, g))
                            act.activation(nm[:], psM[0:HALF, :], ACT.Copy)
                            act.activation(mparts[:, (k - 1) % 2, 0, :], psM[0:HALF, :], ACT.Copy).then_inc(misc_free, 1)
                        elif what == "B":
                            kt, heads = units_b[arg]
                            u = nB.at(k, g) + arg
                            w = len(heads) * (T if layer == 1 else T - kt * P)
                            act.wait_ge(b_ready, u + 1)
                            if nB.c[k] + arg >= 4:
                                act.wait_ge(pv_done, u - 3)
                            act.activation(Pt[:, (nB.c[k] + arg) % 4, 0:w], psB[:, arg % 2, 0:w], ACT.Exp).then_inc(p_ready, 1)
                        elif what == "OC":
                            act.wait_ge(pv_done, nB.at(k, g) + len(units_b))
                            act.activation(Ob[:, k % 2, :], psO[:], ACT.Copy).then_inc(o_copied, 1)
                        elif what == "LS":
                            b = ln_sequence(k, g)
                            act.wait_ge(ln_step, 12 * b + 11)
                            act.activation(sd[:], m2[:], ACT.Sqrt).then_inc(sd_ready, 1)
                        elif what == "XT":
                            act.wait_ge(misc_ready, misc_index(k, g, pos) + 1)
                            if k > 4:
                                act.wait_ge(xnT1_stored, 16 * ln_sequence(k, g))
                            act.activation(xnT1[:], psM[:], ACT.Copy).then_inc(misc_free, 1)
                        elif what == "R" and arg == 0:
                            act.wait_ge(shifted, 1)
                            act.activation(pr, pr, ACT.Exp).then_inc(acted, 1)
                        elif what == "R" and arg == 6:
                            act.wait_ge(gap_ready, 1)
                            act.activation(small[:, 6, :], small[:, 6, :], ACT.Exp).then_inc(acted, 1)
                        elif what == "CT":
                            if arg == 0:
                                for e in range(STEP_GROUPS):
                                    act.wait_ge(w_loaded[e], 16 * GROUP * (len(EXPERT_STEPS) + 1))
                            act.wait_ge(misc_ready, misc_index(k, g, pos) + 1)
                            act.activation(ct, psM[0:E, :], ACT.Copy).then_inc(misc_free, 1)
                        elif what == "EH":
                            act.wait_ge(misc_ready, misc_index(k, g, pos) + 1)
                            for i in range(GROUP):
                                m = act.activation(hT[:, arg, i * P:(i + 1) * P], psM[:, i * P:(i + 1) * P], ACT.Gelu,
                                                   bias=ew[:, arg, i, 2 * D:2 * D + 1])
                            m.then_inc(misc_free, 1)
                        elif what == "ONT":
                            act.wait_ge(misc_ready, misc_index(k, g, pos) + 1)
                            act.activation(ONT[:], psM[:], ACT.Copy).then_inc(misc_free, 1)
                run_steps(act, step)
                if layer == 0:
                    act.wait_ge(n.aw_loaded[1], 16 * 23)
                    act.activation(n.aw[1]["bqs"][:], n.aw[1]["bq"][:], ACT.Copy, scale=SCALE).then_inc(bias_scaled, 1)
                    act.wait_ge(bias_scaled, 1)

            @block.vector
            def _(dve):
                chained = 0

                def then(ins, sem=None):
                    nonlocal chained
                    if sem is not None:
                        ins.then_inc(sem, 1)
                        dve.wait_ge(sem, 1)
                        return
                    ins.then_inc(chain, 1)
                    chained += 1
                    dve.wait_ge(chain, chained)

                def find_top(top, ix, hot_j, half):
                    ev = n.expert[:].unsqueeze(1).broadcast_to([P, TILES, E])
                    if half == 0:
                        then(dve.tensor_reduce(top, pr, AX, ALU.max))
                        then(dve.tensor_tensor(eq[:], pr, bc(top, E), ALU.is_equal))
                        then(dve.tensor_tensor(eq[:], eq[:], ev, ALU.mult))
                    else:
                        then(dve.tensor_reduce(ix, eq[:], AX, ALU.min))
                        then(dve.tensor_tensor(hot_j, ev, bc(ix, E), ALU.is_equal))

                def route(stage):
                    mx, sm, rs, top1, top2, id1, dif, id2, w_0 = (small[:, j, :] for j in range(9))
                    if stage == 0:
                        then(dve.tensor_reduce(mx, logits[:], AX, ALU.max))
                        then(dve.tensor_tensor(pr, logits[:], bc(mx, E), ALU.subtract), shifted)
                    elif stage == 1:
                        dve.wait_ge(acted, 1)
                        then(dve.tensor_reduce(sm, pr, AX, ALU.add))
                        then(dve.reciprocal(rs, sm))
                        then(dve.tensor_tensor(pr, pr, bc(rs, E), ALU.mult))
                    elif stage == 2:
                        find_top(top1, id1, hot[0], 0)
                    elif stage == 3:
                        find_top(top1, id1, hot[0], 1)
                        then(dve.scalar_tensor_tensor(pr, hot[0], -4.0, pr, ALU.mult, ALU.add))
                    elif stage == 4:
                        find_top(top2, id2, hot[1], 0)
                    elif stage == 5:
                        find_top(top2, id2, hot[1], 1)
                        then(dve.tensor_tensor(count, hot[0], hot[1], ALU.add), count_ready)
                    elif stage == 6:
                        then(dve.tensor_tensor(dif, top2, top1, ALU.subtract), gap_ready)
                    elif stage == 7:
                        dve.wait_ge(acted, 2)
                        then(dve.tensor_scalar(w_0, dif, 1.0, None, ALU.add))
                        then(dve.reciprocal(n.weights[:, 0, :], w_0))
                        then(dve.tensor_tensor(n.weights[:, 1, :], dif, n.weights[:, 0, :], ALU.mult))
                    elif stage == 8:
                        then(dve.tensor_tensor(pr, hot[0], bc(n.weights[:, 0, :], E), ALU.mult))
                        then(dve.tensor_tensor(eq[:], hot[1], bc(n.weights[:, 1, :], E), ALU.mult))
                        then(dve.tensor_tensor(eq[:], eq[:], pr, ALU.add), combined)
                    elif stage in (9, 10):
                        if stage == 9:
                            then(dve.tensor_tensor(before, before, sums[0], ALU.subtract))
                        for at, d in enumerate((1, 2, 4, 8, 16)):
                            if (at < 3) == (stage == 9):
                                src, dst = sums[at % 2], sums[1 - at % 2]
                                dve.tensor_copy(dst[:, 0:d, :], src[:, 0:d, :])
                                then(dve.tensor_tensor(dst[:, d:, :], src[:, d:, :], src[:, :TILES - d, :], ALU.add))
                        if stage == 10:
                            then(dve.tensor_tensor(before, before, sums[1], ALU.add))
                    elif stage == 11:
                        then(dve.tensor_scalar(nt[:], sums[1][:, TILES - 1, :], 1.0 / P, (P - 1) / P - 0.498, ALU.mult, ALU.add))
                        then(dve.tensor_scalar(nt[:], nt[:], ROUND, None, ALU.add))
                        then(dve.tensor_scalar(nt[:], nt[:], -ROUND, None, ALU.add))
                        then(dve.tensor_copy(ends[0][:], nt[:]))
                        for at, d in enumerate((1, 2, 4, 8, 16)):
                            src, dst = ends[at % 2], ends[1 - at % 2]
                            dve.tensor_copy(dst[:, 0:d], src[:, 0:d])
                            then(dve.tensor_tensor(dst[:, d:], src[:, d:], src[:, :E - d], ALU.add))
                    elif stage == 12:
                        then(dve.tensor_tensor(first[:], ends[1][:], nt[:], ALU.subtract))
                        then(dve.tensor_scalar(first[:], first[:], float(P), None, ALU.mult))
                        then(dve.tensor_tensor(before, before, first[:].unsqueeze(1).broadcast_to([P, TILES, E]), ALU.add))
                    elif stage in (13, 14):
                        j = stage - 13
                        then(dve.tensor_tensor(pr, before, hot[j], ALU.mult))
                        then(dve.tensor_reduce(small[:, 9 + j, :], pr, AX, ALU.add))
                        m = dve.tensor_copy(n.slots[:, j, :], small[:, 9 + j, :])
                        if j == 1:
                            then(m, slots_ready)
                    elif stage == 15:
                        for part in range(2):
                            tiles = slice(part * CMP, (part + 1) * CMP)
                            then(dve.tensor_tensor(cmp, ends[1][0:1, :].unsqueeze(1).broadcast_to([1, CMP, E]),
                                                   bc(n.slot_tile[:, tiles], E), ALU.is_le))
                            then(dve.tensor_reduce(te[:, tiles], cmp, AX, ALU.add))
                        then(dve.tensor_scalar(n.tile_expert[:], te[:], float(E - 1), None, ALU.min), experts_ready)

                def add_choices(t):
                    dve.wait_ge(gathered[t // 4 % 4], 128 * (t // 16 + 1))
                    for j in range(2):
                        if j:
                            dve.wait_ge(added, 2 * t + 1)
                        dve.scalar_tensor_tensor(n.x[:, t, :], got[:, t % 16, j, :], n.weights[:, j, t:t + 1],
                                                 n.x[:, t, :], ALU.mult, ALU.add).then_inc(added, 1)

                def step(k, g):
                    for pos, (what, arg) in enumerate(scripts[k]):
                        if what == "A":
                            i, heads = units_a[arg]
                            par = (nA.c[k] + arg) % 2
                            w = T if layer == 1 else (i + 1) * P
                            if arg == 0 and k >= 2:
                                dve.wait_ge(misc_ready, nM.at(k, g))
                            dve.wait_ge(a_ready, nA.at(k, g) + arg + 1)
                            src = psA[:, par, :, 0:w] if T // w == 1 else \
                                psA[:, par].rearrange("p b (x w) -> p (b x) w", w=w)
                            dve.tensor_reduce(maxes[:, k % 2, i, heads[0]:heads[0] + len(heads)], src, AX,
                                              ALU.max, negate=True).then_inc(a_free, 1)
                            if layer == 1 and k == AFTER + 1:
                                if arg == 0:
                                    dve.wait_ge(misc_free, nM.at(k, 0))
                                add_choices(arg)
                        elif what == "LS":
                            b = ln_sequence(k, g)
                            base = 12 * b
                            if isinstance(b, int):
                                dve.wait_ge(misc_free, misc_index(k, g, pos))
                            for i in range(NT):
                                dve.bn_stats(stats[:, i, :], n.x[:, bass.ds(b * NT + i, 1), :].rearrange("p o k -> p (o k)")
                                             ).then_inc(ln_step, 1)
                            dve.wait_ge(ln_step, base + 4)
                            dve.tensor_tensor(mean[:], stats[:, :, 1], stats[:, :, 4], ALU.add).then_inc(ln_step, 1)
                            dve.tensor_tensor(dm[:], stats[:, :, 1], stats[:, :, 4], ALU.subtract).then_inc(ln_step, 1)
                            dve.tensor_tensor(m2[:], stats[:, :, 2], stats[:, :, 5], ALU.add).then_inc(ln_step, 1)
                            dve.wait_ge(ln_step, base + 7)
                            dve.tensor_scalar(mean[:], mean[:], 0.5, None, ALU.mult).then_inc(ln_step, 1)
                            dve.tensor_tensor(dm[:], dm[:], dm[:], ALU.mult).then_inc(ln_step, 1)
                            dve.wait_ge(ln_step, base + 9)
                            dve.scalar_tensor_tensor(m2[:], dm[:], float(P // 4), m2[:], ALU.mult, ALU.add).then_inc(ln_step, 1)
                            dve.wait_ge(ln_step, base + 10)
                            dve.tensor_scalar(m2[:], m2[:], 1.0 / D, EPS, ALU.mult, ALU.add).then_inc(ln_step, 1)
                        elif what == "LN":
                            b = ln_sequence(k, g)
                            dve.wait_ge(sd_ready, b + 1)
                            dve.reciprocal(rstd[:], sd[:]).then_inc(ln_step, 1)
                            dve.wait_ge(ln_step, 12 * b + 12)
                            if k > 4:
                                dve.wait_ge(xn_copied, b)
                            for i in range(NT):
                                m = dve.tensor_scalar(
                                    xn1[:, i, :],
                                    n.x[:, bass.ds(b * NT + i, 1), :].rearrange("p o k -> p (o k)"),
                                    mean[:, i:i + 1], rstd[:, i:i + 1], ALU.subtract, ALU.mult)
                            m.then_inc(xn_ready, 1)
                        elif what == "LG":
                            dve.wait_ge(misc_ready, misc_index(k, g, pos) + 1)
                            dve.tensor_copy(n.logits[:, bass.ds(ln_sequence(k, g) * NT, NT), :],
                                            psM[:, 0:NT * EXPERTS].rearrange("p (i e) -> p i e", e=EXPERTS)
                                            ).then_inc(misc_free, 1)
                        elif what == "R":
                            route(arg)
                        elif what in ("RS", "RC"):
                            dve.wait_ge(misc_ready, misc_index(k, g, pos) + 1)
                            dst = sums[0] if what == "RS" else before
                            dve.tensor_copy(dst[:, arg * TILES // 2:(arg + 1) * TILES // 2, :],
                                            psM[:].rearrange("p (t e) -> p t e", e=E)).then_inc(misc_free, 1)
                        elif what == "CB":
                            dve.wait_ge(misc_ready, misc_index(k, g, pos) + 1)
                            xv = n.x[:, arg * NT:(arg + 1) * NT, :]
                            dve.tensor_tensor(xv, psM[:].rearrange("p (i d) -> p i d", d=D), xv, ALU.add).then_inc(misc_free, 1)
                        elif what == "EX":
                            dve.wait_ge(misc_ready, misc_index(k, g, pos) + 1)
                            dve.tensor_copy(xT[:, arg], psM[:]).then_inc(misc_free, 1)
                        elif what == "EY":
                            dve.wait_ge(misc_ready, misc_index(k, g, pos) + 1)
                            dve.tensor_copy(ys[:, arg].rearrange("p t d -> p (t d)"), psM[:]).then_inc(misc_free, 1)
                        elif what == "V":
                            dve.wait_ge(misc_ready, misc_index(k, g, pos) + 1)
                            if k > 2:
                                dve.wait_ge(pv_done, nB.at(k, g))
                            src = psM[:].rearrange("p (i r j d) -> p i r j d", i=NT, r=4, j=4)
                            for r in range(4):
                                m = dve.tensor_copy(V[:, (k // 2) % 2, :, r, :, HD * r:HD * (r + 1)], src[:, :, r])
                            m.then_inc(misc_free, 1)
                        elif what == "OT":
                            dve.wait_ge(misc_ready, misc_index(k, g, pos) + 1)
                            o = psM[:].rearrange("p (m w) -> p m w", w=32)
                            den, val = 16 * (1 - arg), 16 * arg
                            dve.reciprocal(rden[:, arg], o[:, :, den:den + 2]).then_inc(den_ready, 1)
                            dve.wait_ge(den_ready, nOT.at(k, g) + arg + 1)
                            dve.tensor_tensor(
                                ON[:].rearrange("p i (j w) -> p (i j) w", w=32)[:, :, val:val + 16].rearrange(
                                    "p m (r d) -> p m r d", d=HD),
                                o[:, :, val:val + 16].rearrange("p m (r d) -> p m r d", d=HD),
                                rden[:, arg].unsqueeze(3).broadcast_to([P, 4 * NT, 2, HD]), ALU.mult
                            ).then_inc(misc_free, 1)
                        elif what == "WO":
                            dve.wait_ge(misc_ready, misc_index(k, g, pos) + 1)
                            if layer == 1 and k == STEPS - 1:
                                dve.wait_ge(added, 2 * TILES)
                            b = (k - 3) // 2
                            xv = n.x[:, bass.ds((b + 2 * g) * NT, NT), :]
                            dve.tensor_tensor(xv, psM[:].rearrange("p (i d) -> p i d", i=NT), xv, ALU.add).then_inc(misc_free, 1)
                    if layer == 1 and k == 16:
                        dve.wait_ge(misc_free, nM.at(k, 0))
                        for t in range(16, TILES):
                            add_choices(t)
                run_steps(dve, step)
                dve.wait_ge(misc_free, nM.at(STEPS, 0))

            @block.gpsimd
            def _(pool):
                nS = Counts([3 * sum((x[0] in ("PJ", "PN") and x[1] != "C") or x[0] == "MT" for x in scripts[k])
                             for k in range(STEPS)])

                def scatter(t0, t1):
                    for t in range(t0, t1):
                        for j in range(2):
                            pool.indirect_dma_start(
                                out=n.xs_dram, out_offset=bass.IndirectOffsetOnAxis(ap=n.slots[:, j, t:t + 1], axis=0),
                                in_=n.slots_flat[:, t * D:(t + 1) * D], in_offset=None).then_inc(placed, 16)

                def gather(t0):
                    for t in range(t0, t0 + 16):
                        if t >= 16 and t % 4 == 0:
                            pool.wait_ge(added, 2 * (t - 12))
                        for j in range(2):
                            pool.indirect_dma_start(
                                out=got[:, t % 16, j, :], out_offset=None, in_=n.ys_dram,
                                in_offset=bass.IndirectOffsetOnAxis(ap=n.slots[:, j, t:t + 1], axis=0)
                            ).then_inc(gathered[t // 4 % 4], 16)

                def split(f, parts3, base, done):
                    pool.tensor_tensor(f, f, parts3[0], ALU.subtract).then_inc(split_step, 1)
                    pool.wait_ge(split_step, base + 1)
                    pool.tensor_tensor(parts3[1], f, n.zeros[0:f.shape[0], :], ALU.add).then_inc(split_step, 1)
                    pool.wait_ge(split_step, base + 2)
                    pool.tensor_tensor(parts3[2], f, parts3[1], ALU.subtract).then_inc(done, 1)

                def step(k, g):
                    count = 0
                    for pos, (what, arg) in enumerate(scripts[k]):
                        base = (nS.at(k, g) // 3 * 2 if isinstance(nS.at(k, g), int)
                                else nS.at(k, 0) // 3 * 2 + nS.round // 3 * 2 * g)
                        if what in ("PJ", "PN") and arg != "C":
                            pool.wait_ge(misc_free, misc_index(k, g, pos) + 1)
                            s = "QK".index(arg)
                            split(qkf[:, s, :], [parts[:, s, x, :] for x in range(3)], base + 2 * count, parts_ready)
                            count += 1
                        elif what == "MT":
                            pool.wait_ge(misc_free, misc_index(k, g, pos) + 1)
                            split(nm[:], [mparts[:, (k - 1) % 2, x, :] for x in range(3)], base + 2 * count, max_ready)
                            count += 1
                            if layer == 1 and k in (4, 5):
                                scatter(16 * k - 56, 16 * k - 48)
                        elif what == "LN":
                            b = ln_sequence(k, g)
                            pool.wait_ge(xn_ready, b + 1)
                            pool.tensor_tensor(xn_all[:, bass.ds(b * NT, NT), :], xn1[:],
                                               n.zeros[:].rearrange("p (i d) -> p i d", d=D), ALU.add).then_inc(xn_copied, 1)
                    if layer == 0 and k == STEPS - 1:
                        pool.wait_ge(xn_copied, SEQS)
                        for x in range(3):
                            m = pool.tensor_tensor(
                                n.alpha_eye[:, :, x, :], n.ident[:].unsqueeze(1).broadcast_to([P, HEADS, P]),
                                n.alpha_parts[:, x, 1:].unsqueeze(2).broadcast_to([P, HEADS, P]), ALU.mult)
                        m.then_inc(eyes, 1)
                        pool.wait_ge(eyes, 1)
                    if layer == 1 and k == 3:
                        pool.wait_ge(slots_ready, 1)
                        scatter(0, 8)
                    elif layer == 1 and k == 4:
                        scatter(16, 24)
                    elif layer == 1 and k in (AFTER, AFTER + 1):
                        if k == AFTER:
                            for e in range(STEP_GROUPS):
                                pool.wait_ge(ys_stored[e], 16 * len(EXPERT_STEPS))
                                pool.wait_ge(xs_loaded[e], 16 * (len(EXPERT_STEPS) + 1))
                                pool.wait_ge(w_loaded[e], 16 * GROUP * (len(EXPERT_STEPS) + 1))
                        gather(16 * (k - AFTER))
                run_steps(pool, step)


def program(nc, ins, out):
    n = Net(nc, ins, out)
    with n.ctx:
        n.mean = n.sb("mean", [P, TILES])
        n.rstd = n.sb("rstd", [P, TILES])
        with ExitStack() as f:
            load_constants(n, f)
            layernorm_stats(n, 0)
            ffn(n)
        allocate_attention_weights(n, None, 1)
        n.slots_flat = n.sb("slots_flat", [P, STEP_GROUPS * GROUP * (2 * D + 2 * D + 1)])
        n.logits = n.sb("logits", [P, TILES, EXPERTS])
        n.alpha_eye = n.sb("alpha_eye", [P, HEADS, 3, P], BF16)
        n.slots = n.sb("slots", [P, 2, TILES], I32)
        n.weights = n.sb("weights", [P, 2, TILES])
        n.tile_expert = n.sb("tile_expert", [1, LOAD_TILES], I32)
        prepare_values(n)
        attention(n, 0)
        attention(n, 1)


INPUTS = ['L0_attn_x', 'L0_attn_W_DKV', 'L0_attn_W_UK', 'L0_attn_W_UV', 'L0_attn_W_UQ', 'L0_attn_W_O',
          'L0_ffn_w_gate', 'L0_ffn_w_up', 'L0_ffn_w_down', 'L1_attn_qkv_w', 'L1_attn_qkv_b',
          'L1_attn_out_w', 'L1_attn_out_b', 'L1_attn_decay_alpha', 'L1_ffn_Wg', 'L1_ffn_W1', 'L1_ffn_b1',
          'L1_ffn_W2', 'L1_ffn_b2']


def const_arrays():
    i = np.arange(P)
    rows = np.zeros((ROWS - PRODUCT_ROWS, T), np.float32)
    t = np.arange(T)
    for kt in range(NT):
        here = (t // P == kt)
        for part in range(3):
            rows[(kt * 2 + 0) * 3 + part] = here * (t % P)
            rows[(kt * 2 + 1) * 3 + part] = here
    rows[BIAS_ROWS:] = 1.0
    pat = np.zeros((HEADS, NT, 2, T), np.float32)
    for kt in range(NT):
        sign = np.sign(t // P - kt)
        pat[:, kt, 0] = sign
        pat[:, kt, 1] = -sign * (t - P * kt)
    up = (i[:, None] < i[None, :])
    return {
        "c_ident": np.eye(P, dtype=np.float32),
        "c_mask_q": np.where(up, NEG, 0).astype(np.float32),
        "c_mask_k": np.where(up.T, NEG, 0).astype(np.float32),
        "c_dist": -np.abs(i[:, None] - i[None, :]).astype(np.float32),
        "c_upper": up.astype(np.float32),
        "c_krows": rows,
        "c_qpat": pat.reshape(P, T),
        "c_expert": np.broadcast_to(np.arange(EXPERTS, dtype=np.float32) - 2 * EXPERTS, (P, EXPERTS)).copy(),
        "c_slot_tile": np.arange(LOAD_TILES, dtype=np.float32).reshape(1, LOAD_TILES),
    }


def kernel(**inputs):
    import concourse.bacc as bacc
    from concourse.bass_utils import run_bass_kernel_spmd
    a = {k: np.ascontiguousarray(inputs[k]) for k in INPUTS}
    a["qkv_wT"] = np.ascontiguousarray(a["L1_attn_qkv_w"].T)
    a["out_wT"] = np.ascontiguousarray(a["L1_attn_out_w"].T)
    a["alpha_rows"] = np.repeat(a["L1_attn_decay_alpha"], NT * 2).reshape(P, 1)
    a["alpha_all"] = np.tile(a["L1_attn_decay_alpha"], (P, 1))
    a["expert_w"] = np.concatenate([a["L1_ffn_W1"], a["L1_ffn_W2"], a["L1_ffn_b1"][:, :, None]], axis=2)
    a.update(const_arrays())
    for k in ("L1_attn_qkv_w", "L1_attn_out_w", "L1_attn_decay_alpha", "L1_ffn_W1", "L1_ffn_W2", "L1_ffn_b1"):
        del a[k]
    nc = bacc.Bacc("TRN2", target_bir_lowering=False, num_devices=1)
    ins = {k: nc.dram_tensor("in_" + k, v.shape, mybir.dt.from_np(v.dtype), kind="ExternalInput").ap()
           for k, v in a.items()}
    out = nc.dram_tensor("out", (SEQS, T, D), F32, kind="ExternalOutput").ap()
    program(nc, ins, out)
    r = run_bass_kernel_spmd(nc, [{"in_" + k: v for k, v in a.items()}], core_ids=[0])
    return r.results[0]["out"]
```
